# Optimizing a Trainium2 kernel written in Bass

```python
import numpy as np
import jax
import jax.numpy as jnp

def _softmax(x, axis=-1):
    return jax.nn.softmax(x, axis=axis)

def _gelu(x):
    return jax.nn.gelu(x, approximate=True)

def _silu(x):
    return jax.nn.silu(x)

def _sigmoid(x):
    return jax.nn.sigmoid(x)

def _layernorm(x, axis=-1, eps=1e-05):
    m = jnp.mean(x, axis=axis, keepdims=True)
    v = jnp.var(x, axis=axis, keepdims=True)
    return (x - m) / jnp.sqrt(v + eps)

def _scatter_add(tgt, idx, src, axis=0):
    return tgt.at[idx].add(src)

def _segment_sum(src, seg, n):
    return jax.ops.segment_sum(src, seg, n)
kernel_name = 'mk_flamingo_gated_d4_seqx_r8_029792'

def setup_inputs(seed: int=0):
    np.random.seed(seed)
    _w = jnp.asarray

    def _rec_inputs():
        import jax
        import jax.numpy as jnp
        _rk = jax.random.key(seed)
        x = -0.0003929 + 0.9999 * jax.random.normal(jax.random.fold_in(_rk, 1), (16, 128, 256), jnp.float32)
        _lenS = 128 - jax.random.randint(jax.random.fold_in(_rk, 7), (16,), 0, max(1, 128 // 4) + 1, jnp.int32)
        _lenS2 = 128 - jax.random.randint(jax.random.fold_in(_rk, 8), (16,), 0, max(1, 128 // 4) + 1, jnp.int32)
        _ctx_1024P = jax.random.normal(jax.random.fold_in(_rk, 11), (16, 16, 128), jnp.float32)
        _ctx_1024c = jax.random.dirichlet(jax.random.fold_in(_rk, 511), 0.3 * jnp.ones((16,), jnp.float32), (16, 128))
        _ctx_1024t = jnp.einsum('bsk,bkd->bsd', _ctx_1024c, _ctx_1024P)
        _ctx_1024t = _ctx_1024t * jax.lax.rsqrt(jnp.mean(jnp.square(_ctx_1024t)) + 1e-12) * 0.953939
        ctx_1024 = -0.000494167 + 1.00018 * (_ctx_1024t + 0.3 * jax.random.normal(jax.random.fold_in(_rk, 611), (16, 128, 128), jnp.float32))
        fside_BxSx2_0 = jax.random.uniform(jax.random.fold_in(_rk, 13), (16, 128, 2), jnp.float32, 0.0, 0.999707)
        _validS = jnp.arange(128)[None, :] < _lenS[:, None]
        _validS2 = jnp.arange(128)[None, :] < _lenS2[:, None]
        _causal = jnp.tril(jnp.ones((128, 128), dtype=bool))
        mask_BxS2_bf1 = jnp.ones((16, 128), dtype=bool)
        _g = jax.random.normal(jax.random.fold_in(_rk, 9001), (2, 4), jnp.float32)
        _g = jnp.sign(_g) * jnp.maximum(jnp.abs(_g), 1.0) + (_g == 0) * 1.0
        g_xattn = _g[0]
        g_ffn = _g[1]
        return (x, ctx_1024, fside_BxSx2_0, mask_BxS2_bf1, g_xattn, g_ffn)
    x, ctx_1024, fside_BxSx2_0, mask_BxS2_bf1, g_xattn, g_ffn = _rec_inputs()

    def _L0_xattn_setup():
        import jax, jax.numpy as jnp
        import numpy as np
        N_HEADS = 16
        N_KV_HEADS = 8
        HEAD_DIM = 128
        D_TEXT = 256
        D_VISION = 128
        GROUPS = N_HEADS // N_KV_HEADS
        key = jax.random.key(seed)
        ks = jax.random.split(key, 6)
        B, T_text, T_vis = (4, 256, 72)
        text_hidden = jax.random.normal(ks[0], (B, T_text, D_TEXT), dtype=jnp.float32)
        vision_tokens = jax.random.normal(ks[1], (B, T_vis, D_VISION), dtype=jnp.float32)
        vision_mask = jnp.ones((B, T_vis), dtype=bool)
        s = 0.02
        Wq = jax.random.normal(ks[2], (D_TEXT, N_HEADS * HEAD_DIM), dtype=jnp.float32) * s
        Wk = jax.random.normal(ks[3], (D_VISION, N_KV_HEADS * HEAD_DIM), dtype=jnp.float32) * s
        Wv = jax.random.normal(ks[4], (D_VISION, N_KV_HEADS * HEAD_DIM), dtype=jnp.float32) * s
        Wo = jax.random.normal(ks[5], (N_HEADS * HEAD_DIM, D_TEXT), dtype=jnp.float32) * s
        return {'text_hidden': text_hidden, 'vision_tokens': vision_tokens, 'vision_mask': vision_mask, 'Wq': Wq, 'Wk': Wk, 'Wv': Wv, 'Wo': Wo}
    _L0_xattn_all = _L0_xattn_setup()
    _L0_xattn_in = {k: v for k, v in _L0_xattn_all.items() if k in ('Wq', 'Wk', 'Wv', 'Wo')}
    del _L0_xattn_all

    def _L0_ffn_setup():
        import jax, jax.numpy as jnp
        import numpy as np
        NUM_EXPERTS = 4
        key = jax.random.key(seed)
        k1, k2, k3 = jax.random.split(key, 3)
        B, N, H = (8, 256, 256)
        E = NUM_EXPERTS
        I = H * 4 // E
        x = jax.random.normal(k1, (B, N, H), dtype=jnp.float32)
        gate_up_proj = jax.random.normal(k2, (E, H, 2 * I), dtype=jnp.float32) * 0.02
        down_proj = jax.random.normal(k3, (E, I, H), dtype=jnp.float32) * 0.02
        return {'x': x, 'gate_up_proj': gate_up_proj, 'down_proj': down_proj}
    _L0_ffn_all = _L0_ffn_setup()
    _L0_ffn_in = {k: v for k, v in _L0_ffn_all.items() if k in ('gate_up_proj', 'down_proj')}
    del _L0_ffn_all

    def _L1_xattn_setup():
        import jax, jax.numpy as jnp
        import numpy as np
        DIM = 256
        CTX_DIM = 128
        N_HEADS = 32
        HEAD_DIM = DIM // N_HEADS
        POS_DIM = 2
        B, N, CTXN = (2, 256, 256)
        ROPE_BASE = 10000.0

        def apply_axial_rope(x, pos):
            b, n, h, d = x.shape
            p = pos.shape[-1]
            dpa = d // p
            half = dpa // 2
            freqs = ROPE_BASE ** (-jnp.arange(half, dtype=x.dtype) / half)
            ang = pos[..., :, None] * freqs
            cos = jnp.cos(ang)[:, :, None, :, :]
            sin = jnp.sin(ang)[:, :, None, :, :]
            xr = x.reshape(b, n, h, p, half, 2)
            x1, x2 = (xr[..., 0], xr[..., 1])
            out = jnp.stack([x1 * cos - x2 * sin, x1 * sin + x2 * cos], axis=-1)
            return out.reshape(b, n, h, d)
        key = jax.random.key(seed)
        ks = jax.random.split(key, 8)
        x = jax.random.normal(ks[0], (B, N, DIM), jnp.float32)
        ctx = jax.random.normal(ks[1], (B, CTXN, CTX_DIM), jnp.float32)
        pos_map = jax.random.uniform(ks[2], (B, N, POS_DIM), jnp.float32)
        ctx_pos_map = jax.random.uniform(ks[3], (B, CTXN, POS_DIM), jnp.float32)
        Wq = jax.random.normal(ks[4], (DIM, DIM), jnp.float32) / np.sqrt(DIM)
        Wkv = jax.random.normal(ks[5], (CTX_DIM, 2 * DIM), jnp.float32) / np.sqrt(CTX_DIM)
        Wout = jax.random.normal(ks[6], (DIM, DIM), jnp.float32) / np.sqrt(DIM)
        bout = jnp.zeros((DIM,), jnp.float32)
        return {'x': x, 'ctx': ctx, 'pos_map': pos_map, 'ctx_pos_map': ctx_pos_map, 'Wq': Wq, 'Wkv': Wkv, 'Wout': Wout, 'bout': bout}
    _L1_xattn_all = _L1_xattn_setup()
    _L1_xattn_in = {k: v for k, v in _L1_xattn_all.items() if k in ('Wq', 'Wkv', 'Wout', 'bout')}
    del _L1_xattn_all

    def _L1_ffn_setup():
        import jax, jax.numpy as jnp
        import numpy as np
        H = 256
        I = 176
        E = 8
        K = 2
        B, S = (2, 256)
        key = jax.random.key(seed)
        k0, k1, k2, k3, k4 = jax.random.split(key, 5)
        scale = 1.0 / np.sqrt(H)
        x = jax.random.normal(k0, (B, S, H), dtype=jnp.float32)
        Wr = jax.random.normal(k1, (H, E), dtype=jnp.float32) * scale
        Wg = jax.random.normal(k2, (E, H, I), dtype=jnp.float32) * scale
        Wu = jax.random.normal(k3, (E, H, I), dtype=jnp.float32) * scale
        Wd = jax.random.normal(k4, (E, I, H), dtype=jnp.float32) * (1.0 / np.sqrt(I))
        return {'x': x, 'Wr': Wr, 'Wg': Wg, 'Wu': Wu, 'Wd': Wd}
    _L1_ffn_all = _L1_ffn_setup()
    _L1_ffn_in = {k: v for k, v in _L1_ffn_all.items() if k in ('Wr', 'Wg', 'Wu', 'Wd')}
    del _L1_ffn_all

    def _L2_xattn_setup():
        import jax, jax.numpy as jnp
        import numpy as np
        EPS = 1e-05

        def rmsnorm(x, g, eps=EPS):
            var = jnp.mean(jnp.square(x), axis=-1, keepdims=True)
            return x * jax.lax.rsqrt(var + eps) * g
        key = jax.random.key(seed)
        ks = jax.random.split(key, 8)
        B, Sq, Skv = (2, 512, 64)
        dim, cdim, H, D = (256, 128, 16, 128)
        inner = H * D
        s = lambda f: 1.0 / np.sqrt(f)
        return {'hidden_states': jax.random.normal(ks[0], (B, Sq, dim), jnp.float32), 'encoder_hidden_states': jax.random.normal(ks[1], (B, Skv, cdim), jnp.float32), 'Wq': jax.random.normal(ks[2], (dim, inner), jnp.float32) * s(dim), 'Wk': jax.random.normal(ks[3], (cdim, inner), jnp.float32) * s(cdim), 'Wv': jax.random.normal(ks[4], (cdim, inner), jnp.float32) * s(cdim), 'Wo': jax.random.normal(ks[5], (inner, dim), jnp.float32) * s(inner), 'gq': jnp.ones((D,), jnp.float32), 'gk': jnp.ones((D,), jnp.float32)}
    _L2_xattn_all = _L2_xattn_setup()
    _L2_xattn_in = {k: v for k, v in _L2_xattn_all.items() if k in ('Wq', 'Wk', 'Wv', 'Wo', 'gq', 'gk')}
    del _L2_xattn_all

    def _L2_ffn_setup():
        import jax, jax.numpy as jnp
        import numpy as np
        HIDDEN = 256
        EXPERT_FF = 176
        NUM_EXPERTS = 16
        NUM_SHARED = 2
        SHARED_FF = EXPERT_FF * NUM_SHARED
        TOP_K = 4
        SCALE = 1.0
        BATCH, SEQ = (1, 256)

        def _moe_forward(hidden_states, Wg, W1, W2, W3, W1s, W2s, W3s):
            B, S, D = hidden_states.shape
            x = hidden_states.reshape(-1, D)
            T = x.shape[0]
            E = Wg.shape[0]
            shared = jax.nn.silu(x @ W1s.T) * (x @ W3s.T) @ W2s.T
            logits = x @ Wg.T
            probs = jax.nn.softmax(logits.astype(jnp.float32), axis=-1)
            topk_w, sel = jax.lax.top_k(probs, TOP_K)
            topk_w = topk_w.astype(x.dtype) * SCALE
            combine = jnp.zeros((T, E), x.dtype).at[jnp.arange(T)[:, None], sel].add(topk_w)
            h = jax.nn.silu(jnp.einsum('td,efd->etf', x, W1)) * jnp.einsum('td,efd->etf', x, W3)
            routed = jnp.einsum('etf,edf->td', h * combine.T[:, :, None], W2)
            return (shared + routed).reshape(B, S, D)
        key = jax.random.key(seed)
        ks = jax.random.split(key, 8)
        std = 0.02
        return {'hidden_states': jax.random.normal(ks[0], (BATCH, SEQ, HIDDEN), dtype=jnp.float32), 'Wg': jax.random.normal(ks[1], (NUM_EXPERTS, HIDDEN), dtype=jnp.float32) * std, 'W1': jax.random.normal(ks[2], (NUM_EXPERTS, EXPERT_FF, HIDDEN), dtype=jnp.float32) * std, 'W2': jax.random.normal(ks[3], (NUM_EXPERTS, HIDDEN, EXPERT_FF), dtype=jnp.float32) * std, 'W3': jax.random.normal(ks[4], (NUM_EXPERTS, EXPERT_FF, HIDDEN), dtype=jnp.float32) * std, 'W1s': jax.random.normal(ks[5], (SHARED_FF, HIDDEN), dtype=jnp.float32) * std, 'W2s': jax.random.normal(ks[6], (HIDDEN, SHARED_FF), dtype=jnp.float32) * std, 'W3s': jax.random.normal(ks[7], (SHARED_FF, HIDDEN), dtype=jnp.float32) * std}
    _L2_ffn_all = _L2_ffn_setup()
    _L2_ffn_in = {k: v for k, v in _L2_ffn_all.items() if k in ('Wg', 'W1', 'W2', 'W3', 'W1s', 'W2s', 'W3s')}
    del _L2_ffn_all

    def _L3_xattn_setup():
        import jax, jax.numpy as jnp
        import numpy as np
        B, S1, S2, DCA = (2, 256, 128, 16)
        QDIM, KDIM, H = (256, 128, 16)
        HD = QDIM // H
        SCALE = HD ** (-0.5)
        EPS = 1e-06
        DCA_WEIGHT = 1.0

        def _ln(t, w, b):
            m = jnp.mean(t, axis=-1, keepdims=True)
            v = jnp.var(t, axis=-1, keepdims=True)
            return (t - m) * jax.lax.rsqrt(v + EPS) * w + b

        def _attn(q, k, v):
            s = jnp.einsum('bhqd,bhkd->bhqk', q, k) * SCALE
            p = jax.nn.softmax(s, axis=-1)
            return jnp.einsum('bhqk,bhkd->bhqd', p, v)
        key = jax.random.key(seed)
        ks = jax.random.split(key, 8)
        w = lambda k, shape: jax.random.normal(k, shape, jnp.float32) * 0.02
        return {'x': jax.random.normal(ks[0], (B, S1, QDIM), jnp.float32), 'y': jax.random.normal(ks[1], (B, S2 + DCA, KDIM), jnp.float32), 'Wq': w(ks[2], (QDIM, QDIM)), 'bq': jnp.zeros((QDIM,), jnp.float32), 'Wk': w(ks[3], (KDIM, QDIM)), 'bk': jnp.zeros((QDIM,), jnp.float32), 'Wv': w(ks[4], (KDIM, QDIM)), 'bv': jnp.zeros((QDIM,), jnp.float32), 'Wkv_dca': w(ks[5], (KDIM, 2 * QDIM)), 'bkv_dca': jnp.zeros((2 * QDIM,), jnp.float32), 'qn_w': jnp.ones((HD,), jnp.float32), 'qn_b': jnp.zeros((HD,), jnp.float32), 'kn_w': jnp.ones((HD,), jnp.float32), 'kn_b': jnp.zeros((HD,), jnp.float32), 'kn_dca_w': jnp.ones((HD,), jnp.float32), 'kn_dca_b': jnp.zeros((HD,), jnp.float32), 'Wo': w(ks[6], (QDIM, QDIM)), 'bo': jnp.zeros((QDIM,), jnp.float32)}
    _L3_xattn_all = _L3_xattn_setup()
    _L3_xattn_in = {k: v for k, v in _L3_xattn_all.items() if k in ('Wq', 'bq', 'Wk', 'bk', 'Wv', 'bv', 'Wkv_dca', 'bkv_dca', 'qn_w', 'qn_b', 'kn_w', 'kn_b', 'kn_dca_w', 'kn_dca_b', 'Wo', 'bo')}
    del _L3_xattn_all

    def _L3_ffn_setup():
        import jax, jax.numpy as jnp
        import numpy as np
        TOP_K = 8
        CAPACITY = 128
        key = jax.random.key(seed)
        k1, k2, k3, k4 = jax.random.split(key, 4)
        B, S, H, E, I = (2, 128, 256, 64, 96)
        hidden_states = jax.random.normal(k1, (B, S, H), dtype=jnp.float32)
        router_weight = jax.random.normal(k2, (E, H), dtype=jnp.float32) * 0.02
        gate_up_proj = jax.random.normal(k3, (E, H, 2 * I), dtype=jnp.float32) * 0.02
        down_proj = jax.random.normal(k4, (E, I, H), dtype=jnp.float32) * 0.02
        return {'hidden_states': hidden_states, 'router_weight': router_weight, 'gate_up_proj': gate_up_proj, 'down_proj': down_proj}
    _L3_ffn_all = _L3_ffn_setup()
    _L3_ffn_in = {k: v for k, v in _L3_ffn_all.items() if k in ('router_weight', 'gate_up_proj', 'down_proj')}
    del _L3_ffn_all
    return {'x': x, 'ctx_1024': ctx_1024, 'fside_BxSx2_0': fside_BxSx2_0, 'mask_BxS2_bf1': mask_BxS2_bf1, 'g_xattn': g_xattn, 'g_ffn': g_ffn, 'L0_xattn_Wq': _L0_xattn_in['Wq'], 'L0_xattn_Wk': _L0_xattn_in['Wk'], 'L0_xattn_Wv': _L0_xattn_in['Wv'], 'L0_xattn_Wo': _L0_xattn_in['Wo'], 'L0_ffn_gate_up_proj': _L0_ffn_in['gate_up_proj'], 'L0_ffn_down_proj': _L0_ffn_in['down_proj'], 'L1_xattn_Wq': _L1_xattn_in['Wq'], 'L1_xattn_Wkv': _L1_xattn_in['Wkv'], 'L1_xattn_Wout': _L1_xattn_in['Wout'], 'L1_xattn_bout': _L1_xattn_in['bout'], 'L1_ffn_Wr': _L1_ffn_in['Wr'], 'L1_ffn_Wg': _L1_ffn_in['Wg'], 'L1_ffn_Wu': _L1_ffn_in['Wu'], 'L1_ffn_Wd': _L1_ffn_in['Wd'], 'L2_xattn_Wq': _L2_xattn_in['Wq'], 'L2_xattn_Wk': _L2_xattn_in['Wk'], 'L2_xattn_Wv': _L2_xattn_in['Wv'], 'L2_xattn_Wo': _L2_xattn_in['Wo'], 'L2_xattn_gq': _L2_xattn_in['gq'], 'L2_xattn_gk': _L2_xattn_in['gk'], 'L2_ffn_Wg': _L2_ffn_in['Wg'], 'L2_ffn_W1': _L2_ffn_in['W1'], 'L2_ffn_W2': _L2_ffn_in['W2'], 'L2_ffn_W3': _L2_ffn_in['W3'], 'L2_ffn_W1s': _L2_ffn_in['W1s'], 'L2_ffn_W2s': _L2_ffn_in['W2s'], 'L2_ffn_W3s': _L2_ffn_in['W3s'], 'L3_xattn_Wq': _L3_xattn_in['Wq'], 'L3_xattn_bq': _L3_xattn_in['bq'], 'L3_xattn_Wk': _L3_xattn_in['Wk'], 'L3_xattn_bk': _L3_xattn_in['bk'], 'L3_xattn_Wv': _L3_xattn_in['Wv'], 'L3_xattn_bv': _L3_xattn_in['bv'], 'L3_xattn_Wkv_dca': _L3_xattn_in['Wkv_dca'], 'L3_xattn_bkv_dca': _L3_xattn_in['bkv_dca'], 'L3_xattn_qn_w': _L3_xattn_in['qn_w'], 'L3_xattn_qn_b': _L3_xattn_in['qn_b'], 'L3_xattn_kn_w': _L3_xattn_in['kn_w'], 'L3_xattn_kn_b': _L3_xattn_in['kn_b'], 'L3_xattn_kn_dca_w': _L3_xattn_in['kn_dca_w'], 'L3_xattn_kn_dca_b': _L3_xattn_in['kn_dca_b'], 'L3_xattn_Wo': _L3_xattn_in['Wo'], 'L3_xattn_bo': _L3_xattn_in['bo'], 'L3_ffn_router_weight': _L3_ffn_in['router_weight'], 'L3_ffn_gate_up_proj': _L3_ffn_in['gate_up_proj'], 'L3_ffn_down_proj': _L3_ffn_in['down_proj']}

def reference(x, ctx_1024, fside_BxSx2_0, mask_BxS2_bf1, g_xattn, g_ffn, L0_xattn_Wq, L0_xattn_Wk, L0_xattn_Wv, L0_xattn_Wo, L0_ffn_gate_up_proj, L0_ffn_down_proj, L1_xattn_Wq, L1_xattn_Wkv, L1_xattn_Wout, L1_xattn_bout, L1_ffn_Wr, L1_ffn_Wg, L1_ffn_Wu, L1_ffn_Wd, L2_xattn_Wq, L2_xattn_Wk, L2_xattn_Wv, L2_xattn_Wo, L2_xattn_gq, L2_xattn_gk, L2_ffn_Wg, L2_ffn_W1, L2_ffn_W2, L2_ffn_W3, L2_ffn_W1s, L2_ffn_W2s, L2_ffn_W3s, L3_xattn_Wq, L3_xattn_bq, L3_xattn_Wk, L3_xattn_bk, L3_xattn_Wv, L3_xattn_bv, L3_xattn_Wkv_dca, L3_xattn_bkv_dca, L3_xattn_qn_w, L3_xattn_qn_b, L3_xattn_kn_w, L3_xattn_kn_b, L3_xattn_kn_dca_w, L3_xattn_kn_dca_b, L3_xattn_Wo, L3_xattn_bo, L3_ffn_router_weight, L3_ffn_gate_up_proj, L3_ffn_down_proj):
    import jax
    import jax.numpy as jnp

    def _L0_xattn_ref(text_hidden, vision_tokens, vision_mask, Wq, Wk, Wv, Wo):
        import jax, jax.numpy as jnp
        import numpy as np
        N_HEADS = 16
        N_KV_HEADS = 8
        HEAD_DIM = 128
        D_TEXT = 256
        D_VISION = 128
        GROUPS = N_HEADS // N_KV_HEADS
        B, T_text, _ = text_hidden.shape
        T_vis = vision_tokens.shape[1]
        scale = jnp.float32(np.sqrt(HEAD_DIM))
        q = (text_hidden @ Wq).reshape(B, T_text, N_HEADS, HEAD_DIM).transpose(0, 2, 1, 3)
        k = (vision_tokens @ Wk).reshape(B, T_vis, N_KV_HEADS, HEAD_DIM).transpose(0, 2, 1, 3)
        v = (vision_tokens @ Wv).reshape(B, T_vis, N_KV_HEADS, HEAD_DIM).transpose(0, 2, 1, 3)
        k = jnp.repeat(k, GROUPS, axis=1)
        v = jnp.repeat(v, GROUPS, axis=1)
        scores = jnp.einsum('bhtd,bhsd->bhts', q, k) / scale
        mask = vision_mask[:, None, None, :]
        scores = jnp.where(mask, scores, -jnp.inf)
        attn = jax.nn.softmax(scores, axis=-1)
        attn = jnp.nan_to_num(attn, nan=0.0)
        out = jnp.einsum('bhts,bhsd->bhtd', attn, v)
        out = out.transpose(0, 2, 1, 3).reshape(B, T_text, N_HEADS * HEAD_DIM)
        return out @ Wo

    def _L0_ffn_ref(x, gate_up_proj, down_proj):
        import jax, jax.numpy as jnp
        import numpy as np
        NUM_EXPERTS = 4
        B, N, H = x.shape
        E, _, two_I = gate_up_proj.shape
        I = two_I // 2
        G = N // E
        x4 = x.reshape(B, G, E, H)
        gu = jnp.einsum('bgeh,ehd->bged', x4, gate_up_proj)
        gate, up = (gu[..., :I], gu[..., I:])
        inter = jax.nn.silu(gate) * up
        out = jnp.einsum('bgei,eih->bgeh', inter, down_proj)
        return out.reshape(B, N, H)

    def _L1_xattn_ref(x, ctx, pos_map, ctx_pos_map, Wq, Wkv, Wout, bout):
        import jax, jax.numpy as jnp
        import numpy as np
        DIM = 256
        CTX_DIM = 128
        N_HEADS = 32
        HEAD_DIM = DIM // N_HEADS
        POS_DIM = 2
        B, N, CTXN = (2, 256, 256)
        ROPE_BASE = 10000.0

        def apply_axial_rope(x, pos):
            b, n, h, d = x.shape
            p = pos.shape[-1]
            dpa = d // p
            half = dpa // 2
            freqs = ROPE_BASE ** (-jnp.arange(half, dtype=x.dtype) / half)
            ang = pos[..., :, None] * freqs
            cos = jnp.cos(ang)[:, :, None, :, :]
            sin = jnp.sin(ang)[:, :, None, :, :]
            xr = x.reshape(b, n, h, p, half, 2)
            x1, x2 = (xr[..., 0], xr[..., 1])
            out = jnp.stack([x1 * cos - x2 * sin, x1 * sin + x2 * cos], axis=-1)
            return out.reshape(b, n, h, d)
        b, n, _ = x.shape
        ctx_n = ctx.shape[1]
        q = (x @ Wq).reshape(b, n, N_HEADS, HEAD_DIM)
        k, v = jnp.split(ctx @ Wkv, 2, axis=-1)
        k = k.reshape(b, ctx_n, N_HEADS, HEAD_DIM)
        v = v.reshape(b, ctx_n, N_HEADS, HEAD_DIM)
        q = apply_axial_rope(q, pos_map)
        k = apply_axial_rope(k, ctx_pos_map)
        scale = 1.0 / np.sqrt(HEAD_DIM).astype(np.float32)
        logits = jnp.einsum('bqhd,bkhd->bhqk', q, k) * scale
        w = jax.nn.softmax(logits, axis=-1)
        attn = jnp.einsum('bhqk,bkhd->bqhd', w, v)
        attn = attn.reshape(b, n, N_HEADS * HEAD_DIM)
        return attn @ Wout + bout

    def _L1_ffn_ref(x, Wr, Wg, Wu, Wd):
        import jax, jax.numpy as jnp
        import numpy as np
        H = 256
        I = 176
        E = 8
        K = 2
        B, S = (2, 256)
        router_logits = jnp.einsum('bsh,he->bse', x, Wr)
        probs = jax.nn.softmax(router_logits.astype(jnp.float32), axis=-1)
        topk_w, topk_idx = jax.lax.top_k(probs, K)
        topk_w = topk_w / jnp.sum(topk_w, axis=-1, keepdims=True)
        onehot = jax.nn.one_hot(topk_idx, E, dtype=topk_w.dtype)
        combine = jnp.einsum('bsk,bske->bse', topk_w, onehot)
        g = jnp.einsum('bsh,ehi->besi', x, Wg)
        u = jnp.einsum('bsh,ehi->besi', x, Wu)
        h = jax.nn.silu(g) * u
        y = jnp.einsum('besi,eih->besh', h, Wd)
        out = jnp.einsum('bse,besh->bsh', combine.astype(x.dtype), y)
        return out

    def _L2_xattn_ref(hidden_states, encoder_hidden_states, Wq, Wk, Wv, Wo, gq, gk):
        import jax, jax.numpy as jnp
        import numpy as np
        EPS = 1e-05

        def rmsnorm(x, g, eps=EPS):
            var = jnp.mean(jnp.square(x), axis=-1, keepdims=True)
            return x * jax.lax.rsqrt(var + eps) * g
        B, Sq, _ = hidden_states.shape
        Skv = encoder_hidden_states.shape[1]
        D = gq.shape[0]
        H = Wq.shape[1] // D
        scale = 1.0 / np.sqrt(D)
        q = (hidden_states @ Wq).reshape(B, Sq, H, D)
        k = (encoder_hidden_states @ Wk).reshape(B, Skv, H, D)
        v = (encoder_hidden_states @ Wv).reshape(B, Skv, H, D)
        q = rmsnorm(q, gq)
        k = rmsnorm(k, gk)
        scores = jnp.einsum('bqhd,bkhd->bhqk', q, k) * scale
        attn = jax.nn.softmax(scores, axis=-1)
        out = jnp.einsum('bhqk,bkhd->bqhd', attn, v)
        out = out.reshape(B, Sq, H * D)
        return out @ Wo

    def _L2_ffn_ref(hidden_states, Wg, W1, W2, W3, W1s, W2s, W3s):
        import jax, jax.numpy as jnp
        import numpy as np
        HIDDEN = 256
        EXPERT_FF = 176
        NUM_EXPERTS = 16
        NUM_SHARED = 2
        SHARED_FF = EXPERT_FF * NUM_SHARED
        TOP_K = 4
        SCALE = 1.0
        BATCH, SEQ = (1, 256)

        def _moe_forward(hidden_states, Wg, W1, W2, W3, W1s, W2s, W3s):
            B, S, D = hidden_states.shape
            x = hidden_states.reshape(-1, D)
            T = x.shape[0]
            E = Wg.shape[0]
            shared = jax.nn.silu(x @ W1s.T) * (x @ W3s.T) @ W2s.T
            logits = x @ Wg.T
            probs = jax.nn.softmax(logits.astype(jnp.float32), axis=-1)
            topk_w, sel = jax.lax.top_k(probs, TOP_K)
            topk_w = topk_w.astype(x.dtype) * SCALE
            combine = jnp.zeros((T, E), x.dtype).at[jnp.arange(T)[:, None], sel].add(topk_w)
            h = jax.nn.silu(jnp.einsum('td,efd->etf', x, W1)) * jnp.einsum('td,efd->etf', x, W3)
            routed = jnp.einsum('etf,edf->td', h * combine.T[:, :, None], W2)
            return (shared + routed).reshape(B, S, D)
        return _moe_forward(hidden_states, Wg, W1, W2, W3, W1s, W2s, W3s)

    def _L3_xattn_ref(x, y, Wq, bq, Wk, bk, Wv, bv, Wkv_dca, bkv_dca, qn_w, qn_b, kn_w, kn_b, kn_dca_w, kn_dca_b, Wo, bo):
        import jax, jax.numpy as jnp
        import numpy as np
        B, S1, S2, DCA = (2, 256, 128, 16)
        QDIM, KDIM, H = (256, 128, 16)
        HD = QDIM // H
        SCALE = HD ** (-0.5)
        EPS = 1e-06
        DCA_WEIGHT = 1.0

        def _ln(t, w, b):
            m = jnp.mean(t, axis=-1, keepdims=True)
            v = jnp.var(t, axis=-1, keepdims=True)
            return (t - m) * jax.lax.rsqrt(v + EPS) * w + b

        def _attn(q, k, v):
            s = jnp.einsum('bhqd,bhkd->bhqk', q, k) * SCALE
            p = jax.nn.softmax(s, axis=-1)
            return jnp.einsum('bhqk,bhkd->bhqd', p, v)
        b, s1, _ = x.shape
        y_dca = y[:, -DCA:, :]
        y_main = y[:, :-DCA, :]
        kv_dca = (y_dca @ Wkv_dca + bkv_dca).reshape(b, DCA, 2, H, HD)
        k_dca = _ln(kv_dca[:, :, 0], kn_dca_w, kn_dca_b)
        v_dca = kv_dca[:, :, 1]
        s2 = y_main.shape[1]
        q = _ln((x @ Wq + bq).reshape(b, s1, H, HD), qn_w, qn_b)
        kv = jnp.concatenate([y_main @ Wk + bk, y_main @ Wv + bv], axis=-1)
        kv = kv.reshape(b, s2, H, 2 * HD)
        k = _ln(kv[..., :HD], kn_w, kn_b)
        v = kv[..., HD:]
        qT = q.transpose(0, 2, 1, 3)
        ctx = _attn(qT, k.transpose(0, 2, 1, 3), v.transpose(0, 2, 1, 3))
        ctx = ctx.transpose(0, 2, 1, 3).reshape(b, s1, QDIM)
        ctx_dca = _attn(qT, k_dca.transpose(0, 2, 1, 3), v_dca.transpose(0, 2, 1, 3))
        ctx_dca = ctx_dca.transpose(0, 2, 1, 3).reshape(b, s1, QDIM)
        ctx = ctx + DCA_WEIGHT * ctx_dca
        return ctx @ Wo + bo

    def _L3_ffn_ref(hidden_states, router_weight, gate_up_proj, down_proj):
        import jax, jax.numpy as jnp
        import numpy as np
        TOP_K = 8
        CAPACITY = 128
        B, S, H = hidden_states.shape
        E = router_weight.shape[0]
        K, C = (TOP_K, CAPACITY)
        x = hidden_states.reshape(-1, H)
        logits = x @ router_weight.T
        probs = jax.nn.softmax(logits, axis=-1)
        topw, topi = jax.lax.top_k(probs, K)
        topw = topw / jnp.sum(topw, axis=-1, keepdims=True)
        flat_e = topi.reshape(-1)
        oh = jax.nn.one_hot(flat_e, E, dtype=jnp.int32)
        pos = jnp.take_along_axis(jnp.cumsum(oh, axis=0), flat_e[:, None], axis=1)[:, 0] - 1
        x_rep = jnp.repeat(x, K, axis=0)
        xe = jnp.zeros((E, C, H), x.dtype).at[flat_e, pos].set(x_rep, mode='drop')
        gu = jnp.einsum('ech,ehf->ecf', xe, gate_up_proj)
        g, u = jnp.split(gu, 2, axis=-1)
        h = jax.nn.silu(g) * u
        ye = jnp.einsum('eci,eih->ech', h, down_proj)
        valid = pos < C
        y_flat = jnp.where(valid[:, None], ye[flat_e, jnp.minimum(pos, C - 1)], 0.0)
        y = jnp.sum(y_flat.reshape(-1, K, H) * topw.reshape(-1, K)[..., None], axis=1)
        return y.reshape(B, S, H)
    x = x + jnp.tanh(g_xattn[0]) * _L0_xattn_ref(_layernorm(x, axis=-1), ctx_1024, mask_BxS2_bf1, L0_xattn_Wq, L0_xattn_Wk, L0_xattn_Wv, L0_xattn_Wo)
    x = x + jnp.tanh(g_ffn[0]) * _L0_ffn_ref(_layernorm(x, axis=-1), L0_ffn_gate_up_proj, L0_ffn_down_proj)
    x = x + jnp.tanh(g_xattn[1]) * _L1_xattn_ref(_layernorm(x, axis=-1), ctx_1024, fside_BxSx2_0, fside_BxSx2_0, L1_xattn_Wq, L1_xattn_Wkv, L1_xattn_Wout, L1_xattn_bout)
    x = x + jnp.tanh(g_ffn[1]) * _L1_ffn_ref(_layernorm(x, axis=-1), L1_ffn_Wr, L1_ffn_Wg, L1_ffn_Wu, L1_ffn_Wd)
    x = x + jnp.tanh(g_xattn[2]) * _L2_xattn_ref(_layernorm(x, axis=-1), ctx_1024, L2_xattn_Wq, L2_xattn_Wk, L2_xattn_Wv, L2_xattn_Wo, L2_xattn_gq, L2_xattn_gk)
    x = x + jnp.tanh(g_ffn[2]) * _L2_ffn_ref(_layernorm(x, axis=-1), L2_ffn_Wg, L2_ffn_W1, L2_ffn_W2, L2_ffn_W3, L2_ffn_W1s, L2_ffn_W2s, L2_ffn_W3s)
    x = x + jnp.tanh(g_xattn[3]) * _L3_xattn_ref(_layernorm(x, axis=-1), ctx_1024, L3_xattn_Wq, L3_xattn_bq, L3_xattn_Wk, L3_xattn_bk, L3_xattn_Wv, L3_xattn_bv, L3_xattn_Wkv_dca, L3_xattn_bkv_dca, L3_xattn_qn_w, L3_xattn_qn_b, L3_xattn_kn_w, L3_xattn_kn_b, L3_xattn_kn_dca_w, L3_xattn_kn_dca_b, L3_xattn_Wo, L3_xattn_bo)
    x = x + jnp.tanh(g_ffn[3]) * _L3_ffn_ref(_layernorm(x, axis=-1), L3_ffn_router_weight, L3_ffn_gate_up_proj, L3_ffn_down_proj)
    return x

_drawn_inputs = setup_inputs


def setup_inputs(seed=0):
    import zlib

    import numpy as np

    out = dict(_drawn_inputs(seed))
    spreads = {'L1_xattn_bout': (0.0, 0.1),
     'L2_xattn_gq': (1.0, 0.6),
     'L2_xattn_gk': (1.0, 0.6),
     'L3_xattn_bq': (0.0, 2.0),
     'L3_xattn_bk': (0.0, 0.631),
     'L3_xattn_bv': (0.0, 0.633),
     'L3_xattn_bkv_dca': (0.0, 0.493),
     'L3_xattn_qn_w': (1.0, 0.6),
     'L3_xattn_qn_b': (0.0, 2.0),
     'L3_xattn_kn_w': (1.0, 0.6),
     'L3_xattn_kn_b': (0.0, 2.0),
     'L3_xattn_kn_dca_w': (1.0, 0.6),
     'L3_xattn_kn_dca_b': (0.0, 2.0),
     'L3_xattn_bo': (0.0, 0.1)}
    factors = {'g_ffn': 35.784,
     'L0_xattn_Wq': 4.84,
     'L0_xattn_Wk': 5.974,
     'L2_ffn_Wg': 8.0,
     'L2_ffn_W1': 8.0,
     'L2_ffn_W2': 8.0,
     'L2_ffn_W3': 8.0,
     'L2_ffn_W1s': 4.91,
     'L2_ffn_W2s': 4.798,
     'L2_ffn_W3s': 4.793,
     'L3_xattn_Wq': 4.962,
     'L3_xattn_Wk': 3.534,
     'L3_xattn_Wv': 3.598,
     'L3_ffn_router_weight': 8.0,
     'L3_ffn_gate_up_proj': 8.0,
     'L3_ffn_down_proj': 8.0}
    for name, (base, spread) in spreads.items():
        noise = np.random.default_rng([zlib.crc32(name.encode()), seed]).standard_normal(out[name].shape)
        drawn = base * np.exp(spread * noise) if base else spread * noise
        out[name] = jnp.asarray(drawn.astype(out[name].dtype))
    for name, factor in factors.items():
        out[name] = (out[name] * factor).astype(out[name].dtype)
    return out
```

```python
from contextlib import ExitStack

import concourse.bass as bass
from concourse import mybir

F32 = mybir.dt.float32
BF16 = mybir.dt.bfloat16
I32 = mybir.dt.int32
U32 = mybir.dt.uint32
U8 = mybir.dt.uint8
ACT = mybir.ActivationFunctionType
ALU = mybir.AluOpType
AX = mybir.AxisListType

P = 128
B = 16
D = 256
KD = D // P
TB = 4
W = TB * P
NS = B // TB
HEADS = 16
LN_EPS = 1e-5
RMS_EPS = 1e-5
LN3_EPS = 1e-6
TINY = 1e-30
NEG_BIG = 1e30
CREDIT = 4


class Signal:

    def __init__(self, sem, per, bodies, base):
        self.sem, self.per, self.base = sem, per, base
        self.end = base + per * bodies

    def value(self, body, item):
        return body * self.per + (self.base + item + 1)


def build(nc, a, out):
    ctx = ExitStack()
    with ctx:
        _build(nc, ctx, a, out)


def _build(nc, ctx, a, out):
    def sb(name, shape, dt=F32):
        return ctx.enter_context(nc.sbuf_tensor(name, shape, dt))

    signals = {}

    def semaphore(name):
        return ctx.enter_context(nc.semaphore(name))

    def dma_signal(name, first):
        return Signal(semaphore(name), 16, NS, 16 * first)

    def signal(name, per, bodies=NS):
        last = signals.get(name)
        if last is None:
            signals[name] = Signal(semaphore(name), per, bodies, CREDIT)
        else:
            signals[name] = Signal(last.sem, per, bodies, last.end)
        return signals[name]

    go = semaphore("go")
    waits_met = semaphore("waits_met")

    def hold(eng, sem, value):
        eng.wait_ge(sem, value)
        if not isinstance(value, int):
            eng.sem_inc(waits_met, 1)

    def done(eng, sig, body, item):
        hold(eng, sig.sem, sig.value(body, item))

    class Chain:

        def __init__(self, eng, sig, body, first=0):
            self.eng, self.sig, self.body, self.n = eng, sig, body, first

        def __call__(self, ins):
            ins.then_inc(self.sig.sem, 1)
            done(self.eng, self.sig, self.body, self.n)
            self.n += 1

        def close(self):
            assert self.n == self.sig.per, (self.sig.sem, self.n, self.sig.per)

    X = sb("x_res", [P, B, D])
    XNT = sb("xn_T", [P, KD, B * P])
    CTX = sb("ctx", [P, B, P])
    CTXT = sb("ctx_T", [P, B * P])
    YT = sb("y_T", [P, KD, W])
    XN = sb("xn", [P, TB, D])
    R1 = sb("weights_1", [P, 12288])
    R2 = sb("weights_2", [P, 19200])
    WK = sb("work", [P, 6144])
    ident = sb("ident", [P, P])
    ident_b = sb("ident_b", [P, P], BF16)
    ones_b = sb("ones_b", [1, P], BF16)
    gates = sb("gates", [P, 8])
    neg_half = sb("neg_half", [P, 512 // 8])
    bn = sb("bn", [P, TB, 6])
    mv = sb("mv", [P, TB, 2])
    var = sb("var", [P, TB])
    rstd = sb("rstd", [P, TB])
    any_key = sb("any_key", [P, B])
    mx = sb("mx", [P, 2, TB])
    negm = sb("negm", [P, 2, TB])
    sums = sb("sums", [P, 2, TB])
    rinv = sb("rinv", [P, 2, TB])

    PS = ctx.enter_context(nc.psum_tensor("ps", [P, 8, 512], F32))
    Y = [PS[:, 0, :], PS[:, 1, :]]
    TP = PS[:, 2, :]
    B3 = PS[:, 3, :]
    B4, B5, B6, B7 = (PS[:, i, :] for i in range(4, 8))

    def mm(out, lhsT, rhs, start=True, stop=True):
        return nc.tensor.matmul(out, lhsT, rhs, start=start, stop=stop, skip_group_check=True)

    def tok(s):
        return bass.ds(s * W, W)

    def tile(x, o, n):
        return x[:, o:o + n]

    l0_wq = tile(R1, 0, 4096).rearrange("p (k n) -> p k n", k=KD)
    l0_wk = tile(R1, 4096, 1024)
    l0_wv = tile(R1, 5120, 1024)
    l0_wo = tile(R1, 6144, 4096).rearrange("p (h n) -> p h n", h=HEADS)
    l0_gu = tile(R2, 0, 4096).rearrange("p (e k n) -> p e k n", e=4, k=KD)
    l0_dn = tile(R2, 4096, 2048).rearrange("p (e k n) -> p e k n", e=4, k=KD)

    q_sb = tile(WK, 0, 1024).rearrange("p (n c) -> p n c", n=2)
    p_sb = tile(WK, 1024, 2048).rearrange("p (n c) -> p n c", n=4)
    pt_sb = tile(WK, 3072, 512)
    o_sb = tile(WK, 3584, 1024).rearrange("p (n c) -> p n c", n=2)
    ctx_s = tile(WK, 4608, 512).rearrange("p (t c) -> p t c", t=TB)
    k0_sb = tile(WK, 5120, 1024).rearrange("p (n c) -> p n c", n=2)
    wv_t = tile(WK, 0, 2048)
    mask_all = tile(WK, 0, 512).bitcast(U8)
    mask_bias = tile(R2, 17000, 1024).bitcast(BF16)
    mask_row = tile(R2, 18024, 512).bitcast(U8)
    ctxt_s = tile(WK, 5120, 512)
    qsq_sb = tile(WK, 5632, 512)
    kr_sb = tile(R2, 0, 2 * HEADS * W).rearrange("p (n h c) -> p n h c", n=2, h=HEADS)
    kn_sb = tile(R2, 2 * HEADS * W, 512)
    ksq_sb = tile(R2, 2 * HEADS * W + 512, 512)
    ones_col = sb("ones_col", [P, 1])
    gqk = sb("gqk", [P, 1])
    gk = sb("gk", [P, 1])
    ksq = sb("ksq", [P, 2, 4])
    kvar = sb("kvar", [P, 2, 4])
    rk = sb("rk", [P, 2, 4])
    qvar = sb("qvar", [P, 2, 4])
    rq = sb("rq", [P, 2, 4])

    in_x = semaphore("in_x")
    in_ctx = semaphore("in_ctx")
    in_small = semaphore("in_small")
    in_l0x = semaphore("in_l0x")
    in_l0f = semaphore("in_l0f")
    out_done = semaphore("out_done")
    ident_made = semaphore("ident_made")
    const_made = semaphore("const_made")
    gates_ready = semaphore("gates_ready")
    mask_ready = semaphore("mask_ready")
    ctx_tr = signal("ctx_tr", NS, 1)
    ctxt_ready = signal("ctxt_ready", NS, 1)
    yt_ready = signal("yt_ready", KD)
    yt_tr = signal("yt_tr", 2)
    y_added = signal("y_added", 2)
    var_ready = signal("var_ready", 1)
    rstd_ready = signal("rstd_ready", 1)
    xn_ready = signal("xn_ready", 1)
    xn_tr = signal("xn_tr", KD)
    xnt_ready = signal("xnt_ready", KD)
    tail_chain = signal("tail_chain", 2)
    xs_stored = dma_signal("xs_stored", 1)

    def tail_pe_y(pe, n, j):
        if j == 0:
            done(pe, yt_ready, n, 1)
            done(pe, xnt_ready, n, -1)
        else:
            done(pe, y_added, n, 0)
        for t in range(2):
            for h in range(KD):
                last = nc.tensor.transpose(TP[:, t * D + h * P:t * D + (h + 1) * P],
                                           YT[:, h, (2 * j + t) * P:(2 * j + t + 1) * P], ident[:])
        last.then_inc(yt_tr.sem, 1)

    def tail_pe_xn(pe, n, k):
        if k == 0:
            done(pe, xn_ready, n, 0)
        else:
            done(pe, xnt_ready, n, 0)
        for t in range(TB):
            last = nc.tensor.transpose(TP[:, t * P:(t + 1) * P], XN[:, t, k * P:(k + 1) * P], ident[:])
        last.then_inc(xn_tr.sem, 1)

    def tail_dve_add(dve, n, s, j):
        done(dve, yt_tr, n, j)
        x2 = X[:, bass.ds(s * TB + 2 * j, 2), :]
        nc.vector.tensor_tensor(x2, TP.rearrange("p (t d) -> p t d", t=2), x2, ALU.add).then_inc(y_added.sem, 1)

    def tail_dve_norm(dve, n, s, store=None):
        link = Chain(dve, tail_chain, n)
        done(dve, y_added, n, 1)
        for t in range(TB):
            ins = nc.vector.bn_stats(bn[:, t, :], X[:, bass.ds(s * TB + t, 1), :].rearrange("p t d -> p (t d)"))
        link(ins)
        for t in range(TB):
            ins = nc.vector.bn_aggr(mv[:, t, :], bn[:, t, :])
        link(ins)
        nc.vector.tensor_scalar(var[:], mv[:, :, 1], LN_EPS, None, ALU.add).then_inc(var_ready.sem, 1)
        done(dve, rstd_ready, n, 0)
        if store is not None:
            done(dve, xs_stored, store, -1)
        for t in range(TB):
            ins = nc.vector.tensor_scalar(XN[:, t, :], X[:, bass.ds(s * TB + t, 1), :].rearrange("p t d -> p (t d)"),
                                          mv[:, t, 0:1], rstd[:, t:t + 1], ALU.subtract, ALU.mult)
        ins.then_inc(xn_ready.sem, 1)
        link.close()

    def tail_pool(pool, n):
        done(pool, var_ready, n, 0)
        nc.gpsimd.tensor_tensor(out=rstd[:], in0=var[:], in1=neg_half[:, 0:TB], op=ALU.pow).then_inc(rstd_ready.sem, 1)

    def tail_act(act, n, s, k):
        done(act, xn_tr, n, k)
        nc.scalar.activation(XNT[:, k, tok(s)], TP, ACT.Copy).then_inc(xnt_ready.sem, 1)

    def tail_pe(pe, n):
        for j in range(2):
            tail_pe_y(pe, n, j)
        for k in range(KD):
            tail_pe_xn(pe, n, k)

    def tail_dve(dve, n, s, store=None):
        for j in range(2):
            tail_dve_add(dve, n, s, j)
        tail_dve_norm(dve, n, s, store)

    def tail_of(i, s):
        return s + (NS - 1 + NS * i), (s + NS - 1) % NS

    class Wide:

        def __init__(self, name, stage, kv_heads, wq, wk, wv, wo, rms):
            self.name, self.stage, self.kv_heads, self.rms = name, stage, kv_heads, rms
            self.wq, self.wk, self.wv, self.wo = wq, wk, wv, wo
            self.share = HEADS // kv_heads
            self.wv_tr = signal("wide_wv_tr", kv_heads // 4, 1)
            self.wvt_ready = signal("wide_wvt_ready", kv_heads // 4, 1)
            self.wvo_mm = signal("wide_wvo_mm", HEADS // 2, 1)
            self.wvo_ready = signal("wide_wvo_ready", HEADS // 2, 1)
            self.ctx_ready = signal("wide_ctx_ready", 1)
            self.k_mm = signal("wide_k_mm", kv_heads)
            self.k_ready = signal("wide_k_ready", kv_heads)
            self.q_mm = signal("wide_q_mm", HEADS)
            self.q_ready = signal("wide_q_ready", HEADS)
            self.s_mm = signal("wide_s_mm", HEADS)
            self.negm_ready = signal("wide_negm_ready", HEADS)
            self.p_ready = signal("wide_p_ready", HEADS)
            self.rinv_ready = signal("wide_rinv_ready", HEADS)
            self.pn_ready = signal("wide_pn_ready", HEADS)
            self.pt_tr = signal("wide_pt_tr", HEADS)
            self.pt_ready = signal("wide_pt_ready", HEADS)
            self.o_mm = signal("wide_o_mm", HEADS)
            self.o_ready = signal("wide_o_ready", HEADS)
            self.y_mm = signal("wide_y_mm", HEADS)
            self.chain = signal("wide_chain", HEADS * (1 if rms else 3))
            if rms:
                self.qsq_mm = signal("wide_qsq_mm", HEADS)
                self.qvar_ready = signal("wide_qvar_ready", HEADS)
                self.rq_ready = signal("wide_rq_ready", HEADS)
                self.kctx_ready = signal("wide_kctx_ready", 1)
                self.k_chain = signal("wide_k_chain", HEADS)
                self.kt_mm = signal("wide_kt_mm", HEADS)
                self.ksq_ready = signal("wide_ksq_ready", HEADS)
                self.kvar_ready = signal("wide_kvar_ready", HEADS)
                self.rk_ready = signal("wide_rk_ready", HEADS)
                self.kn_ready = signal("wide_kn_ready", HEADS)
                self.kn_tr = signal("wide_kn_tr", HEADS)

    SCALE_WIDE = float(P) ** -0.5
    T_LAG = 4
    Y_LAG = 5

    def wide_prep_pe(pe, A):
        if A.rms:
            done(pe, A.k_ready, 0, HEADS - 1)
        for g in range(A.kv_heads // 4):
            if g >= 2:
                done(pe, A.wvt_ready, 0, g - 2)
            for j in range(4):
                last = nc.tensor.transpose((B4, B5)[g % 2][:, j * P:(j + 1) * P], A.wv[:, (4 * g + j) * P:(4 * g + j + 1) * P],
                                           ident[:])
            last.then_inc(A.wv_tr.sem, 1)
        for c in range(HEADS // 2):
            done(pe, A.wvt_ready, 0, min((2 * c + 1) // A.share // 4, A.kv_heads // 4 - 1))
            if c >= 2:
                done(pe, A.wvo_ready, 0, c - 2)
            for j in range(2):
                h = 2 * c + j
                g = h // A.share
                last = mm((B6, B7)[c % 2][:, j * D:(j + 1) * D], wv_t[:, g * P:(g + 1) * P], A.wo[:, h, :])
            last.then_inc(A.wvo_mm.sem, 1)

    def wide_prep_act(act, A):
        for g in range(A.kv_heads // 4):
            done(act, A.wv_tr, 0, g)
            nc.scalar.activation(wv_t[:, g * W:(g + 1) * W], (B4, B5)[g % 2], ACT.Copy).then_inc(A.wvt_ready.sem, 1)
        for c in range(HEADS // 2):
            done(act, A.wvo_mm, 0, c)
            nc.scalar.activation(A.wo[:, 2 * c:2 * c + 2, :].rearrange("p h n -> p (h n)"), (B6, B7)[c % 2],
                                 ACT.Copy).then_inc(A.wvo_ready.sem, 1)

    def key_mm(pe, A, u, bank):
        hq, b = u // 4, u % 4
        mm(bank, ctxt_s[:, b * P:(b + 1) * P], A.wk[:, hq * W:(hq + 1) * W]).then_inc(A.kt_mm.sem, 1)

    def key_tr(pe, A, body, u, bank):
        done(pe, A.kn_ready, body, u)
        done(pe, A.k_ready, body, u - 1)
        for j in range(4):
            last = nc.tensor.transpose(bank[:, j * P:(j + 1) * P], kn_sb[:, j * P:(j + 1) * P], ident[:])
        last.then_inc(A.kn_tr.sem, 1)

    def key_square(act, A, body, u, bank):
        done(act, A.kt_mm, body, u)
        done(act, A.kvar_ready, body, u - 1)
        nc.scalar.activation(ksq_sb, bank, ACT.Square).then_inc(A.ksq_ready.sem, 1)

    def key_out(act, A, body, u, bank):
        hq, b = u % HEADS // 4, u % 4
        done(act, A.kn_tr, body, u)
        half = (body if u >= 0 else body - 1) % 2
        dst = kr_sb[:, bass.ds(half, 1), 4 * hq:4 * hq + 4, b * P:(b + 1) * P].rearrange("p n h c -> p (n h) c")
        nc.scalar.activation(dst, bank.rearrange("p (j c) -> p j c", j=4), ACT.Copy, scale=gqk[:, 0:1]).then_inc(A.k_ready.sem, 1)

    def key_var(dve, A, body, u, link):
        done(dve, A.ksq_ready, body, u)
        link(nc.vector.tensor_reduce(ksq[:, u % 2, :], ksq_sb.rearrange("p (j c) -> p j c", j=4), AX.X, ALU.add))
        nc.vector.tensor_scalar(kvar[:, u % 2, :], ksq[:, u % 2, :], 1.0 / P, RMS_EPS, ALU.mult, ALU.add)\
            .then_inc(A.kvar_ready.sem, 1)

    def key_norm(dve, A, body, u, bank):
        done(dve, A.rk_ready, body, u)
        done(dve, A.kn_tr, body, u - 1)
        nc.vector.tensor_tensor(kn_sb.rearrange("p (j c) -> p j c", j=4), bank.rearrange("p (j c) -> p j c", j=4),
                                rk[:, u % 2, :].unsqueeze(2).broadcast_to([P, 4, P]), ALU.mult).then_inc(A.kn_ready.sem, 1)

    def key_rms(pool, A, body, u):
        done(pool, A.kvar_ready, body, u)
        nc.gpsimd.tensor_tensor(out=rk[:, u % 2, :], in0=kvar[:, u % 2, :], in1=neg_half[:, 0:4], op=ALU.pow)\
            .then_inc(A.rk_ready.sem, 1)

    KEY_BANKS = (B3, B5, B7)

    def first_keys_pe(pe, A):
        done(pe, A.kctx_ready, 0, 0)
        for u in range(HEADS + 2):
            if u < HEADS:
                done(pe, A.kn_ready, 0, max(u - 3, -1))
                key_mm(pe, A, u, KEY_BANKS[u % 3])
            if u >= 2:
                key_tr(pe, A, 0, u - 2, (B4, B6)[u % 2])

    def first_keys_act(act, A):
        for u in range(HEADS + 3):
            if u < HEADS:
                key_square(act, A, 0, u, KEY_BANKS[u % 3])
            if u >= 3:
                key_out(act, A, 0, u - 3, (B4, B6)[(u - 1) % 2])

    def first_keys_dve(dve, A):
        link = Chain(dve, A.k_chain, 0)
        for u in range(HEADS + 1):
            if u < HEADS:
                key_var(dve, A, 0, u, link)
            if u >= 1:
                key_norm(dve, A, 0, u - 1, KEY_BANKS[(u - 1) % 3])
        link.close()

    def first_keys_pool(pool, A):
        nc.gpsimd.tensor_copy(ctxt_s, CTXT[:, 0:W]).then_inc(A.kctx_ready.sem, 1)
        for u in range(HEADS):
            key_rms(pool, A, 0, u)

    class Body:

        def __init__(self, A, s, new=True, old=True, ahead=False, old_ahead=False):
            self.A, self.s, self.new, self.old, self.ahead, self.old_ahead = A, s, new, old, ahead, old_ahead
            self.steps = range(HEADS if new else Y_LAG)
            if new:
                self.n, self.prev = tail_of(A.stage, s)

        def has(self, h):
            return self.new if h >= 0 else self.old

        def keys(self, u):
            return self.ahead if u >= 0 else self.old_ahead

        def of(self, h):
            return self.s if h >= 0 else self.s - 1

        def chain(self, eng, sig, late, body):
            return Chain(eng, sig, body, -late if self.old else 0)

    TAIL_T = Y_LAG + 2

    def wide_run(engine, A, eng):
        last = NS - 1 if A.rms else NS
        engine(eng, Body(A, 0, old=False, ahead=A.rms))
        with eng.Fori(1, last, 1) as s:
            engine(eng, Body(A, s, ahead=A.rms, old_ahead=A.rms))
        if A.rms:
            engine(eng, Body(A, last, old_ahead=True))
        engine(eng, Body(A, NS, new=False))

    def wide_pe(pe, S):
        A, s = S.A, S.s

        def keys0(g):
            done(pe, A.k_ready, s, g - 1)
            mm(B3, A.wk[:, g * P:(g + 1) * P], CTXT[:, tok(s)]).then_inc(A.k_mm.sem, 1)

        if S.new:
            done(pe, xnt_ready, s + NS * A.stage, 1)
            if not A.rms:
                keys0(0)
        for t in S.steps:
            h = t - T_LAG
            if S.new:
                done(pe, A.qvar_ready if A.rms else A.q_ready, s, t - 1)
                for k in range(KD):
                    last = mm(B4, A.wq[:, k, t * P:(t + 1) * P], XNT[:, k, tok(s)], k == 0, k == KD - 1)
                last.then_inc(A.q_mm.sem, 1)
            if S.has(h):
                done(pe, A.pn_ready, s, h)
                done(pe, A.pt_ready, s, h - 1)
                if S.keys(t - 2):
                    done(pe, A.k_ready, s + 1, t - 2)
                for b in range(TB):
                    last = nc.tensor.transpose(B6[:, b * P:(b + 1) * P], p_sb[:, h % 4, b * P:(b + 1) * P], ident[:])
                last.then_inc(A.pt_tr.sem, 1)
            i = t - 1
            if S.has(i):
                done(pe, A.q_ready, s, i)
                done(pe, A.p_ready, s, i - 1)
                if A.rms:
                    done(pe, A.k_ready, s, i // 4 * 4 + 3)
                else:
                    done(pe, A.k_ready, s, i // A.share)
                    mm(B5, ones_b[0:1, :], mask_bias[0:1, tok(S.of(i))], True, False)
                for b in range(TB):
                    if A.rms:
                        keys = kr_sb[:, bass.ds(S.of(i) % 2, 1), i % HEADS, b * P:(b + 1) * P].rearrange("p n c -> p (n c)")
                    else:
                        keys = k0_sb[:, i // A.share % 2, b * P:(b + 1) * P]
                    last = mm(B5[:, b * P:(b + 1) * P], q_sb[:, i % 2, b * P:(b + 1) * P], keys, A.rms, True)
                last.then_inc(A.s_mm.sem, 1)
            i = t - Y_LAG
            if S.has(i):
                done(pe, A.o_ready, s, i)
                if i == 0:
                    done(pe, yt_ready, S.n, 1)
                for k in range(KD):
                    last = mm(Y[k], A.wo[:, i % HEADS, k * P:(k + 1) * P], o_sb[:, i % 2, :], i % HEADS == 0, i == -1 or i == HEADS - 1)
                last.then_inc(A.y_mm.sem, 1)
            if S.has(h):
                done(pe, A.pt_ready, s, h)
                done(pe, A.o_ready, s, h - 1)
                if h == 0:
                    done(pe, A.ctx_ready, s, 0)
                for b in range(TB):
                    last = mm(B7[:, b * P:(b + 1) * P], ctx_s[:, b, :], pt_sb[:, b * P:(b + 1) * P])
                last.then_inc(A.o_mm.sem, 1)
            if S.new and A.rms:
                done(pe, A.q_ready, s, t)
                for b in range(TB):
                    last = mm(B4[:, b:b + 1], qsq_sb[:, b * P:(b + 1) * P], ones_col[:])
                last.then_inc(A.qsq_mm.sem, 1)
            if S.ahead:
                if t == 0:
                    done(pe, A.kctx_ready, s + 1, 0)
                done(pe, A.kn_ready, s + 1, t - 1)
                key_mm(pe, A, t, B3)
            if S.keys(t - 1):
                key_tr(pe, A, s + 1, t - 1, B6)
            if S.new and not A.rms and t % A.share == A.share - 1 and (t + 1) // A.share < A.kv_heads:
                keys0((t + 1) // A.share)
            if S.new and t - TAIL_T in (0, 1):
                tail_pe_y(pe, S.n, t - TAIL_T)
            if S.new and t - TAIL_T in (4, 5):
                tail_pe_xn(pe, S.n, t - TAIL_T - 4)

    def wide_act(act, S):
        A, s = S.A, S.s

        def keys0(g):
            done(act, A.k_mm, s, g)
            done(act, A.s_mm, s, (g - 1) * A.share - 1)
            nc.scalar.activation(k0_sb[:, g % 2, :], B3, ACT.Copy).then_inc(A.k_ready.sem, 1)

        def out_of_y(n):
            done(act, yt_tr, n - 1, 1)
            done(act, A.y_mm, s, -1)
            g = A.stage // 2
            for k in range(KD):
                nc.scalar.activation(YT[:, k, :], Y[k], ACT.Copy, scale=gates[:, g:g + 1]).then_inc(yt_ready.sem, 1)

        if S.new and not A.rms:
            keys0(0)
        for t in S.steps:
            if t == Y_LAG and S.old:
                out_of_y(S.n)
            if S.keys(t - 2):
                key_out(act, A, s + 1, t - 2, B6)
            if S.keys(t - 1):
                key_square(act, A, s + 1, t - 1, B3)
            if S.new and not A.rms and t and t % A.share == 0:
                keys0(t // A.share)
            if S.new:
                done(act, A.q_mm, s, t)
                done(act, A.s_mm, s, t - 2)
                ins = nc.scalar.activation(q_sb[:, t % 2, :], B4, ACT.Copy)
                if A.rms:
                    done(act, A.qsq_mm, s, t - 1)
                    ins = nc.scalar.activation(qsq_sb, B4, ACT.Square)
                ins.then_inc(A.q_ready.sem, 1)
            h = t - 1
            if S.has(h):
                done(act, A.negm_ready, s, h)
                done(act, A.pt_tr, s, h - 4)
                for b in range(TB):
                    last = nc.scalar.activation(p_sb[:, h % 4, b * P:(b + 1) * P], B5[:, b * P:(b + 1) * P], ACT.Exp,
                                                bias=negm[:, h % 2, b:b + 1],
                                                scale=rq[:, h % 2, b:b + 1] if A.rms else SCALE_WIDE,
                                                accum_out=sums[:, h % 2, b:b + 1])
                last.then_inc(A.p_ready.sem, 1)
            h = t - T_LAG
            if S.has(h):
                done(act, A.o_mm, s, h)
                done(act, A.y_mm, s, h - 2)
                nc.scalar.activation(o_sb[:, h % 2, :], B7, ACT.Copy).then_inc(A.o_ready.sem, 1)
            if S.new and t - TAIL_T in (4, 5):
                tail_act(act, S.n, S.prev, t - TAIL_T - 4)
        if not S.new:
            out_of_y(tail_of(A.stage, s)[0])

    def wide_dve(dve, S):
        A, s = S.A, S.s
        link = S.chain(dve, A.chain, 1 if A.rms else 5, s)
        if S.ahead or S.old_ahead:
            k_link = Chain(dve, A.k_chain, s + 1, -1 if S.old_ahead else 0)
        for t in S.steps:
            h = t - 2
            if S.has(h):
                i = h % 2
                done(dve, A.p_ready, s, h)
                done(dve, A.pn_ready, s, h - 2)
                if A.rms:
                    nc.vector.reciprocal(rinv[:, i, :], sums[:, i, :]).then_inc(A.rinv_ready.sem, 1)
                else:
                    link(nc.vector.tensor_scalar(mx[:, i, :], sums[:, i, :], TINY, None, ALU.max))
                    link(nc.vector.reciprocal(mx[:, i, :], mx[:, i, :]))
                    nc.vector.tensor_tensor(rinv[:, i, :], mx[:, i, :], any_key[:, bass.ds(S.of(h) * TB, TB)], ALU.mult)\
                        .then_inc(A.rinv_ready.sem, 1)
            if S.keys(t - 1):
                key_var(dve, A, s + 1, t - 1, k_link)
            h = t - T_LAG
            if S.has(h):
                done(dve, A.pt_tr, s, h)
                done(dve, A.o_mm, s, h - 1)
                nc.vector.tensor_copy(pt_sb, B6).then_inc(A.pt_ready.sem, 1)
            if S.keys(t - 1):
                key_norm(dve, A, s + 1, t - 1, B3)
            h = t - 1
            if S.has(h):
                i = h % 2
                done(dve, A.s_mm, s, h)
                link(nc.vector.tensor_reduce(mx[:, i, :], B5.rearrange("p (b k) -> p b k", b=TB), AX.X, ALU.max))
                if A.rms:
                    done(dve, A.rq_ready, s, h)
                    nc.vector.scalar_tensor_tensor(negm[:, i, :], mx[:, i, :], -1.0, rq[:, i, :], ALU.mult, ALU.mult)\
                        .then_inc(A.negm_ready.sem, 1)
                else:
                    nc.vector.tensor_scalar(negm[:, i, :], mx[:, i, :], -SCALE_WIDE, None, ALU.mult)\
                        .then_inc(A.negm_ready.sem, 1)
            if S.new and A.rms:
                done(dve, A.qsq_mm, s, t)
                done(dve, A.p_ready, s, t - 2)
                nc.vector.tensor_scalar(qvar[:, t % 2, :], B4[:, 0:TB], 1.0 / P, RMS_EPS, ALU.mult, ALU.add)\
                    .then_inc(A.qvar_ready.sem, 1)
            if S.new and t - TAIL_T in (0, 1):
                tail_dve_add(dve, S.n, S.prev, t - TAIL_T)
            if S.new and t - TAIL_T == 2:
                tail_dve_norm(dve, S.n, S.prev)

    def wide_pool(pool, S):
        A, s = S.A, S.s
        if S.new and not S.old:
            done(pool, yt_ready, S.n, 1)
        if S.ahead:
            done(pool, A.kt_mm, s, HEADS - 1)
            nc.gpsimd.tensor_copy(ctxt_s, CTXT[:, tok(s + 1)]).then_inc(A.kctx_ready.sem, 1)
        for t in S.steps:
            h = t - 2
            if S.has(h):
                done(pool, A.rinv_ready, s, h)
                pv = p_sb[:, h % 4, :].rearrange("p (b k) -> p b k", b=TB)
                nc.gpsimd.tensor_tensor(out=pv, in0=pv, in1=rinv[:, h % 2, :].unsqueeze(2).broadcast_to([P, TB, P]),
                                        op=ALU.mult).then_inc(A.pn_ready.sem, 1)
            if S.keys(t - 1):
                key_rms(pool, A, s + 1, t - 1)
            if S.new and A.rms:
                done(pool, A.qvar_ready, s, t)
                nc.gpsimd.tensor_tensor(out=rq[:, t % 2, :], in0=qvar[:, t % 2, :], in1=neg_half[:, 0:4], op=ALU.pow)\
                    .then_inc(A.rq_ready.sem, 1)
            if S.new and t == T_LAG - 1:
                done(pool, A.o_mm, s, -1)
                nc.gpsimd.tensor_copy(ctx_s, CTX[:, bass.ds(s * TB, TB), :]).then_inc(A.ctx_ready.sem, 1)
            if S.new and t - TAIL_T == 2:
                tail_pool(pool, S.n)


    L0 = Wide("a0", 0, 8, l0_wq, l0_wk, l0_wv, l0_wo, False)

    E0 = 4
    sg0 = tile(WK, 0, 512).rearrange("p (n c) -> p n c", n=2)
    h0 = tile(WK, 512, 512).rearrange("p (n k c) -> p n k c", n=2, k=2)
    f0_gu = signal("moe_g_mm", E0)
    f0_sg = signal("moe_sg_ready", E0)
    f0_h = signal("moe_h_ready", E0)
    f0_y = signal("moe_y_mm", E0)
    TE = W // E0

    def ffn0_pe(pe, i, s):
        n, prev = tail_of(i, s)
        done(pe, xnt_ready, s + NS * i, 1)
        xe = XNT.rearrange("p k (s t e) -> p k s e t", s=NS, e=E0)
        for e in range(E0 + 1):
            if e < E0:
                done(pe, f0_h, s, max(e - 2, -1))
                bank = (B4, B5)[e % 2]
                for m in range(4):
                    for k in range(KD):
                        rhs = xe[:, k, bass.ds(s, 1), e, :].rearrange("p s t -> p (s t)")
                        last = mm(bank[:, m * P:(m + 1) * P], l0_gu[:, e, k, m * P:(m + 1) * P], rhs, k == 0, k == KD - 1)
                last.then_inc(f0_gu.sem, 1)
            if e < 2:
                tail_pe_y(pe, n, e)
            if e >= 3:
                tail_pe_xn(pe, n, e - 3)
            if e >= 1:
                j = e - 1
                done(pe, f0_h, s, j)
                if j == 0:
                    done(pe, yt_ready, n, 1)
                for k in range(KD):
                    for m in range(2):
                        last = mm(Y[k][:, j * TE:(j + 1) * TE], l0_dn[:, j, m, k * P:(k + 1) * P], h0[:, j % 2, m, :],
                                  m == 0, m == 1)
                last.then_inc(f0_y.sem, 1)

    def ffn0_act(act, i, s):
        n, prev = tail_of(i, s)
        for e in range(E0):
            done(act, f0_gu, s, e)
            done(act, f0_h, s, max(e - 2, -1))
            nc.scalar.activation(sg0[:, e % 2, :], (B4, B5)[e % 2][:, 0:2 * P], ACT.Silu).then_inc(f0_sg.sem, 1)
        tail_act(act, n, prev, 0)
        done(act, yt_tr, n, 1)
        done(act, f0_y, s, E0 - 1)
        g = 4 + i // 2
        for k in range(KD):
            nc.scalar.activation(YT[:, k, :].rearrange("p (t e) -> p e t", e=E0), Y[k].rearrange("p (e t) -> p e t", e=E0),
                                 ACT.Copy, scale=gates[:, g:g + 1]).then_inc(yt_ready.sem, 1)
        tail_act(act, n, prev, 1)

    def ffn0_dve(dve, i, s):
        n, prev = tail_of(i, s)
        for e in range(E0):
            done(dve, f0_sg, s, e)
            done(dve, f0_y, s, max(e - 2, -1))
            nc.vector.tensor_tensor(h0[:, e % 2, :, :].rearrange("p k c -> p (k c)"), sg0[:, e % 2, :],
                                    (B4, B5)[e % 2][:, 2 * P:4 * P], ALU.mult).then_inc(f0_h.sem, 1)
            if e < 2:
                tail_dve_add(dve, n, prev, e)
            if e == 1:
                tail_dve_norm(dve, n, prev)

    def ffn0_pool(pool, i, s):
        n, prev = tail_of(i, s)
        tail_pool(pool, n)

    NB = 4

    class Narrow:

        def __init__(self, name, stage, heads, main, wout, bias):
            self.name, self.stage, self.heads, self.wout, self.bias = name, stage, heads, wout, bias
            self.split = main < P
            self.parts = ((0, 0, main), (1, main, P)) if self.split else ((0, 0, P),)
            self.hd = D // heads
            self.rows = NB * self.hd
            self.per_half = P // self.rows
            self.groups = KD * self.per_half
            self.n = TB * self.groups
            self.units = TB * KD
            n, u = self.n, self.units
            self.chain = signal("narrow_chain", n + u)
            self.qk_ready = signal("narrow_qk_ready", 1)
            self.kblk_ready = signal("narrow_kblk_ready", u)
            self.s_mm = signal("narrow_s_mm", n)
            self.negm_ready = signal("narrow_negm_ready", n)
            self.p_ready = signal("narrow_p_ready", n)
            self.rinv_ready = signal("narrow_rinv_ready", n)
            self.pn_ready = signal("narrow_pn_ready", n)
            self.pt_tr = signal("narrow_pt_tr", n)
            self.pt_ready = signal("narrow_pt_ready", n)
            self.o_mm = signal("narrow_o_mm", n)
            self.ot_ready = signal("narrow_ot_ready", u)
            self.y_mm = signal("narrow_y_mm", KD)

    n_p = tile(WK, 0, 2048).rearrange("p (n h k) -> p n h k", n=4, h=NB)
    n_pt = tile(WK, 2048, 1024).rearrange("p (n c) -> p n c", n=2)
    n_kblk = tile(WK, 3072, 1024).rearrange("p (n h k) -> p n h k", n=2, h=NB)
    n_own = tile(WK, 4096, 1024).rearrange("p (n h q) -> p n h q", n=2, h=NB)
    n_mx = sb("n_mx", [P, 4, 2 * NB])
    n_negm = sb("n_negm", [P, 4, 2 * NB])
    n_sums = sb("n_sums", [P, 4, 2 * NB])
    n_rinv = sb("n_rinv", [P, 4, 2 * NB])
    N_LAG = 4
    V_LAG = N_LAG + 1
    N_END = V_LAG + 1
    S_BANKS = (B4, B5, B3)

    def narrow_pe(pe, A, s, q_t, v_pad, o_t, beside=None):
        n, prev = tail_of(A.stage, s)
        done(pe, A.qk_ready, s, 0)
        for t in range(A.n + N_END):
            if N_LAG <= t < A.n + N_LAG:
                u = t - N_LAG
                done(pe, A.pn_ready, s, u)
                done(pe, A.pt_ready, s, u - 1)
                for j in range(NB):
                    last = nc.tensor.transpose(B6[:, j * P:(j + 1) * P], n_p[:, u % 4, j, :], ident[:])
                last.then_inc(A.pt_tr.sem, 1)
            if t < A.n:
                c, r = t // A.per_half, t % A.per_half
                b, hf = c // KD, c % KD
                r0 = r * A.rows
                if r == 0:
                    done(pe, A.kblk_ready, s, c)
                done(pe, A.p_ready, s, max(t - 3, -1))
                mm(S_BANKS[t % 3], q_t[r0:r0 + A.rows, hf, b * P:(b + 1) * P],
                   n_kblk[r0:r0 + A.rows, c % 2, :, :].rearrange("p h k -> p (h k)")).then_inc(A.s_mm.sem, 1)
            if V_LAG <= t < A.n + V_LAG:
                u = t - V_LAG
                c, r = u // A.per_half, u % A.per_half
                b, hf = c // KD, c % KD
                done(pe, A.pt_ready, s, u)
                if u == 0:
                    done(pe, yt_ready, n, 1)
                if r == 0:
                    done(pe, A.ot_ready, s, max(c - 2, -1))
                mm(narrow_out(c), v_pad[:, b, hf, r, :], n_pt[:, u % 2, :], r == 0, r == A.per_half - 1).then_inc(A.o_mm.sem, 1)
            if t in (2, 3):
                tail_pe_y(pe, n, t - 2)
            if t in (6, 7):
                tail_pe_xn(pe, n, t - 6)
            if beside is not None:
                beside(t)
        done(pe, A.ot_ready, s, A.units - 1)
        for k in range(KD):
            for hf in range(KD):
                last = mm(Y[k], A.wout[:, hf, k * P:(k + 1) * P], o_t[:, hf, :], hf == 0, hf == KD - 1)
            last.then_inc(A.y_mm.sem, 1)

    def narrow_out(c):
        return (B7, Y[1])[c % 2]

    def narrow_act(act, A, s, scale, beside=None):
        n, prev = tail_of(A.stage, s)
        for t in range(A.n + N_END):
            if not A.split and N_LAG <= t < A.n + N_LAG:
                u = t - N_LAG
                done(act, A.pt_tr, s, u)
                done(act, A.o_mm, s, max(u - 2, -1))
                nc.scalar.activation(n_pt[:, u % 2, :], B6, ACT.Copy).then_inc(A.pt_ready.sem, 1)
            if t < A.n:
                i = t % 4
                done(act, A.negm_ready, s, t)
                done(act, A.pt_tr, s, max(t - 4, -1))
                done(act, A.rinv_ready, s, max(t - 4, -1))
                for x, lo, hi in A.parts:
                    for j in range(NB):
                        m = x * NB + j
                        last = nc.scalar.activation(n_p[:, i, j, lo:hi], S_BANKS[t % 3][:, j * P + lo:j * P + hi], ACT.Exp,
                                                    bias=n_negm[:, i, m:m + 1], scale=scale, accum_out=n_sums[:, i, m:m + 1])
                last.then_inc(A.p_ready.sem, 1)
            if t in (6, 7):
                tail_act(act, n, prev, t - 6)
            if beside is not None:
                beside(t)
        done(act, yt_tr, n, 1)
        g = A.stage // 2
        for k in range(KD):
            done(act, A.y_mm, s, k)
            nc.scalar.activation(YT[:, k, :], Y[k], ACT.Identity, scale=gates[:, g:g + 1], bias=A.bias[:, k:k + 1])\
                .then_inc(yt_ready.sem, 1)

    def narrow_dve(dve, A, s, o_t, head_mask, scale, beside=None):
        n, prev = tail_of(A.stage, s)
        link = Chain(dve, A.chain, s)
        m = NB * len(A.parts)
        for t in range(A.n + N_END):
            if A.split and N_LAG <= t < A.n + N_LAG:
                u = t - N_LAG
                done(dve, A.pt_tr, s, u)
                done(dve, A.o_mm, s, max(u - 2, -1))
                nc.vector.tensor_copy(n_pt[:, u % 2, :], B6).then_inc(A.pt_ready.sem, 1)
            if t < A.n:
                done(dve, A.s_mm, s, t)
                bank = S_BANKS[t % 3].rearrange("p (h k) -> p h k", h=NB)
                for x, lo, hi in A.parts:
                    ins = nc.vector.tensor_reduce(n_mx[:, t % 4, x * NB:(x + 1) * NB], bank[:, :, lo:hi], AX.X, ALU.max)
                link(ins)
                done(dve, A.p_ready, s, max(t - 4, -1))
                nc.vector.tensor_scalar(n_negm[:, t % 4, 0:m], n_mx[:, t % 4, 0:m], -scale, None, ALU.mult)\
                    .then_inc(A.negm_ready.sem, 1)
            if 1 <= t <= A.n:
                u = t - 1
                done(dve, A.p_ready, s, u)
                done(dve, A.pn_ready, s, max(u - 4, -1))
                nc.vector.reciprocal(n_rinv[:, u % 4, 0:m], n_sums[:, u % 4, 0:m]).then_inc(A.rinv_ready.sem, 1)
            if t in (2, 3):
                tail_dve_add(dve, n, prev, t - 2)
            if t == 4:
                tail_dve_norm(dve, n, prev, s if A.split else None)
            u = t - V_LAG
            if u > 0 and u % A.per_half == 0:
                c = u // A.per_half - 1
                b, hf = c // KD, c % KD
                done(dve, A.o_mm, s, u - 1)
                link(nc.vector.tensor_tensor(n_own[:, c % 2], narrow_out(c).rearrange("p (h q) -> p h q", h=NB),
                                             head_mask[:].unsqueeze(2).broadcast_to([P, NB, P]), ALU.mult))
                if c == 0:
                    done(dve, A.y_mm, s, -1)
                nc.vector.tensor_reduce(o_t[:, hf, b * P:(b + 1) * P], n_own[:, c % 2].rearrange("p h q -> p q h"), AX.X, ALU.add)\
                    .then_inc(A.ot_ready.sem, 1)
            if beside is not None:
                beside(t)
        link.close()

    def narrow_pool(pool, A, s, k_t, head_mask, beside=None):
        n, prev = tail_of(A.stage, s)
        done(pool, A.qk_ready, s, 0)

        def key_blocks(c):
            b, hf = c // KD, c % KD
            done(pool, A.s_mm, s, max((c - 1) * A.per_half - 1, -1))
            nc.gpsimd.tensor_tensor(out=n_kblk[:, c % 2, :, :],
                                    in0=k_t[:, hf, b * P:(b + 1) * P].unsqueeze(1).broadcast_to([P, NB, P]),
                                    in1=head_mask[:].unsqueeze(2).broadcast_to([P, NB, P]),
                                    op=ALU.mult).then_inc(A.kblk_ready.sem, 1)

        key_blocks(0)
        key_blocks(1)
        for t in range(A.n + 2):
            if t >= 2:
                u = t - 2
                done(pool, A.rinv_ready, s, u)
                for x, lo, hi in A.parts:
                    pv = n_p[:, u % 4, :, lo:hi]
                    ins = nc.gpsimd.tensor_tensor(out=pv, in0=pv, op=ALU.mult,
                                                  in1=n_rinv[:, u % 4, x * NB:(x + 1) * NB].unsqueeze(2).broadcast_to([P, NB, hi - lo]))
                ins.then_inc(A.pn_ready.sem, 1)
            if t and t % A.per_half == 0 and t // A.per_half + 1 < A.units:
                key_blocks(t // A.per_half + 1)
            if t == 5:
                tail_pool(pool, n)
            if beside is not None:
                beside(t)

    L1H, L1HD = 32, 8
    TWO_PI_HI = 6.28125
    TWO_PI_LO = 2 * 3.141592653589793 - TWO_PI_HI
    ROUND = 1.5 * 2 ** 23
    PI = 3.1415925
    l1_wq = tile(R2, 6144, 512).rearrange("p (k n) -> p k n", k=KD)
    l1_wqs = tile(R2, 6656, 512).rearrange("p (k n) -> p k n", k=KD)
    l1_wkv = tile(R2, 7168, 512)
    l1_wks = tile(R2, 7680, 256)
    l1_wout = tile(R2, 7936, 512).rearrange("p (k n) -> p k n", k=KD)
    pos_t = tile(R2, 17000, 2048)
    r_cos = tile(R2, 8448, 512)
    r_sin = tile(R2, 8960, 512)
    r_k = tile(R2, 9472, 512)
    r_a = tile(R2, 9984, 512)
    r_b = tile(R2, 10496, 512)
    l1_q = tile(R2, 11008, 1024).rearrange("p (k c) -> p k c", k=KD)
    l1_k = tile(R2, 12032, 1024).rearrange("p (k c) -> p k c", k=KD)
    l1_v = tile(R1, 0, TB * KD * 4 * P).rearrange("p (t h r c) -> p t h r c", t=TB, h=KD, r=4)
    l1_ot = tile(R2, 14080, 1024).rearrange("p (k c) -> p k c", k=KD)
    l1_cs = tile(R2, 15104, 512)
    freq = sb("freq", [2, P])
    hmask8 = sb("hmask8", [P, NB])
    hmask16 = sb("hmask16", [P, NB])
    head_sel8 = sb("head_sel8", [P, 4, NB])
    head_sel16 = sb("head_sel16", [P, 2, NB])
    pool_consts = semaphore("pool_consts")
    hmask_ready = semaphore("hmask_ready")
    l1_bias = sb("l1_bias", [P, KD])
    in_l1x = semaphore("in_l1x")
    l1w_ready = semaphore("l1w_ready")
    L1 = Narrow("a1", 2, L1H, P, l1_wout, l1_bias)
    l1_ctx = signal("narrow_in_ready", 1)
    ang_mm = signal("a1_ang_mm", 1)
    ang_ready = signal("a1_ang_ready", 2)
    sin_ready = signal("a1_sin_ready", 2)
    rope_mm = signal("a1_rope_mm", 4)
    rope_ready = signal("a1_rope_ready", 4)
    rope_chain = signal("narrow_qk_chain", 13)
    l1_v_mm = signal("narrow_v_mm", 2)

    ROPE_BANKS = ((B5, B6), (B7, B4), (B5, B6), (B7, B4))

    def rope_pe(pe, s):
        done(pe, xnt_ready, s + NS * L1.stage, 1)
        mm(B4, freq[0:2, :], pos_t[0:2, tok(s)]).then_inc(ang_mm.sem, 1)
        for i in range(4):
            hf = i % 2
            if i == 1:
                done(pe, ang_ready, s, 1)
            if i >= 2:
                done(pe, rope_ready, s, i - 2)
            for bank, wq, wk in zip(ROPE_BANKS[i], (l1_wq, l1_wqs), (l1_wkv, l1_wks)):
                if i < 2:
                    for k in range(KD):
                        last = mm(bank, wq[:, k, hf * P:(hf + 1) * P], XNT[:, k, tok(s)], k == 0, k == KD - 1)
                else:
                    last = mm(bank, wk[:, hf * P:(hf + 1) * P], CTXT[:, tok(s)])
            last.then_inc(rope_mm.sem, 1)
        done(pe, l1_ctx, s, 0)
        done(pe, rope_ready, s, 2)
        for j in range(2):
            for t in range(2):
                b = 2 * j + t
                last = mm((B5, B6)[j][:, t * D:(t + 1) * D], l1_cs[:, b * P:(b + 1) * P], l1_wkv[:, D:2 * D])
            last.then_inc(l1_v_mm.sem, 1)

    def rope_act(act, s):
        for i, dst in enumerate((r_sin, r_cos)):
            done(act, ang_ready, s, i)
            nc.scalar.activation(dst, dst, ACT.Sin).then_inc(sin_ready.sem, 1)
        for j in range(2):
            if j == 1:
                done(act, rope_ready, s, 3)
            done(act, l1_v_mm, s, j)
            v = (B5, B6)[j].rearrange("p (t h r c) -> p t h r c", t=2, h=KD, r=4)
            for r in range(4):
                c = slice(r * P // 4, (r + 1) * P // 4)
                ins = nc.scalar.activation(l1_v[:, 2 * j:2 * j + 2, :, r, c], v[:, :, :, r, :], ACT.Copy)
        ins.then_inc(L1.qk_ready.sem, 1)

    def rope_dve(dve, s):
        link = Chain(dve, rope_chain, s)
        done(dve, ang_mm, s, 0)
        for dst, shift in ((r_sin, 0.0), (r_cos, 0.25)):
            link(nc.vector.tensor_scalar(r_k, B4, 1.0 / (TWO_PI_HI + TWO_PI_LO), shift, ALU.mult, ALU.add))
            link(nc.vector.tensor_scalar(r_k, r_k, ROUND, -ROUND, ALU.add, ALU.add))
            link(nc.vector.scalar_tensor_tensor(r_a, r_k, -TWO_PI_HI, B4, ALU.mult, ALU.add))
            link(nc.vector.scalar_tensor_tensor(r_b, r_k, -TWO_PI_LO, r_a, ALU.mult, ALU.add))
            if shift:
                link(nc.vector.tensor_scalar(r_b, r_b, 0.5 * 3.141592653589793, None, ALU.add))
            nc.vector.tensor_scalar(dst, r_b, -PI, PI, ALU.max, ALU.min).then_inc(ang_ready.sem, 1)
        done(dve, sin_ready, s, 1)
        for i in range(4):
            done(dve, rope_mm, s, i)
            dst = (l1_q, l1_k)[i // 2][:, i % 2, :]
            nc.vector.tensor_tensor(r_a, ROPE_BANKS[i][0], r_cos, ALU.mult)
            link(nc.vector.tensor_tensor(r_b, ROPE_BANKS[i][1], r_sin, ALU.mult))
            nc.vector.tensor_tensor(dst, r_a, r_b, ALU.add).then_inc(rope_ready.sem, 1)
            done(dve, rope_ready, s, i)
        link.close()

    def rope_pool(pool, s):
        n, prev = tail_of(L1.stage, s)
        done(pool, yt_ready, n, 1)
        nc.gpsimd.tensor_copy(l1_cs, CTXT[:, tok(s)]).then_inc(l1_ctx.sem, 1)


    class Router:

        def __init__(self, name, stage, experts, top_k, w, arena, base, banks):
            self.name, self.stage, self.E, self.K, self.w = name, stage, experts, top_k, w
            self.lg_bank, self.lt_bank = banks
            self.lg_mm = signal("moe_lg_mm", 1)
            self.lg_ready = signal("moe_lg_ready", 1)
            self.lg_tr = signal("moe_lg_tr", 1)
            self.sub_ready = signal("moe_sub_ready", 1)
            self.e_ready = signal("moe_e_ready", 1)
            self.chain = None
            o = [base]

            def take(n):
                o[0] += n
                return tile(arena, o[0] - n, n)

            E = experts
            self.lg_sb = take(W)
            self.e = take(TB * E).rearrange("p (t e) -> p t e", t=TB)
            self.c = take(TB * E).rearrange("p (t e) -> p t e", t=TB)
            self.oh = take(TB * E).rearrange("p (t e) -> p t e", t=TB)
            self.top = take(TB * 8).rearrange("p (t k) -> p t k", t=TB)
            self.ixf = take(TB * 8).rearrange("p (t k) -> p t k", t=TB)
            self.ix = take(TB * 8).bitcast(U32).rearrange("p (t k) -> p t k", t=TB)
            self.small = take(4 * TB)
            self.end = o[0]

    iota = sb("iota", [P, 64])
    iota_i = sb("iota_i", [P, 64], I32)

    def router_logits(pe, A, s):
        done(pe, xnt_ready, s + NS * A.stage, 1)
        for k in range(KD):
            last = mm(A.lg_bank[0:A.E, :], A.w[:, k, :], XNT[:, k, tok(s)], k == 0, k == KD - 1)
        last.then_inc(A.lg_mm.sem, 1)

    def router_turn(pe, A, s):
        done(pe, A.lg_ready, s, 0)
        for t in range(TB):
            last = nc.tensor.transpose(A.lt_bank[:, t * A.E:(t + 1) * A.E], A.lg_sb[0:A.E, t * P:(t + 1) * P], ident[0:A.E, 0:A.E])
        last.then_inc(A.lg_tr.sem, 1)

    def router_out(act, A, s):
        done(act, A.lg_mm, s, 0)
        nc.scalar.activation(A.lg_sb[0:A.E, :], A.lg_bank[0:A.E, :], ACT.Copy).then_inc(A.lg_ready.sem, 1)

    def router_exp(act, A, s):
        done(act, A.sub_ready, s, 0)
        nc.scalar.activation(A.e, A.e, ACT.Exp).then_inc(A.e_ready.sem, 1)

    def router_sub(dve, A, s, link):
        done(dve, A.lg_tr, s, 0)
        lg = A.lt_bank[:, 0:TB * A.E].rearrange("p (t e) -> p t e", t=TB)
        top1 = A.small[:, 0:TB]
        link(nc.vector.tensor_reduce(top1, lg, AX.X, ALU.max))
        nc.vector.tensor_tensor(A.e, lg, top1.unsqueeze(2).broadcast_to([P, TB, A.E]), ALU.subtract).then_inc(A.sub_ready.sem, 1)

    def router_top(dve, A, s, link, over_all):
        den = A.small[:, TB:2 * TB]
        done(dve, A.e_ready, s, 0)
        for t in range(TB):
            ins = nc.vector.max(A.top[:, t, :], A.e[:, t, :])
        link(ins)
        for t in range(TB):
            ins = nc.vector.max_index(A.ix[:, t, :], A.top[:, t, :], A.e[:, t, :])
        link(ins)
        nc.vector.tensor_copy(A.ixf, A.ix)
        link(nc.vector.tensor_reduce(den, A.e if over_all else A.top[:, :, 0:A.K], AX.X, ALU.add))
        link(nc.vector.reciprocal(den, den))
        link(nc.vector.tensor_tensor(A.top, A.top, den.unsqueeze(2).broadcast_to([P, TB, 8]), ALU.mult))

    def one_hot(A, k):
        return nc.vector.tensor_tensor(A.oh, iota[:, 0:A.E].unsqueeze(1).broadcast_to([P, TB, A.E]),
                                       A.ixf[:, :, k:k + 1].broadcast_to([P, TB, A.E]), ALU.is_equal)

    class Dense:

        def __init__(self, name, stage, router, ff, extra, wg, wu, wd, sel):
            self.name, self.stage, self.r = name, stage, router
            self.cols = router.E * ff
            self.total = self.cols + extra
            self.ff = ff
            self.m = -(-self.total // P)
            self.routed = self.cols // P
            self.wg, self.wu, self.wd = wg, wu, wd
            self.E3 = 3 * router.E
            router.chain = signal("moe_r_chain", 3 * router.K + 9)
            self.c_ready = signal("moe_c_ready", 1)
            self.c_tr = signal("moe_c_tr", 1)
            self.ct_ready = signal("moe_ct_ready", 1)
            self.g_mm = signal("moe_g_mm", self.m)
            self.u_mm = signal("moe_u_mm", self.m)
            self.w_mm = signal("moe_w_mm", self.routed)
            self.sg_ready = signal("moe_sg_ready", self.m)
            self.su_ready = signal("moe_su_ready", self.m)
            self.h_ready = signal("moe_h_ready", self.m)
            self.y_mm = signal("moe_y_mm", self.m)
            o = router.end
            self.c3 = tile(WK, o, TB * self.E3 // 2).bitcast(BF16).rearrange("p (t x e) -> p t x e", t=TB, x=3)
            o += TB * self.E3 // 2
            self.ct = tile(WK, o, W // 2).bitcast(BF16)
            o += W // 2
            self.sg = tile(WK, o, 2 * W).rearrange("p (n c) -> p n c", n=2)
            self.h = tile(WK, o + 2 * W, 2 * W).rearrange("p (n c) -> p n c", n=2)
            self.sel = sel.bitcast(BF16)

        def width(self, m):
            return min(P, self.total - m * P)

    def dense_pe(pe, A, s):
        n, prev = tail_of(A.stage, s)
        router_logits(pe, A.r, s)
        router_turn(pe, A.r, s)
        tail_pe_y(pe, n, 0)
        done(pe, A.c_ready, s, 0)
        b7 = B7.bitcast(BF16)
        for t in range(TB):
            last = nc.tensor.transpose(b7[0:A.E3, t * P:(t + 1) * P], A.c3[:, t, :, :].rearrange("p x e -> p (x e)"), ident_b[:])
        last.then_inc(A.c_tr.sem, 1)
        for m in range(A.m + 1):
            if m < A.m:
                w = A.width(m)
                for sig, wt, bank, freed in ((A.g_mm, A.wg, B4, A.sg_ready), (A.u_mm, A.wu, B5, A.su_ready)):
                    done(pe, freed, s, m - 1)
                    for k in range(KD):
                        last = mm(bank[0:w, :], wt[:, k, m * P:m * P + w], XNT[:, k, tok(s)], k == 0, k == KD - 1)
                    last.then_inc(sig.sem, 1)
            if m >= 1:
                j = m - 1
                w = A.width(j)
                done(pe, A.h_ready, s, j)
                if j == 0:
                    done(pe, yt_ready, n, 1)
                for k in range(KD):
                    last = mm(Y[k], A.wd[0:w, j, k * P:(k + 1) * P], A.h[0:w, j % 2, :], j == 0, j == A.m - 1)
                last.then_inc(A.y_mm.sem, 1)
            if m < A.routed:
                done(pe, A.h_ready, s, m - 1)
                done(pe, A.ct_ready, s, 0)
                mm(B6, A.sel[0:A.E3, m * P:(m + 1) * P], A.ct[0:A.E3, :]).then_inc(A.w_mm.sem, 1)
            if m == 2:
                tail_pe_y(pe, n, 1)
            if m in (5, 7):
                tail_pe_xn(pe, n, (m - 5) // 2)

    def dense_act(act, A, s):
        n, prev = tail_of(A.stage, s)
        router_out(act, A.r, s)
        router_exp(act, A.r, s)
        done(act, A.c_tr, s, 0)
        nc.scalar.activation(A.ct[0:A.E3, :], B7.bitcast(BF16)[0:A.E3, 0:W], ACT.Copy).then_inc(A.ct_ready.sem, 1)
        for m in range(A.m):
            w = A.width(m)
            done(act, A.g_mm, s, m)
            done(act, A.h_ready, s, max(m - 2, -1))
            nc.scalar.activation(A.sg[0:w, m % 2, :], B4[0:w, :], ACT.Silu).then_inc(A.sg_ready.sem, 1)
            if m in (5, 7):
                tail_act(act, n, prev, (m - 5) // 2)
        done(act, yt_tr, n, 1)
        done(act, A.y_mm, s, A.m - 1)
        g = 4 + A.stage // 2
        for k in range(KD):
            nc.scalar.activation(YT[:, k, :], Y[k], ACT.Copy, scale=gates[:, g:g + 1]).then_inc(yt_ready.sem, 1)

    def dense_dve(dve, A, s, over_all):
        n, prev = tail_of(A.stage, s)
        R = A.r
        link = Chain(dve, R.chain, s)
        router_sub(dve, R, s, link)
        router_top(dve, R, s, link, over_all)
        for k in range(R.K):
            link(one_hot(R, k))
            link(nc.vector.tensor_tensor(R.c if k == 0 else R.oh, R.oh, R.top[:, :, k:k + 1].broadcast_to([P, TB, R.E]), ALU.mult))
            if k:
                link(nc.vector.tensor_tensor(R.c, R.c, R.oh, ALU.add))
        link(nc.vector.tensor_copy(A.c3[:, :, 0, :], R.c))
        link(nc.vector.tensor_tensor(R.c, R.c, A.c3[:, :, 0, :], ALU.subtract))
        link(nc.vector.tensor_copy(A.c3[:, :, 1, :], R.c))
        link(nc.vector.tensor_tensor(R.c, R.c, A.c3[:, :, 1, :], ALU.subtract))
        nc.vector.tensor_copy(A.c3[:, :, 2, :], R.c).then_inc(A.c_ready.sem, 1)
        link.close()
        for m in range(A.m):
            w = A.width(m)
            done(dve, A.sg_ready, s, m)
            done(dve, A.u_mm, s, m)
            done(dve, A.y_mm, s, max(m - 2, -1))
            if m < A.routed:
                nc.vector.tensor_tensor(A.sg[0:w, m % 2, :], A.sg[0:w, m % 2, :], B5[0:w, :], ALU.mult).then_inc(A.su_ready.sem, 1)
                done(dve, A.su_ready, s, m)
                done(dve, A.w_mm, s, m)
                nc.vector.tensor_tensor(A.h[0:w, m % 2, :], A.sg[0:w, m % 2, :], B6[0:w, :], ALU.mult).then_inc(A.h_ready.sem, 1)
            else:
                nc.vector.tensor_tensor(A.h[0:w, m % 2, :], A.sg[0:w, m % 2, :], B5[0:w, :], ALU.mult).then_inc(A.su_ready.sem, 1)
                done(dve, A.su_ready, s, m)
                dve.sem_inc(A.h_ready.sem, 1)
            if m in (0, 2):
                tail_dve_add(dve, n, prev, m // 2)
            if m == 3:
                tail_dve_norm(dve, n, prev)

    def dense_pool(pool, A, s):
        n, prev = tail_of(A.stage, s)
        tail_pool(pool, n)

    def make_sel(ordered, A, sel, tmp):
        for x in range(3):
            part = tmp.bitcast(BF16)[0:A.E3, 0:A.cols]
            ordered(nc.gpsimd.memset(part, 1.0))
            for sign, base in ((1, 0), (-1, A.ff - 1)):
                ordered(nc.gpsimd.affine_select(out=part, in_=part, compare_op=ALU.is_ge, fill=0.0,
                                                base=base + sign * A.ff * A.r.E * x, pattern=[[sign, A.cols]],
                                                channel_multiplier=-sign * A.ff))
            if x == 0:
                ordered(nc.gpsimd.tensor_copy(sel[0:A.E3, :], part))
            else:
                ordered(nc.gpsimd.tensor_tensor(out=sel[0:A.E3, :], in0=sel[0:A.E3, :], in1=part, op=ALU.add))

    L1E, L1F, L1K = 8, 176, 2
    l1_wr = tile(R2, 15616, KD * L1E).rearrange("p (k n) -> p k n", k=KD)
    l1_wg = tile(R2, 0, KD * L1E * L1F).rearrange("p (k n) -> p k n", k=KD)
    l1_wu = tile(R2, 2816, KD * L1E * L1F).rearrange("p (k n) -> p k n", k=KD)
    l1_wd = tile(R2, 6144, L1E * L1F * D // P).rearrange("p (m n) -> p m n", n=D)
    F1 = Dense("f1", 3, Router("f1", 3, L1E, L1K, l1_wr, WK, 0, (B4, B5)), L1F, 0, l1_wg, l1_wu, l1_wd, tile(R2, 15632, 704))
    in_l1f = semaphore("in_l1f")

    l2_wq = tile(R1, 0, 4096).rearrange("p (k n) -> p k n", k=KD)
    l2_wk = tile(R1, 4096, 2048)
    l2_wv = tile(R1, 6144, 2048)
    l2_wo = tile(R1, 8192, 4096).rearrange("p (h n) -> p h n", h=HEADS)
    in_l2x = semaphore("in_l2x")
    gqk_ready = semaphore("gqk_ready")
    L2 = Wide("a2", 4, 16, l2_wq, l2_wk, l2_wv, l2_wo, True)

    L2E, L2F, L2S, L2K = 16, 176, 352, 4
    L2C = L2E * L2F + L2S
    L2M = -(-L2C // P)
    l2_w1t = tile(R2, 0, KD * L2C).rearrange("p (k n) -> p k n", k=KD)
    l2_w3t = tile(R2, 6336, KD * L2C).rearrange("p (k n) -> p k n", k=KD)
    l2_w2t = tile(R2, 12672, L2M * D).rearrange("p (m n) -> p m n", n=D)
    l2_wr = tile(R2, 19072, KD * L2E).rearrange("p (k n) -> p k n", k=KD)
    l2_sel_made = tile(R2, 17408, 1408)
    l2_sel = tile(WK, 4700, 1408)
    F2 = Dense("f2", 5, Router("f2", 5, L2E, L2K, l2_wr, WK, 0, (B4, B5)), L2F, L2S, l2_w1t, l2_w3t, l2_w2t, l2_sel)
    RING = 8
    raw = tile(R1, 0, RING * 6 * P).rearrange("p (n c) -> p n c", n=RING)
    raw_in = [semaphore(f"raw_in{i}") for i in range(RING)]
    raw_count = [0] * RING
    raw_after = []
    wr_raw = tile(R2, 18816, D)[0:16, :]
    wr_tr = signal("small_tr", 1, 1)
    wr_ready = signal("small_ready", 1, 1)
    sel_moved = semaphore("sel_moved")
    prep_tr = signal("prep_tr", L2M, 1)
    prep_act = signal("prep_act", L2M, 1)
    prep_dve = signal("prep_dve", L2M, 1)

    def chunk_dmas(m):
        w = F2.width(m)
        slot = raw[:, m % RING, :]
        halves = slot[:, 4 * P:6 * P].rearrange("p (h c) -> p h c", h=KD)
        routed = m < F2.routed
        r0 = m * P if routed else (m - F2.routed) * P
        for x, name in enumerate(("W1", "W3")):
            src = a["L2_ffn_" + name].rearrange("e f d -> (e f) d") if routed else a["L2_ffn_" + name + "s"]
            yield slot[0:w, x * D:(x + 1) * D], src[r0:r0 + w, :]
        if not routed:
            yield halves[:, :, 0:w], a["L2_ffn_W2s"][:, r0:r0 + w].rearrange("(h p) f -> p h f", p=P)
            return
        at = r0
        while at < r0 + w:
            e, f0 = divmod(at, L2F)
            n = min(L2F - f0, r0 + w - at)
            yield halves[:, :, at - r0:at - r0 + n], a["L2_ffn_W2"][e, :, f0:f0 + n].rearrange("(h p) f -> p h f", p=P)
            at += n

    def prep_sp(sp):
        done(sp, L2.y_mm, NS - 1, HEADS - 1)
        for m in range(L2M):
            if m >= RING:
                done(sp, prep_tr, 0, m - RING)
            for dst, src in chunk_dmas(m):
                sp.dma_start(dst, src).then_inc(raw_in[m % RING], 16)

    def prep_pe(pe):
        count = [0] * RING
        for k in range(KD):
            last = nc.tensor.transpose(B4[:, k * L2E:(k + 1) * L2E], wr_raw[:, k * P:(k + 1) * P], ident[0:L2E, 0:L2E])
        last.then_inc(wr_tr.sem, 1)
        done(pe, wr_ready, 0, 0)
        for m in range(L2M):
            w = F2.width(m)
            count[m % RING] += 16 * len(list(chunk_dmas(m)))
            pe.wait_ge(raw_in[m % RING], count[m % RING])
            if m >= 2:
                done(pe, prep_act, 0, m - 2)
                done(pe, prep_dve, 0, m - 2)
            slot = raw[:, m % RING, :]
            for j in range(4):
                nc.tensor.transpose((B4, B5)[m % 2][:, j * P:j * P + w], slot[0:w, j * P:(j + 1) * P], ident[0:w, 0:w])
            for j in range(KD):
                last = nc.tensor.transpose((B6, B7)[m % 2][0:w, j * P:(j + 1) * P], slot[:, (4 + j) * P:(4 + j) * P + w], ident[:])
            last.then_inc(prep_tr.sem, 1)

    def prep_act_engine(act):
        done(act, L2.y_mm, NS - 1, HEADS - 1)
        act.wait_ge(pool_consts, 3)
        nc.scalar.activation(F2.sel[0:F2.E3, :], l2_sel_made.bitcast(BF16)[0:F2.E3, :], ACT.Copy).then_inc(sel_moved, 1)
        done(act, wr_tr, 0, 0)
        nc.scalar.activation(l2_wr.rearrange("p k n -> p (k n)"), B4[:, 0:KD * L2E], ACT.Copy).then_inc(wr_ready.sem, 1)
        for m in range(L2M):
            w = F2.width(m)
            done(act, prep_tr, 0, m)
            bank = (B4, B5)[m % 2].rearrange("p (x k c) -> p x k c", x=2, k=KD)
            nc.scalar.activation(l2_w1t[:, :, m * P:m * P + w], bank[:, 0, :, 0:w], ACT.Copy)
            nc.scalar.activation(l2_w3t[:, :, m * P:m * P + w], bank[:, 1, :, 0:w], ACT.Copy).then_inc(prep_act.sem, 1)

    def prep_dve_engine(dve):
        dve.wait_ge(sel_moved, 1)
        for m in range(L2M):
            w = F2.width(m)
            done(dve, prep_tr, 0, m)
            nc.vector.tensor_copy(l2_w2t[0:w, m, :], (B6, B7)[m % 2][0:w, 0:D]).then_inc(prep_dve.sem, 1)

    L3H, L3HD = 16, 16
    MAIN = P - 16
    l3_wq = tile(R1, 0, 512).rearrange("p (k n) -> p k n", k=KD)
    l3_cat = tile(R1, 512, 512)
    l3_wm = tile(R1, 1024, 512)
    l3_wd = tile(R1, 1536, 512)
    l3_wo = tile(R1, 2048, 512).rearrange("p (k n) -> p k n", k=KD)
    l3_bqk = tile(R1, 2560, 512)
    vec_rows = tile(R1, 3072, P)
    l3_vec = tile(R1, 3200, 6)
    l3_bo = tile(R1, 3206, KD)
    l3_mean = tile(R1, 3210, 96)
    l3_bv = tile(R1, 3328, D)
    l3_x = tile(R1, 3840, 1024).rearrange("p (k c) -> p k c", k=KD)
    l3_cm = tile(R1, 4864, 512)
    l3_cd = tile(R1, 5376, 512)
    l3_qk = tile(R1, 5888, 2048).rearrange("p (b c) -> p b c", b=TB)
    l3_sq = [tile(x, o, W) for x, o in ((R1, 7936), (R1, 7936 + W), (WK, 5120), (WK, 5120 + W))]
    l3_b1 = tile(R1, 7936, D)
    l3_b2 = tile(R1, 7936 + D, D)
    l3_q = tile(R1, 8960, 1024).rearrange("p (k c) -> p k c", k=KD)
    l3_k = tile(R1, 9984, 1024).rearrange("p (k c) -> p k c", k=KD)
    l3_ot = tile(R1, 11008, 1024).rearrange("p (k c) -> p k c", k=KD)
    l3_var = tile(R1, 12032, 128).rearrange("p (b g) -> p b g", b=TB)
    l3_r = tile(R1, 12160, 128).rearrange("p (b g) -> p b g", b=TB)
    l3_v = tile(R2, 0, TB * KD * 2 * P).rearrange("p (t h r c) -> p t h r c", t=TB, h=KD, r=2)
    l3_zero_row = tile(R1, 5888, D)
    in_l3x = semaphore("in_l3x")
    vec_tr = signal("small_tr", 1, 1)
    vec_ready = signal("small_ready", 2, 1)
    L3 = Narrow("a3", 6, L3H, MAIN, l3_wo, l3_bo)
    l3_w = signal("l3_w_ready", 4, 1)
    l3_in = signal("narrow_in_ready", 1, NS + 1)
    l3_qk_mm = signal("l3_qk_mm", TB)
    l3_v_mm = signal("narrow_v_mm", 2)
    l3_v_ready = signal("l3_v_ready", 1)
    l3_add = signal("l3_add", TB)
    l3_sq_ready = signal("l3_sq_ready", TB)
    l3_chain = signal("narrow_qk_chain", 2)
    l3_var_ready = signal("l3_var_ready", 1)
    l3_sd_ready = signal("l3_sd_ready", 1)
    l3_n_ready = signal("l3_n_ready", TB)
    l3_tr = signal("l3_tr", TB)
    xs = nc.dram_tensor("xn_rows", ((B + 1) * P, D), F32, kind="Internal").ap()
    xs_rows = xs.rearrange("(b p) d -> p b d", p=P)
    L3_LOADS = 18

    def l3_loads(sp):
        done(sp, prep_tr, 0, L2M - 1)
        w = "L3_xattn_"
        count = 0

        def load(dst, src):
            nonlocal count
            sp.dma_start(dst, src).then_inc(in_l3x, 16)
            count += 1

        load(l3_wq, a[w + "Wq"].rearrange("(k p) n -> p k n", p=P))
        load(l3_cat[:, 0:D], a[w + "Wk"])
        load(l3_cat[:, D:2 * D], a[w + "Wv"])
        load(l3_wd, a[w + "Wkv_dca"])
        load(l3_wo, a[w + "Wo"].rearrange("(k p) n -> p k n", p=P))
        load(l3_bo, a[w + "bo"].rearrange("(k p) -> p k", p=P))
        for j, name in enumerate(("qn_w", "qn_b", "kn_w", "kn_b", "kn_dca_w", "kn_dca_b")):
            load(vec_rows[j:j + 1, :].rearrange("p (g d) -> p g d", d=L3HD),
                 a[w + name].rearrange("(o u d) -> o u d", o=1, u=1).broadcast_to([1, P // L3HD, L3HD]))
        load(l3_bqk[:, 0:D], a[w + "bq"].rearrange("(o n) -> o n", o=1).broadcast_to([P, D]))
        dca = a[w + "bkv_dca"].rearrange("(o x n) -> o x n", o=1, x=2)
        load(l3_bqk[MAIN:P, D:2 * D], dca[:, 0, :].broadcast_to([P - MAIN, D]))
        load(l3_bv[MAIN:P, :], dca[:, 1, :].broadcast_to([P - MAIN, D]))
        load(l3_b1[0:MAIN, :], a[w + "bk"].rearrange("(o n) -> o n", o=1).broadcast_to([MAIN, D]))
        load(l3_b2[0:MAIN, :], a[w + "bv"].rearrange("(o n) -> o n", o=1).broadcast_to([MAIN, D]))
        assert count == L3_LOADS - 1

    def l3_store(sp, n, s, prev):
        done(sp, xn_ready, n, 0)
        sp.dma_start(xs_rows[:, bass.ds(prev * TB, TB), :], XN[:]).then_inc(xs_stored.sem, 16)

    def l3_setup_pe(pe):
        pe.wait_ge(in_l3x, 16 * (L3_LOADS - 1))
        nc.tensor.transpose(B7[:, 0:6], vec_rows[0:6, :], ident[0:6, 0:6]).then_inc(vec_tr.sem, 1)

    def l3_setup_act(act):
        act.wait_ge(in_l3x, 16 * (L3_LOADS - 1))
        done(act, vec_tr, 0, 0)
        nc.scalar.activation(l3_vec, B7[:, 0:6], ACT.Copy).then_inc(vec_ready.sem, 1)
        nc.scalar.activation(l3_bo, l3_bo, ACT.Copy, scale=gates[:, 3:4]).then_inc(vec_ready.sem, 1)

    def l3_setup_dve(dve):
        dve.wait_ge(in_l3x, 16 * (L3_LOADS - 1))
        dve.wait_ge(pool_consts, 4)
        link = Chain(dve, l3_w, 0)
        half = L3H // 2
        for x, dst in ((0, l3_bqk[0:MAIN, D:2 * D]), (1, l3_bv[0:MAIN, :])):
            for src, h0 in ((l3_b1, 0), (l3_b2, half)):
                ins = nc.vector.tensor_copy(dst.rearrange("p (h d) -> p h d", d=L3HD)[:, h0:h0 + half, :],
                                            src[0:MAIN, :].rearrange("p (h x d) -> p h x d", x=2, d=L3HD)[:, :, x, :])
        ins = nc.vector.tensor_copy(l3_wm.rearrange("p (x h d) -> p h x d", x=2, d=L3HD), l3_cat.rearrange("p (h x d) -> p h x d", x=2, d=L3HD))
        link(ins)
        centred = (l3_wq.rearrange("p k n -> p (k n)"), l3_wm[:, 0:D], l3_wd[:, 0:D], l3_bqk)
        heads = [(t.rearrange("p (g d) -> p g d", d=L3HD), t.shape[1] // L3HD) for t in centred]
        at = 0
        for g, c in heads:
            ins = nc.vector.tensor_reduce(l3_mean[:, at:at + c], g, AX.X, ALU.add)
            at += c
        link(ins)
        link(nc.vector.tensor_scalar(l3_mean, l3_mean, 1.0 / L3HD, None, ALU.mult))
        at = 0
        for g, c in heads:
            ins = nc.vector.tensor_tensor(g, g, l3_mean[:, at:at + c].unsqueeze(2).broadcast_to([P, c, L3HD]), ALU.subtract)
            at += c
        link(ins)
        link.close()

    def l3_setup_pool(pool):
        done(pool, prep_tr, 0, L2M - 1)
        done(pool, F2.y_mm, NS - 1, F2.m - 1)
        nc.gpsimd.memset(l3_v, 0.0).then_inc(pool_consts, 1)
        nc.gpsimd.memset(l3_zero_row, 0.0).then_inc(pool_consts, 1)
        nc.gpsimd.memset(l3_cm.rearrange("p (b k) -> p b k", b=TB)[:, :, MAIN:P], 0.0)
        nc.gpsimd.memset(l3_cd.rearrange("p (b k) -> p b k", b=TB)[:, :, 0:MAIN], 0.0)

    L3_BANKS = (B4, B5, B6, B7)

    def l3_pe(pe, s):
        n, prev = tail_of(L3.stage, s)
        done(pe, l3_in, s, 0)
        for b in range(TB):
            bank = L3_BANKS[b]
            c = slice(b * P, (b + 1) * P)
            for k in range(KD):
                mm(bank[:, 0:D], l3_x[:, k, c], l3_wq[:, k, :], k == 0, k == KD - 1)
            mm(bank[:, D:2 * D], l3_cm[:, c], l3_wm[:, 0:D], True, False)
            mm(bank[:, D:2 * D], l3_cd[:, c], l3_wd[:, 0:D], False, True).then_inc(l3_qk_mm.sem, 1)
            if b == 0:
                done(pe, yt_ready, n, 1)
            v = Y[b // 2][:, b % 2 * D:(b % 2 + 1) * D]
            mm(v, l3_cm[:, c], l3_wm[:, D:2 * D], True, False)
            last = mm(v, l3_cd[:, c], l3_wd[:, D:2 * D], False, True)
            if b % 2:
                last.then_inc(l3_v_mm.sem, 1)
        for b in range(TB):
            done(pe, l3_n_ready, s, b)
            for j in range(4):
                last = nc.tensor.transpose(L3_BANKS[b][:, j * P:(j + 1) * P], l3_qk[:, b, j * P:(j + 1) * P], ident[:])
            last.then_inc(l3_tr.sem, 1)
        done(pe, l3_v_ready, s, 0)

    def l3_act(act, s):
        for b in range(TB):
            done(act, l3_add, s, b)
            nc.scalar.activation(l3_sq[b], l3_qk[:, b, :], ACT.Square).then_inc(l3_sq_ready.sem, 1)
        done(act, l3_var_ready, s, 0)
        nc.scalar.activation(l3_r, l3_var, ACT.Sqrt).then_inc(l3_sd_ready.sem, 1)
        for b in range(TB):
            done(act, l3_tr, s, b)
            bank = L3_BANKS[b].rearrange("p (x k c) -> p x k c", x=2, k=KD)
            for dst, x, lo, hi, j in ((l3_q, 0, 0, P, 0), (l3_k, 1, 0, MAIN, 2), (l3_k, 1, MAIN, P, 4)):
                last = nc.scalar.activation(dst[:, :, b * P + lo:b * P + hi], bank[:, x, :, lo:hi], ACT.Identity,
                                            scale=l3_vec[:, j:j + 1], bias=l3_vec[:, j + 1:j + 2])
        last.then_inc(L3.qk_ready.sem, 1)

    def l3_dve(dve, s):
        link = Chain(dve, l3_chain, s)
        done(dve, xs_stored, s, -1)
        for b in range(TB):
            done(dve, l3_qk_mm, s, b)
            nc.vector.tensor_tensor(l3_qk[:, b, :], L3_BANKS[b], l3_bqk, ALU.add).then_inc(l3_add.sem, 1)
        for j in range(2):
            done(dve, l3_v_mm, s, j)
            v = Y[j].rearrange("p (t h r c) -> p t h r c", t=2, h=KD, r=2)
            for r in range(2):
                c = slice(r * P // 2, (r + 1) * P // 2)
                bias = l3_bv.rearrange("p (h r c) -> p h r c", h=KD, r=2)[:, :, r, :].unsqueeze(1).broadcast_to([P, 2, KD, P // 2])
                last = nc.vector.tensor_tensor(l3_v[:, 2 * j:2 * j + 2, :, r, c], v[:, :, :, r, :], bias, ALU.add)
        last.then_inc(l3_v_ready.sem, 1)
        for b in range(TB):
            done(dve, l3_sq_ready, s, b)
            ins = nc.vector.tensor_reduce(l3_var[:, b, :], l3_sq[b].rearrange("p (g d) -> p g d", d=L3HD), AX.X, ALU.add)
        link(ins)
        nc.vector.tensor_scalar(l3_var, l3_var, 1.0 / L3HD, LN3_EPS, ALU.mult, ALU.add).then_inc(l3_var_ready.sem, 1)
        done(dve, l3_sd_ready, s, 0)
        link(nc.vector.reciprocal(l3_r, l3_r))
        for b in range(TB):
            g = l3_qk[:, b, :].rearrange("p (g d) -> p g d", d=L3HD)
            nc.vector.tensor_tensor(g, g, l3_r[:, b, :].unsqueeze(2).broadcast_to([P, 32, L3HD]), ALU.mult)\
                .then_inc(l3_n_ready.sem, 1)
        link.close()

    def l3_copies(pool, s):
        c = CTXT[:, tok(s % NS)].rearrange("p (b k) -> p b k", b=TB)
        nc.gpsimd.tensor_copy(l3_cm.rearrange("p (b k) -> p b k", b=TB)[:, :, 0:MAIN], c[:, :, 0:MAIN])
        nc.gpsimd.tensor_copy(l3_cd.rearrange("p (b k) -> p b k", b=TB)[:, :, MAIN:P], c[:, :, MAIN:P])
        nc.gpsimd.tensor_copy(l3_x, XNT[:, :, tok(s % NS)]).then_inc(l3_in.sem, 1)

    L3E, L3F, L3K = 64, 96, 8
    SLOTS = P * L3E
    AHEAD = 6
    XR = 8
    GE = 16
    NG = L3E // GE
    QE = 4
    at = TB * KD * 2 * P

    def room(n, dt=F32):
        nonlocal at
        at += n
        return tile(R2, at - n, n).bitcast(dt) if dt != F32 else tile(R2, at - n, n)

    f3_wr = room(KD * L3E).rearrange("p (k n) -> p k n", k=KD)
    R3 = Router("f3", 7, L3E, L3K, f3_wr, R2, at, (Y[0], Y[0]))
    at = R3.end
    R3.chain = signal("moe_r_chain", 6 + 6)
    f3_oh = room(TB * L3K * L3E).rearrange("p (t k e) -> p t k e", t=TB, k=L3K)
    f3_map = room(TB * L3E).rearrange("p (t e) -> p t e", t=TB)
    f3_m = room(TB * L3E // 2, BF16).rearrange("p (t e) -> p t e", t=TB)
    f3_carry = room(L3E // 2, BF16)
    f3_msum = room(L3E)
    f3_slot = room(TB * L3K).rearrange("p (t k) -> p t k", t=TB)
    f3_slot_u = room(TB * L3K, U32).rearrange("p (t k) -> p t k", t=TB)
    f3_pay = room(TB * L3K * 2).rearrange("p (t k x) -> p t k x", t=TB, x=2)
    f3_pay_i = f3_pay.bitcast(I32)
    f3_before = room(P // 2, BF16)
    f3_ones = room(P // 2, BF16)
    f3_wr_raw = room(D)[0:L3E, :]
    f3_ids = room(B, I32)
    f3_tab = room((L3E + AHEAD) * 2).rearrange("p (e x) -> p e x", x=2)
    f3_tab_i = f3_tab.bitcast(I32)
    f3_idx_g = room(GE, U32)
    f3_idx_s = room(GE, U32)
    f3_wt = room(GE)
    f3_zero = room(D)
    f3_gu = room(GE * KD * 2 * L3F).rearrange("p (e k n) -> p e k n", e=GE, k=KD)
    f3_dn = room(GE * D).rearrange("p (e n) -> p e n", e=GE)[0:L3F]
    assert at <= 19200
    f3_xe = tile(WK, 0, XR * D).rearrange("p (n d) -> p n d", n=XR)
    f3_xt = tile(WK, 2048, 512).rearrange("p (n k c) -> p n k c", n=2, k=KD)
    f3_sg = tile(WK, 2560, 256).rearrange("p (n c) -> p n c", n=2)
    f3_h = tile(WK, 2816, 256).rearrange("p (n c) -> p n c", n=2)
    f3_y = tile(WK, 3072, 512).rearrange("p (n d) -> p n d", n=2)
    f3_sum = [tile(R1, i * B * D, B * D).rearrange("p (b d) -> p b d", b=B) for i in range(2)]
    table = nc.dram_tensor("slots", (SLOTS, 2), F32, kind="Internal").ap()
    table_rows = table.rearrange("(p e) x -> p e x", e=L3E)
    acc = [nc.dram_tensor(f"moe_sum{i}", ((B + 1) * P, D), F32, kind="Internal").ap() for i in range(2)]
    in_f3r = semaphore("in_f3r")
    f3_wr_tr = signal("small_tr", 1, 1)
    f3_wr_ready = signal("small_ready", 1, 1)
    f3_made = semaphore("f3_made")
    f3_m_ready = signal("f3_m_ready", 1)
    f3_map_ready = signal("f3_map_ready", 1)
    f3_pos = Y[0][:, TB * L3E:2 * TB * L3E]
    ROUTE_END = L3.n + N_END - 1
    f3_pos_mm = signal("f3_pos_mm", 1)
    f3_slots_ready = signal("f3_slots_ready", 1)
    tab_written = Signal(semaphore("tab_written"), 16 * TB * L3K, NS, 16)
    tab_read = semaphore("tab_read")
    f3_idx_ready = signal("f3_idx_ready", 1, NG)
    f3_w_in = [Signal(semaphore(f"f3_w_in{i}"), 32, NG, 0) for i in range(GE // QE)]
    f3_gathered = [Signal(semaphore(f"f3_gathered{i}"), 16 * GE // XR, NG, 0) for i in range(XR)]
    f3_added = [Signal(semaphore(f"f3_added{i}"), 16 * GE // 2, NG, 16) for i in range(2)]
    f3_xt_tr = signal("f3_xt_tr", GE, NG)
    f3_xt_ready = signal("f3_xt_ready", GE, NG)
    f3_gu_mm = signal("moe_g_mm", GE, NG)
    f3_sg_ready = signal("moe_sg_ready", GE, NG)
    f3_h_ready = signal("moe_h_ready", GE, NG)
    f3_y_mm = signal("moe_y_mm", GE, NG)
    f3_y_ready = signal("f3_y_ready", GE, NG)
    sum_in = [semaphore(f"sum_in{i}") for i in range(NS)]
    x_done = semaphore("x_done")
    sum_chain = semaphore("sum_chain")

    def f3_weights(sp, g, q):
        es = bass.ds(g * GE + q * QE, QE)
        sp.dma_start(f3_gu[:, q * QE:(q + 1) * QE], a["L3_ffn_gate_up_proj"][es].rearrange("e (k p) n -> p e k n", p=P))\
            .then_inc(f3_w_in[q].sem, 16)
        sp.dma_start(f3_dn[:, q * QE:(q + 1) * QE], a["L3_ffn_down_proj"][es].rearrange("e f d -> f e d"))\
            .then_inc(f3_w_in[q].sem, 16)

    def f3_loads(sp):
        done(sp, F2.y_mm, NS - 1, F2.m - 1)
        sp.dma_start(f3_wr_raw, a["L3_ffn_router_weight"]).then_inc(in_f3r, 16)
        for q in range(GE // QE):
            f3_weights(sp, 0, q)

    def f3_sp(sp):
        l3_store(sp, NS * 7 + NS - 1, 0, NS - 1)
        sp.wait_ge(tab_written.sem, tab_written.end)
        sp.dma_start(f3_tab[:, 0:L3E, :], table_rows).then_inc(tab_read, 16)
        with sp.Fori(1, NG, 1) as g:
            for q in range(GE // QE):
                done(sp, f3_y_mm, g - 1, (q + 1) * QE - 1)
                f3_weights(sp, g, q)
        for i in range(2):
            sp.wait_ge(f3_added[i].sem, f3_added[i].end)
        for j in range(NS):
            b = slice(j * TB, (j + 1) * TB)
            for i in range(2):
                sp.dma_start(f3_sum[i][:, b], acc[i].rearrange("(b p) d -> p b d", p=P)[:, b]).then_inc(sum_in[j], 16)
        for j in range(NS):
            b = slice(j * TB, (j + 1) * TB)
            sp.wait_ge(x_done, j + 1)
            sp.dma_start(out.rearrange("b p d -> p b d")[:, b], X[:, b]).then_inc(out_done, 16)
        sp.wait_ge(out_done, 16 * NS)

    def f3_setup_pool(pool):
        made = 0

        def ordered(ins):
            nonlocal made
            made += 1
            ins.then_inc(f3_made, 1)
            pool.wait_ge(f3_made, made)

        nc.gpsimd.iota(f3_tab_i[:, :, 0], pattern=[[0, L3E + AHEAD]], base=B * P, channel_multiplier=1)
        nc.gpsimd.memset(f3_tab[:, :, 1], 0.0)
        ordered(nc.gpsimd.memset(f3_zero, 0.0))
        pool.dma_start(table_rows, f3_tab[:, 0:L3E, :]).then_inc(tab_written.sem, 16)
        for i in range(2):
            pool.dma_start(acc[i].rearrange("(b p) d -> p b d", p=P), f3_zero.unsqueeze(1).broadcast_to([P, B + 1, D]))\
                .then_inc(f3_added[i].sem, 16)
        nc.gpsimd.iota(f3_ids, pattern=[[P, B]], base=0, channel_multiplier=1)
        nc.gpsimd.memset(f3_carry, 0.0)
        nc.gpsimd.memset(f3_ones, 1.0)
        ordered(nc.gpsimd.memset(f3_before, 1.0))
        ordered(nc.gpsimd.affine_select(out=f3_before, in_=f3_before, compare_op=ALU.is_ge, fill=0.0, base=-1, pattern=[[1, P]],
                                        channel_multiplier=-1))
        pool.sem_inc(pool_consts, 1)

    def f3_route_pool(pool, s):
        done(pool, f3_slots_ready, s, 0)
        done(pool, tab_written, s, -1)
        for t in range(TB):
            for k in range(L3K):
                nc.gpsimd.indirect_dma_start(table, bass.IndirectOffsetOnAxis(ap=f3_slot_u[:, t, k:k + 1], axis=0),
                                             f3_pay[:, t, k, :], None, bounds_check=SLOTS - 1, oob_is_err=False)\
                    .then_inc(tab_written.sem, 16)

    def f3_setup_pe(pe):
        pe.wait_ge(in_f3r, 16)
        for k in range(KD):
            last = nc.tensor.transpose(B4[:, k * L3E:(k + 1) * L3E], f3_wr_raw[:, k * P:(k + 1) * P], ident[0:L3E, 0:L3E])
        last.then_inc(f3_wr_tr.sem, 1)
        done(pe, f3_wr_ready, 0, 0)
        pe.wait_ge(pool_consts, 6)

    def f3_setup_act(act):
        done(act, f3_wr_tr, 0, 0)
        nc.scalar.activation(f3_wr.rearrange("p k n -> p (k n)"), B4[:, 0:KD * L3E], ACT.Copy).then_inc(f3_wr_ready.sem, 1)

    def f3_places(pe, r):
        done(pe, f3_m_ready, r, 0)
        for t in range(TB):
            pos = f3_pos[:, t * L3E:(t + 1) * L3E]
            mm(pos, f3_ones, f3_carry, True, False)
            for u in range(t):
                mm(pos, f3_ones, f3_m[:, u, :], False, False)
            last = mm(pos, f3_before, f3_m[:, t, :], False, True)
        last.then_inc(f3_pos_mm.sem, 1)

    def f3_route_pe(pe, r, t):
        if t == 8:
            router_logits(pe, R3, r)
        if t == 9:
            router_turn(pe, R3, r)
        if t == 14:
            f3_places(pe, r)
        if t == ROUTE_END:
            done(pe, f3_map_ready, r, 0)

    def f3_route_act(act, r, t):
        if t == 8:
            router_out(act, R3, r)
        if t == 11:
            router_exp(act, R3, r)

    def f3_choices(dve, r, link):
        link(nc.vector.tensor_tensor(f3_oh.rearrange("p t k e -> p (t k) e"), iota[:].unsqueeze(1).broadcast_to([P, TB * L3K, L3E]),
                                     R3.ixf.rearrange("p t k -> p (t k)").unsqueeze(2).broadcast_to([P, TB * L3K, L3E]), ALU.is_equal))
        with nc.allow_low_precision(reason="whole numbers up to 8"):
            nc.vector.tensor_reduce(f3_m, f3_oh.rearrange("p t k e -> p t e k"), AX.X, ALU.add).then_inc(f3_m_ready.sem, 1)

    def f3_slots(dve, r, link):
        done(dve, tab_written, r, -1)
        nc.vector.tensor_copy(f3_pay_i[:, :, :, 0], f3_ids[:, bass.ds(r * TB, TB)].unsqueeze(2).broadcast_to([P, TB, L3K]))
        nc.vector.tensor_copy(f3_pay[:, :, :, 1], R3.top)
        done(dve, f3_pos_mm, r, 0)
        link(nc.vector.scalar_tensor_tensor(f3_map, f3_pos.rearrange("p (t e) -> p t e", t=TB), float(L3E),
                                            iota[:].unsqueeze(1).broadcast_to([P, TB, L3E]), ALU.mult, ALU.add))
        dve.sem_inc(f3_map_ready.sem, 1)
        link(nc.vector.tensor_reduce(f3_msum, f3_m.rearrange("p t e -> p e t"), AX.X, ALU.add))
        nc.vector.tensor_tensor(f3_carry, f3_carry, f3_msum, ALU.add)
        link(nc.vector.tensor_tensor(f3_oh, f3_oh, f3_map.unsqueeze(2).broadcast_to([P, TB, L3K, L3E]), ALU.mult))
        link(nc.vector.tensor_reduce(f3_slot, f3_oh, AX.X, ALU.add))
        link(nc.vector.tensor_copy(f3_slot_u, f3_slot))
        dve.sem_inc(f3_slots_ready.sem, 1)

    def f3_route_dve(dve, r, t, link):
        if t == 10:
            router_sub(dve, R3, r, link)
        if t == 12:
            router_top(dve, R3, r, link, False)
        if t == 13:
            f3_choices(dve, r, link)
        if t == 15:
            f3_slots(dve, r, link)
            link.close()

    def f3_pool_start(pool):
        pool.wait_ge(tab_read, 16)
        pool.wait_ge(xs_stored.sem, 16 * (1 + NS + 1))
        nc.gpsimd.tensor_copy(f3_idx_g[:, 0:AHEAD], f3_tab_i.bitcast(U32)[:, 0:AHEAD, 0]).then_inc(f3_made, 1)
        pool.wait_ge(f3_made, 4)
        for j in range(AHEAD):
            nc.gpsimd.indirect_dma_start(f3_xe[:, j % XR, :], None, xs, bass.IndirectOffsetOnAxis(ap=f3_idx_g[:, j:j + 1], axis=0))\
                .then_inc(f3_gathered[j % XR].sem, 16)

    def f3_pool(pool, g):
        done(pool, f3_gathered[(AHEAD - 1) % XR], g, 15)
        done(pool, f3_added[0], g, -1)
        done(pool, f3_added[1], g, -1)
        tab = f3_tab_i.bitcast(U32)
        nc.gpsimd.tensor_copy(f3_idx_g, tab[:, bass.ds(g * GE + AHEAD, GE), 0])
        nc.gpsimd.tensor_copy(f3_idx_s, tab[:, bass.ds(g * GE, GE), 0])
        nc.gpsimd.tensor_copy(f3_wt, f3_tab[:, bass.ds(g * GE, GE), 1]).then_inc(f3_idx_ready.sem, 1)
        done(pool, f3_idx_ready, g, 0)
        for j in range(GE):
            r = (j + AHEAD) % XR
            done(pool, f3_xt_tr, g, j + AHEAD - XR)
            nc.gpsimd.indirect_dma_start(f3_xe[:, r, :], None, xs, bass.IndirectOffsetOnAxis(ap=f3_idx_g[:, j:j + 1], axis=0))\
                .then_inc(f3_gathered[r].sem, 16)
            done(pool, f3_y_ready, g, j)
            done(pool, f3_added[j % 2], g, 16 * (j // 2) - 1)
            nc.gpsimd.indirect_dma_start(acc[j % 2], bass.IndirectOffsetOnAxis(ap=f3_idx_s[:, j:j + 1], axis=0), f3_y[:, j % 2, :], None,
                                         bounds_check=(B + 1) * P - 1, compute_op=ALU.add).then_inc(f3_added[j % 2].sem, 16)

    def f3_pe(pe, g):
        for j in range(GE + 3):
            if j < GE:
                done(pe, f3_gathered[j % XR], g, 16 * (j // XR) + 15)
                done(pe, f3_xt_ready, g, j - 2 if j >= 2 else -1)
                for k in range(KD):
                    last = nc.tensor.transpose(PS[:, j % 2, k * P:(k + 1) * P], f3_xe[:, j % XR, k * P:(k + 1) * P], ident[:])
                last.then_inc(f3_xt_tr.sem, 1)
            if j >= 3:
                e = j - 3
                done(pe, f3_h_ready, g, e)
                done(pe, f3_y_ready, g, e - 2 if e >= 2 else -1)
                mm(PS[:, 4 + e % 2, 0:D], f3_h[0:L3F, e % 2, :], f3_dn[:, e, :]).then_inc(f3_y_mm.sem, 1)
            if 1 <= j <= GE:
                e = j - 1
                done(pe, f3_xt_ready, g, e)
                if e % QE == 0:
                    done(pe, f3_w_in[e // QE], g, 31)
                done(pe, f3_h_ready, g, e - 2 if e >= 2 else -1)
                for x in range(2):
                    for k in range(KD):
                        last = mm(PS[0:L3F, 2 + e % 2, x * P:(x + 1) * P], f3_gu[:, e, k, x * L3F:(x + 1) * L3F], f3_xt[:, e % 2, k, :],
                                  k == 0, k == KD - 1)
                last.then_inc(f3_gu_mm.sem, 1)

    def f3_act(act, g):
        for j in range(GE + 1):
            if j < GE:
                done(act, f3_xt_tr, g, j)
                done(act, f3_gu_mm, g, j - 2 if j >= 2 else -1)
                nc.scalar.activation(f3_xt[:, j % 2, :, :].rearrange("p k c -> p (k c)"), PS[:, j % 2, 0:D], ACT.Copy)\
                    .then_inc(f3_xt_ready.sem, 1)
            if j >= 1:
                e = j - 1
                done(act, f3_gu_mm, g, e)
                done(act, f3_h_ready, g, e - 2 if e >= 2 else -1)
                nc.scalar.activation(f3_sg[0:L3F, e % 2, :], PS[0:L3F, 2 + e % 2, 0:P], ACT.Silu).then_inc(f3_sg_ready.sem, 1)

    def f3_dve(dve, g):
        done(dve, f3_idx_ready, g, 0)
        for j in range(GE + 2):
            if j < GE:
                done(dve, f3_sg_ready, g, j)
                done(dve, f3_y_mm, g, j - 2 if j >= 2 else -1)
                nc.vector.tensor_tensor(f3_h[0:L3F, j % 2, :], f3_sg[0:L3F, j % 2, :], PS[0:L3F, 2 + j % 2, P:2 * P], ALU.mult)\
                    .then_inc(f3_h_ready.sem, 1)
            if j >= 2:
                e = j - 2
                done(dve, f3_y_mm, g, e)
                done(dve, f3_added[e % 2], g, 16 * (e // 2) - 1)
                nc.vector.tensor_scalar(f3_y[:, e % 2, :], PS[:, 4 + e % 2, 0:D], f3_wt[:, e:e + 1], None, ALU.mult)\
                    .then_inc(f3_y_ready.sem, 1)

    def f3_end_dve(dve):
        for j in range(NS):
            b = slice(j * TB, (j + 1) * TB)
            dve.wait_ge(sum_in[j], 32)
            nc.vector.tensor_tensor(f3_sum[0][:, b], f3_sum[0][:, b], f3_sum[1][:, b], ALU.add).then_inc(sum_chain, 1)
            dve.wait_ge(sum_chain, j + 1)
            nc.vector.scalar_tensor_tensor(X[:, b], f3_sum[0][:, b], gates[:, 7:8], X[:, b], ALU.mult, ALU.add).then_inc(x_done, 1)

    block = ctx.enter_context(nc.Block())
    n_tails = NS - 1 + NS * 7 + 1

    @block.sync
    def _(sp):
        ctx.enter_context(nc.allow_non_contiguous_dma(reason="a few vectors that go one element to a partition"))
        sp.dma_start(X[:], a["x"].rearrange("b p d -> p b d")).then_inc(in_x, 16)
        sp.dma_start(CTX[:], a["ctx_1024"].rearrange("b p d -> p b d")).then_inc(in_ctx, 16)
        mask = a["mask_BxS2_bf1"].rearrange("b k -> (b k)").rearrange("(o n) -> o n", o=1)
        sp.dma_start(mask_row[0:1, :], mask).then_inc(in_small, 16)
        sp.dma_start(mask_all, mask.broadcast_to([P, B * P])).then_inc(in_small, 16)
        for j, g in enumerate(("g_xattn", "g_ffn")):
            sp.dma_start(gates[:, 4 * j:4 * j + 4], a[g].rearrange("(o n) -> o n", o=1).broadcast_to([P, 4])).then_inc(in_small, 16)
        sp.dma_start(l0_wv, a["L0_xattn_Wv"]).then_inc(in_l0x, 16)
        sp.dma_start(l0_wo, a["L0_xattn_Wo"].rearrange("(h p) n -> p h n", p=P)).then_inc(in_l0x, 16)
        sp.dma_start(l0_wk, a["L0_xattn_Wk"]).then_inc(in_l0x, 16)
        sp.dma_start(l0_wq, a["L0_xattn_Wq"].rearrange("(k p) n -> p k n", p=P)).then_inc(in_l0x, 16)
        sp.dma_start(l0_gu, a["L0_ffn_gate_up_proj"].rearrange("e (k p) n -> p e k n", p=P)).then_inc(in_l0f, 16)
        sp.dma_start(l0_dn, a["L0_ffn_down_proj"].rearrange("e (k p) n -> p e k n", p=P)).then_inc(in_l0f, 16)
        sp.dma_start(l1_wq, a["L1_xattn_Wq"].rearrange("(k p) n -> p k n", p=P)).then_inc(in_l1x, 16)
        sp.dma_start(l1_wkv, a["L1_xattn_Wkv"]).then_inc(in_l1x, 16)
        sp.dma_start(l1_wout, a["L1_xattn_Wout"].rearrange("(k p) n -> p k n", p=P)).then_inc(in_l1x, 16)
        sp.dma_start(l1_bias[:], a["L1_xattn_bout"].rearrange("(k p) -> p k", p=P)).then_inc(in_l1x, 16)
        done(sp, L0.y_mm, NS - 1, HEADS - 1)
        sp.dma_start(pos_t[0:2, :], a["fside_BxSx2_0"].rearrange("b t c -> c (b t)")).then_inc(in_l1x, 16)
        sp.dma_start(l1_wr, a["L1_ffn_Wr"].rearrange("(k p) n -> p k n", p=P)).then_inc(in_l1f, 16)
        done(sp, f0_y, NS - 1, E0 - 1)
        for w, name in ((l1_wg, "L1_ffn_Wg"), (l1_wu, "L1_ffn_Wu")):
            for k in range(KD):
                sp.dma_start(w[:, k, :].rearrange("p (e n) -> p e n", e=L1E),
                             a[name][:, k * P:(k + 1) * P, :].rearrange("e p n -> p e n")).then_inc(in_l1f, 16)
        done(sp, L1.y_mm, NS - 1, KD - 1)
        sp.dma_start(wr_raw[:], a["L2_ffn_Wg"]).then_inc(in_l2x, 16)
        sp.dma_start(l1_wd, a["L1_ffn_Wd"].rearrange("e f d -> (e f) d").rearrange("(m p) n -> p m n", p=P)).then_inc(in_l1f, 16)
        sp.dma_start(l2_wv, a["L2_xattn_Wv"]).then_inc(in_l2x, 16)
        sp.dma_start(l2_wo, a["L2_xattn_Wo"].rearrange("(h p) n -> p h n", p=P)).then_inc(in_l2x, 16)
        sp.dma_start(l2_wk, a["L2_xattn_Wk"]).then_inc(in_l2x, 16)
        sp.dma_start(l2_wq, a["L2_xattn_Wq"].rearrange("(k p) n -> p k n", p=P)).then_inc(in_l2x, 16)
        sp.dma_start(gqk[:], a["L2_xattn_gq"].rearrange("(p o) -> p o", o=1)).then_inc(in_l2x, 16)
        sp.dma_start(gk[:], a["L2_xattn_gk"].rearrange("(p o) -> p o", o=1)).then_inc(in_l2x, 16)
        prep_sp(sp)
        l3_loads(sp)
        sp.wait_ge(pool_consts, 5)
        sp.dma_start(xs[B * P:, :], l3_zero_row).then_inc(xs_stored.sem, 16)
        f3_loads(sp)
        with sp.Fori(0, NS, 1) as s:
            n, prev = tail_of(L3.stage, s)
            l3_store(sp, n, s, prev)
        f3_sp(sp)

    @block.gpsimd
    def _(pool):
        for sig in signals.values():
            pool.sem_inc(sig.sem, CREDIT)
        pool.sem_inc(go, 1)
        nc.gpsimd.memset(neg_half[:], -0.5)
        nc.gpsimd.memset(ident[:], 0.0).then_inc(ident_made, 1)
        pool.wait_ge(ident_made, 1)
        nc.gpsimd.affine_select(out=ident[:], in_=ident[:], compare_op=ALU.not_equal, fill=1.0, base=0, pattern=[[-1, P]],
                                channel_multiplier=1).then_inc(ident_made, 1)
        pool.wait_ge(ident_made, 2)
        nc.gpsimd.tensor_copy(ident_b[:], ident[:]).then_inc(ident_made, 1)
        made = 3

        def ordered(ins):
            nonlocal made
            made += 1
            ins.then_inc(ident_made, 1)
            pool.wait_ge(ident_made, made)

        fv = freq[:].rearrange("c (h p x t) -> c h p x t", h=L1H // KD, p=2, x=2)
        ordered(nc.gpsimd.memset(freq[:], 0.0))
        for x, f in enumerate((1.0, 10000.0 ** -0.5)):
            ordered(nc.gpsimd.affine_select(out=fv[:, :, :, x, :], in_=fv[:, :, :, x, :], compare_op=ALU.not_equal, fill=f, base=0,
                                            pattern=[[0, L1H // KD], [-1, 2], [0, 2]], channel_multiplier=1))
        for sel, hd in ((head_sel8, 8), (head_sel16, 16)):
            groups = P // (NB * hd)
            ordered(nc.gpsimd.memset(sel[:], 1.0))
            for sign, base in ((1, 0), (-1, hd - 1)):
                ordered(nc.gpsimd.affine_select(out=sel[:], in_=sel[:], compare_op=ALU.is_ge, fill=0.0, base=base,
                                                pattern=[[-sign * NB * hd, groups], [-sign * hd, NB]], channel_multiplier=sign))
        ordered(nc.gpsimd.iota(iota_i[:], pattern=[[1, 64]], base=0, channel_multiplier=0))
        ordered(nc.gpsimd.tensor_copy(iota[:], iota_i[:]))
        ordered(nc.gpsimd.memset(ones_col[:], 1.0))
        make_sel(ordered, F1, F1.sel, tile(R2, 8448, 704))
        pool.sem_inc(pool_consts, 1)
        with pool.Fori(0, NS - 1, 1) as n:
            tail_pool(pool, n)
        wide_run(wide_pool, L0, pool)
        with pool.Fori(0, NS, 1) as s:
            ffn0_pool(pool, 1, s)
        pool.wait_ge(hmask_ready, 2)
        done(pool, L0.y_mm, NS - 1, HEADS - 1)
        nc.gpsimd.memset(l1_v, 0.0).then_inc(pool_consts, 1)
        with pool.Fori(0, NS, 1) as s:
            rope_pool(pool, s)
            narrow_pool(pool, L1, s, l1_k, hmask8)
        done(pool, rope_ready, NS - 1, 3)
        make_sel(ordered, F2, l2_sel_made.bitcast(BF16), tile(R2, 9000, 1408))
        pool.sem_inc(pool_consts, 1)
        with pool.Fori(0, NS, 1) as s:
            dense_pool(pool, F1, s)
        first_keys_pool(pool, L2)
        wide_run(wide_pool, L2, pool)
        with pool.Fori(0, NS, 1) as s:
            dense_pool(pool, F2, s)
        l3_setup_pool(pool)
        done(pool, xnt_ready, NS * L3.stage, 1)
        l3_copies(pool, 0)

        def l3_pool(s):
            def copies(t):
                if t == 8:
                    done(pool, l3_v_mm, s, 1)
                    done(pool, xnt_ready, s + (NS * L3.stage + 1), 1)
                    l3_copies(pool, s + 1)

            narrow_pool(pool, L3, s, l3_k, hmask16, copies)

        l3_pool(0)
        f3_setup_pool(pool)
        with pool.Fori(1, NS, 1) as s:
            l3_pool(s)
            f3_route_pool(pool, s - 1)
        tail_pool(pool, n_tails - 1)
        f3_route_pool(pool, NS - 1)
        f3_pool_start(pool)
        with pool.Fori(0, NG, 1) as g:
            f3_pool(pool, g)

    @block.tensor
    def _(pe):
        pe.wait_ge(go, 1)
        pe.wait_ge(ident_made, 3)
        pe.wait_ge(in_ctx, 16)
        for g in range(NS):
            for t in range(TB):
                last = nc.tensor.transpose(PS[:, 4 + g, t * P:(t + 1) * P], CTX[:, g * TB + t, :], ident[:])
            last.then_inc(ctx_tr.sem, 1)
        with pe.Fori(0, NS - 1, 1) as n:
            tail_pe(pe, n)
        pe.wait_ge(in_l0x, 64)
        done(pe, ctxt_ready, 0, NS - 1)
        pe.wait_ge(const_made, 2)
        wide_prep_pe(pe, L0)
        done(pe, L0.wvo_ready, 0, HEADS // 2 - 1)
        pe.wait_ge(mask_ready, 2)
        wide_run(wide_pe, L0, pe)
        pe.wait_ge(in_l0f, 32)
        with pe.Fori(0, NS, 1) as s:
            ffn0_pe(pe, 1, s)
        pe.wait_ge(pool_consts, 1)
        pe.wait_ge(in_l1x, 16 * 5)
        pe.wait_ge(l1w_ready, 1)
        with pe.Fori(0, NS, 1) as s:
            rope_pe(pe, s)
            narrow_pe(pe, L1, s, l1_q, l1_v, l1_ot)
        pe.wait_ge(in_l1f, 16 * 6)
        with pe.Fori(0, NS, 1) as s:
            dense_pe(pe, F1, s)
        pe.wait_ge(in_l2x, 16 * 7)
        first_keys_pe(pe, L2)
        wide_prep_pe(pe, L2)
        done(pe, L2.wvo_ready, 0, HEADS // 2 - 1)
        wide_run(wide_pe, L2, pe)
        prep_pe(pe)
        done(pe, prep_act, 0, L2M - 1)
        done(pe, prep_dve, 0, L2M - 1)
        with pe.Fori(0, NS, 1) as s:
            dense_pe(pe, F2, s)
        l3_setup_pe(pe)
        done(pe, vec_ready, 0, 1)
        done(pe, l3_w, 0, 3)
        l3_pe(pe, 0)
        narrow_pe(pe, L3, 0, l3_q, l3_v, l3_ot)
        f3_setup_pe(pe)
        with pe.Fori(1, NS, 1) as s:
            l3_pe(pe, s)
            narrow_pe(pe, L3, s, l3_q, l3_v, l3_ot, lambda t: f3_route_pe(pe, s - 1, t))
        tail_pe(pe, n_tails - 1)
        for t in range(ROUTE_END):
            f3_route_pe(pe, NS - 1, t)
        with pe.Fori(0, NG, 1) as g:
            f3_pe(pe, g)

    @block.scalar
    def _(act):
        act.wait_ge(go, 1)
        act.wait_ge(in_small, 64)
        nc.scalar.activation(gates[:], gates[:], ACT.Tanh).then_inc(gates_ready, 1)
        for g in range(NS):
            done(act, ctx_tr, 0, g)
            nc.scalar.activation(CTXT[:, g * W:(g + 1) * W], PS[:, 4 + g, :], ACT.Copy).then_inc(ctxt_ready.sem, 1)
        with act.Fori(0, NS - 1, 1) as n:
            for k in range(KD):
                tail_act(act, n, n, k)
        act.wait_ge(mask_ready, 2)
        wide_prep_act(act, L0)
        act.wait_ge(gates_ready, 1)
        wide_run(wide_act, L0, act)
        with act.Fori(0, NS, 1) as s:
            ffn0_act(act, 1, s)
        act.wait_ge(in_l1x, 16 * 5)
        for w, ws in ((l1_wq.rearrange("p k (n t) -> p (k n) t", t=2), l1_wqs.rearrange("p k (n t) -> p (k n) t", t=2)),
                      (l1_wkv[:, 0:D].rearrange("p (n t) -> p n t", t=2), l1_wks.rearrange("p (n t) -> p n t", t=2))):
            nc.scalar.activation(ws[:, :, 0], w[:, :, 1], ACT.Copy, scale=-1.0)
            ins = nc.scalar.activation(ws[:, :, 1], w[:, :, 0], ACT.Copy)
        nc.scalar.activation(l1_bias[:], l1_bias[:], ACT.Copy, scale=gates[:, 1:2]).then_inc(l1w_ready, 1)
        act.wait_ge(l1w_ready, 1)
        act.wait_ge(pool_consts, 2)
        with act.Fori(0, NS, 1) as s:
            rope_act(act, s)
            narrow_act(act, L1, s, float(L1HD) ** -0.5)
        with act.Fori(0, NS, 1) as s:
            dense_act(act, F1, s)
        act.wait_ge(gqk_ready, 1)
        first_keys_act(act, L2)
        wide_prep_act(act, L2)
        wide_run(wide_act, L2, act)
        prep_act_engine(act)
        with act.Fori(0, NS, 1) as s:
            dense_act(act, F2, s)
        l3_setup_act(act)
        done(act, vec_ready, 0, 1)
        l3_act(act, 0)
        narrow_act(act, L3, 0, float(L3HD) ** -0.5)
        f3_setup_act(act)
        with act.Fori(1, NS, 1) as s:
            l3_act(act, s)
            narrow_act(act, L3, s, float(L3HD) ** -0.5, lambda t: f3_route_act(act, s - 1, t))
        for k in range(KD):
            tail_act(act, n_tails - 1, NS - 1, k)
        for t in range(ROUTE_END):
            f3_route_act(act, NS - 1, t)
        with act.Fori(0, NG, 1) as g:
            f3_act(act, g)

    @block.vector
    def _(dve):
        dve.wait_ge(go, 1)
        nc.vector.memset(YT[:], 0.0).then_inc(const_made, 1)
        dve.wait_ge(const_made, 1)
        dve.sem_inc(yt_ready.sem, NS * KD)
        nc.vector.memset(ones_b[:], 1.0).then_inc(const_made, 1)
        dve.wait_ge(in_small, 64)
        nc.vector.tensor_scalar(mask_bias[0:1, :], mask_row[0:1, :], 1.0, NEG_BIG, ALU.subtract, ALU.mult).then_inc(mask_ready, 1)
        nc.vector.tensor_reduce(any_key[:], mask_all.rearrange("p (b k) -> p b k", b=B), AX.X, ALU.max).then_inc(mask_ready, 1)
        dve.wait_ge(pool_consts, 1)
        for sel, mask in ((head_sel8, hmask8), (head_sel16, hmask16)):
            nc.vector.tensor_reduce(mask[:], sel[:].rearrange("p r j -> p j r"), AX.X, ALU.add).then_inc(hmask_ready, 1)
        dve.wait_ge(in_x, 16)
        with dve.Fori(0, NS - 1, 1) as n:
            tail_dve(dve, n, n)
        dve.wait_ge(mask_ready, 2)
        wide_run(wide_dve, L0, dve)
        with dve.Fori(0, NS, 1) as s:
            ffn0_dve(dve, 1, s)
        with dve.Fori(0, NS, 1) as s:
            rope_dve(dve, s)
            narrow_dve(dve, L1, s, l1_ot, hmask8, float(L1HD) ** -0.5)
        with dve.Fori(0, NS, 1) as s:
            dense_dve(dve, F1, s, False)
        dve.wait_ge(in_l2x, 16 * 7)
        nc.vector.scalar_tensor_tensor(gqk[:], gqk[:], SCALE_WIDE, gk[:], ALU.mult, ALU.mult).then_inc(gqk_ready, 1)
        first_keys_dve(dve, L2)
        wide_run(wide_dve, L2, dve)
        prep_dve_engine(dve)
        with dve.Fori(0, NS, 1) as s:
            dense_dve(dve, F2, s, True)
        l3_setup_dve(dve)
        l3_dve(dve, 0)
        narrow_dve(dve, L3, 0, l3_ot, hmask16, float(L3HD) ** -0.5)
        dve.wait_ge(pool_consts, 6)
        with dve.Fori(1, NS, 1) as s:
            l3_dve(dve, s)
            link = Chain(dve, R3.chain, s - 1)
            narrow_dve(dve, L3, s, l3_ot, hmask16, float(L3HD) ** -0.5, lambda t: f3_route_dve(dve, s - 1, t, link))
        tail_dve(dve, n_tails - 1, NS - 1, NS)
        link = Chain(dve, R3.chain, NS - 1)
        for t in range(ROUTE_END):
            f3_route_dve(dve, NS - 1, t, link)
        with dve.Fori(0, NG, 1) as g:
            f3_dve(dve, g)
        f3_end_dve(dve)


def kernel(**inputs):
    import numpy as _np
    import concourse.bacc as _bacc
    from concourse import mybir as _mybir
    from concourse.bass_utils import run_bass_kernel_spmd as _run

    nc = _bacc.Bacc("TRN2", target_bir_lowering=False, num_devices=1)
    arrays, args = {}, {}
    for name, x in inputs.items():
        x = _np.ascontiguousarray(x)
        if x.dtype == _np.bool_:
            x = x.view(_np.uint8)
        arrays["in_" + name] = x
        args[name] = nc.dram_tensor("in_" + name, x.shape, _mybir.dt.from_np(x.dtype), kind="ExternalInput").ap()
    out = nc.dram_tensor("out_0", (16, 128, 256), _mybir.dt.float32, kind="ExternalOutput").ap()
    build(nc, args, out)
    r = _run(nc, [arrays], core_ids=[0])
    return r.results[0]["out_0"]
```

```python
from contextlib import ExitStack

import concourse.bass as bass
from concourse import mybir

F32 = mybir.dt.float32
BF16 = mybir.dt.bfloat16
I32 = mybir.dt.int32
U32 = mybir.dt.uint32
U8 = mybir.dt.uint8
ACT = mybir.ActivationFunctionType
ALU = mybir.AluOpType
AX = mybir.AxisListType

P = 128
B = 16
D = 256
KD = D // P
TB = 4
W = TB * P
NS = B // TB
HEADS = 16
LN_EPS = 1e-5
RMS_EPS = 1e-5
LN3_EPS = 1e-6
TINY = 1e-30
NEG_BIG = 1e30
CREDIT = 4


class Signal:

    def __init__(self, sem, per, bodies, base):
        self.sem, self.per, self.base = sem, per, base
        self.end = base + per * bodies

    def value(self, body, item):
        return body * self.per + (self.base + item + 1)


def build(nc, a, out):
    ctx = ExitStack()
    with ctx:
        _build(nc, ctx, a, out)


def _build(nc, ctx, a, out):
    def sb(name, shape, dt=F32):
        return ctx.enter_context(nc.sbuf_tensor(name, shape, dt))

    signals = {}

    def semaphore(name):
        return ctx.enter_context(nc.semaphore(name))

    def dma_signal(name, first):
        return Signal(semaphore(name), 16, NS, 16 * first)

    def signal(name, per, bodies=NS):
        last = signals.get(name)
        if last is None:
            signals[name] = Signal(semaphore(name), per, bodies, CREDIT)
        else:
            signals[name] = Signal(last.sem, per, bodies, last.end)
        return signals[name]

    go = semaphore("go")
    waits_met = semaphore("waits_met")

    def hold(eng, sem, value):
        eng.wait_ge(sem, value)
        if not isinstance(value, int):
            eng.sem_inc(waits_met, 1)

    def done(eng, sig, body, item):
        hold(eng, sig.sem, sig.value(body, item))

    class Chain:

        def __init__(self, eng, sig, body, first=0):
            self.eng, self.sig, self.body, self.n = eng, sig, body, first

        def __call__(self, ins):
            ins.then_inc(self.sig.sem, 1)
            done(self.eng, self.sig, self.body, self.n)
            self.n += 1

        def close(self):
            assert self.n == self.sig.per, (self.sig.sem, self.n, self.sig.per)

    X = sb("x_res", [P, B, D])
    XNT = sb("xn_T", [P, KD, B * P])
    CTX = sb("ctx", [P, B, P])
    CTXT = sb("ctx_T", [P, B * P])
    YT = sb("y_T", [P, KD, W])
    XN = sb("xn", [P, TB, D])
    R1 = sb("weights_1", [P, 12288])
    R2 = sb("weights_2", [P, 19200])
    WK = sb("work", [P, 6144])
    ident = sb("ident", [P, P])
    ident_b = sb("ident_b", [P, P], BF16)
    ones_b = sb("ones_b", [1, P], BF16)
    gates = sb("gates", [P, 8])
    neg_half = sb("neg_half", [P, 512 // 8])
    bn = sb("bn", [P, TB, 6])
    mv = sb("mv", [P, TB, 2])
    var = sb("var", [P, TB])
    rstd = sb("rstd", [P, TB])
    any_key = sb("any_key", [P, B])
    mx = sb("mx", [P, 2, TB])
    negm = sb("negm", [P, 2, TB])
    sums = sb("sums", [P, 2, TB])
    rinv = sb("rinv", [P, 2, TB])

    PS = ctx.enter_context(nc.psum_tensor("ps", [P, 8, 512], F32))
    Y = [PS[:, 0, :], PS[:, 1, :]]
    TP = PS[:, 2, :]
    B3 = PS[:, 3, :]
    B4, B5, B6, B7 = (PS[:, i, :] for i in range(4, 8))

    def mm(out, lhsT, rhs, start=True, stop=True):
        return nc.tensor.matmul(out, lhsT, rhs, start=start, stop=stop, skip_group_check=True)

    def tok(s):
        return bass.ds(s * W, W)

    def tile(x, o, n):
        return x[:, o:o + n]

    l0_wq = tile(R1, 0, 4096).rearrange("p (k n) -> p k n", k=KD)
    l0_wk = tile(R1, 4096, 1024)
    l0_wv = tile(R1, 5120, 1024)
    l0_wo = tile(R1, 6144, 4096).rearrange("p (h n) -> p h n", h=HEADS)
    l0_gu = tile(R2, 0, 4096).rearrange("p (e k n) -> p e k n", e=4, k=KD)
    l0_dn = tile(R2, 4096, 2048).rearrange("p (e k n) -> p e k n", e=4, k=KD)

    q_sb = tile(WK, 0, 1024).rearrange("p (n c) -> p n c", n=2)
    p_sb = tile(WK, 1024, 2048).rearrange("p (n c) -> p n c", n=4)
    pt_sb = tile(WK, 3072, 512)
    o_sb = tile(WK, 3584, 1024).rearrange("p (n c) -> p n c", n=2)
    ctx_s = tile(WK, 4608, 512).rearrange("p (t c) -> p t c", t=TB)
    k0_sb = tile(WK, 5120, 1024).rearrange("p (n c) -> p n c", n=2)
    wv_t = tile(WK, 0, 2048)
    mask_all = tile(WK, 0, 512).bitcast(U8)
    mask_bias = tile(R2, 17000, 1024).bitcast(BF16)
    mask_row = tile(R2, 18024, 512).bitcast(U8)
    ctxt_s = tile(WK, 5120, 512)
    qsq_sb = tile(WK, 5632, 512)
    kr_sb = tile(R2, 0, 2 * HEADS * W).rearrange("p (n h c) -> p n h c", n=2, h=HEADS)
    kn_sb = tile(R2, 2 * HEADS * W, 512)
    ksq_sb = tile(R2, 2 * HEADS * W + 512, 512)
    ones_col = sb("ones_col", [P, 1])
    gqk = sb("gqk", [P, 1])
    gk = sb("gk", [P, 1])
    ksq = sb("ksq", [P, 2, 4])
    kvar = sb("kvar", [P, 2, 4])
    rk = sb("rk", [P, 2, 4])
    qvar = sb("qvar", [P, 2, 4])
    rq = sb("rq", [P, 2, 4])

    in_x = semaphore("in_x")
    in_ctx = semaphore("in_ctx")
    in_small = semaphore("in_small")
    in_l0x = semaphore("in_l0x")
    in_l0f = semaphore("in_l0f")
    out_done = semaphore("out_done")
    ident_made = semaphore("ident_made")
    const_made = semaphore("const_made")
    gates_ready = semaphore("gates_ready")
    mask_ready = semaphore("mask_ready")
    ctx_tr = signal("ctx_tr", NS, 1)
    ctxt_ready = signal("ctxt_ready", NS, 1)
    yt_ready = signal("yt_ready", KD)
    yt_tr = signal("yt_tr", 2)
    y_added = signal("y_added", 2)
    var_ready = signal("var_ready", 1)
    rstd_ready = signal("rstd_ready", 1)
    xn_ready = signal("xn_ready", 1)
    xn_tr = signal("xn_tr", KD)
    xnt_ready = signal("xnt_ready", KD)
    tail_chain = signal("tail_chain", 2)
    xs_stored = dma_signal("xs_stored", 1)

    def tail_pe_y(pe, n, j):
        if j == 0:
            done(pe, yt_ready, n, 1)
            done(pe, xnt_ready, n, -1)
        else:
            done(pe, y_added, n, 0)
        for t in range(2):
            for h in range(KD):
                last = nc.tensor.transpose(TP[:, t * D + h * P:t * D + (h + 1) * P],
                                           YT[:, h, (2 * j + t) * P:(2 * j + t + 1) * P], ident[:])
        last.then_inc(yt_tr.sem, 1)

    def tail_pe_xn(pe, n, k):
        if k == 0:
            done(pe, xn_ready, n, 0)
        else:
            done(pe, xnt_ready, n, 0)
        for t in range(TB):
            last = nc.tensor.transpose(TP[:, t * P:(t + 1) * P], XN[:, t, k * P:(k + 1) * P], ident[:])
        last.then_inc(xn_tr.sem, 1)

    def tail_dve_add(dve, n, s, j):
        done(dve, yt_tr, n, j)
        x2 = X[:, bass.ds(s * TB + 2 * j, 2), :]
        nc.vector.tensor_tensor(x2, TP.rearrange("p (t d) -> p t d", t=2), x2, ALU.add).then_inc(y_added.sem, 1)

    def tail_dve_stats(dve, n, s):
        link = Chain(dve, tail_chain, n)
        done(dve, y_added, n, 1)
        for t in range(TB):
            ins = nc.vector.bn_stats(bn[:, t, :], X[:, bass.ds(s * TB + t, 1), :].rearrange("p t d -> p (t d)"))
        link(ins)
        for t in range(TB):
            ins = nc.vector.bn_aggr(mv[:, t, :], bn[:, t, :])
        link(ins)
        nc.vector.tensor_scalar(var[:], mv[:, :, 1], LN_EPS, None, ALU.add).then_inc(var_ready.sem, 1)
        link.close()

    def tail_dve_norm(dve, n, s, store=None):
        done(dve, rstd_ready, n, 0)
        if store is not None:
            done(dve, xs_stored, store, -1)
        for t in range(TB):
            ins = nc.vector.tensor_scalar(XN[:, t, :], X[:, bass.ds(s * TB + t, 1), :].rearrange("p t d -> p (t d)"),
                                          mv[:, t, 0:1], rstd[:, t:t + 1], ALU.subtract, ALU.mult)
        ins.then_inc(xn_ready.sem, 1)

    def tail_pool(pool, n):
        done(pool, var_ready, n, 0)
        nc.gpsimd.tensor_tensor(out=rstd[:], in0=var[:], in1=neg_half[:, 0:TB], op=ALU.pow).then_inc(rstd_ready.sem, 1)

    def tail_act(act, n, s, k):
        done(act, xn_tr, n, k)
        nc.scalar.activation(XNT[:, k, tok(s)], TP, ACT.Copy).then_inc(xnt_ready.sem, 1)

    def tail_pe(pe, n):
        for j in range(2):
            tail_pe_y(pe, n, j)
        for k in range(KD):
            tail_pe_xn(pe, n, k)

    def tail_dve(dve, n, s, store=None):
        for j in range(2):
            tail_dve_add(dve, n, s, j)
        tail_dve_stats(dve, n, s)
        tail_dve_norm(dve, n, s, store)

    def tail_of(i, s):
        return s + (NS - 1 + NS * i), (s + NS - 1) % NS

    T_LAG = 4
    Y_LAG = 5

    class Wide:

        def __init__(self, name, stage, kv_heads, wq, wk, wv, wo, rms):
            self.name, self.stage, self.kv_heads, self.rms = name, stage, kv_heads, rms
            self.wq, self.wk, self.wv, self.wo = wq, wk, wv, wo
            self.share = HEADS // kv_heads
            self.n, self.late = HEADS, Y_LAG
            self.wv_tr = signal("wide_wv_tr", kv_heads // 4, 1)
            self.wvt_ready = signal("wide_wvt_ready", kv_heads // 4, 1)
            self.wvo_mm = signal("wide_wvo_mm", HEADS // 2, 1)
            self.wvo_ready = signal("wide_wvo_ready", HEADS // 2, 1)
            self.ctx_ready = signal("wide_ctx_ready", 1)
            self.k_mm = signal("wide_k_mm", kv_heads)
            self.k_ready = signal("wide_k_ready", kv_heads)
            self.q_mm = signal("wide_q_mm", HEADS)
            self.q_ready = signal("wide_q_ready", HEADS)
            self.s_mm = signal("wide_s_mm", HEADS)
            self.negm_ready = signal("wide_negm_ready", HEADS)
            self.p_ready = signal("wide_p_ready", HEADS)
            self.rinv_ready = signal("wide_rinv_ready", HEADS)
            self.pn_ready = signal("wide_pn_ready", HEADS)
            self.pt_tr = signal("wide_pt_tr", HEADS)
            self.pt_ready = signal("wide_pt_ready", HEADS)
            self.o_mm = signal("wide_o_mm", HEADS)
            self.o_ready = signal("wide_o_ready", HEADS)
            self.y_mm = signal("wide_y_mm", HEADS)
            self.chain = signal("wide_chain", HEADS * (1 if rms else 3))
            if rms:
                self.qsq_mm = signal("wide_qsq_mm", HEADS)
                self.qvar_ready = signal("wide_qvar_ready", HEADS)
                self.rq_ready = signal("wide_rq_ready", HEADS)
                self.kctx_ready = signal("wide_kctx_ready", 1)
                self.k_chain = signal("wide_k_chain", HEADS)
                self.kt_mm = signal("wide_kt_mm", HEADS)
                self.ksq_ready = signal("wide_ksq_ready", HEADS)
                self.kvar_ready = signal("wide_kvar_ready", HEADS)
                self.rk_ready = signal("wide_rk_ready", HEADS)
                self.kn_ready = signal("wide_kn_ready", HEADS)
                self.kn_tr = signal("wide_kn_tr", HEADS)

    SCALE_WIDE = float(P) ** -0.5

    def wide_prep_pe(pe, A):
        if A.rms:
            pe.wait_ge(A.k_ready.sem, A.k_ready.value(0, HEADS - 1))
        for g in range(A.kv_heads // 4):
            if g >= 2:
                pe.wait_ge(A.wvt_ready.sem, A.wvt_ready.value(0, g - 2))
            for j in range(4):
                last = nc.tensor.transpose((B4, B5)[g % 2][:, j * P:(j + 1) * P], A.wv[:, (4 * g + j) * P:(4 * g + j + 1) * P],
                                           ident[:])
            last.then_inc(A.wv_tr.sem, 1)
        for c in range(HEADS // 2):
            pe.wait_ge(A.wvt_ready.sem, A.wvt_ready.value(0, min((2 * c + 1) // A.share // 4, A.kv_heads // 4 - 1)))
            if c >= 2:
                pe.wait_ge(A.wvo_ready.sem, A.wvo_ready.value(0, c - 2))
            for j in range(2):
                h = 2 * c + j
                g = h // A.share
                last = mm((B6, B7)[c % 2][:, j * D:(j + 1) * D], wv_t[:, g * P:(g + 1) * P], A.wo[:, h, :])
            last.then_inc(A.wvo_mm.sem, 1)

    def wide_prep_act(act, A):
        for g in range(A.kv_heads // 4):
            act.wait_ge(A.wv_tr.sem, A.wv_tr.value(0, g))
            nc.scalar.activation(wv_t[:, g * W:(g + 1) * W], (B4, B5)[g % 2], ACT.Copy).then_inc(A.wvt_ready.sem, 1)
        for c in range(HEADS // 2):
            act.wait_ge(A.wvo_mm.sem, A.wvo_mm.value(0, c))
            nc.scalar.activation(A.wo[:, 2 * c:2 * c + 2, :].rearrange("p h n -> p (h n)"), (B6, B7)[c % 2],
                                 ACT.Copy).then_inc(A.wvo_ready.sem, 1)

    def key_mm(pe, A, u, bank):
        hq, b = u // 4, u % 4
        mm(bank, ctxt_s[:, b * P:(b + 1) * P], A.wk[:, hq * W:(hq + 1) * W]).then_inc(A.kt_mm.sem, 1)

    def key_tr(pe, A, body, u, bank, banks=1):
        done(pe, A.kn_ready, body, u)
        done(pe, A.k_ready, body, u - banks)
        for j in range(4):
            last = nc.tensor.transpose(bank[:, j * P:(j + 1) * P], kn_sb[:, j * P:(j + 1) * P], ident[:])
        last.then_inc(A.kn_tr.sem, 1)

    def key_square(act, A, body, u, bank):
        done(act, A.kt_mm, body, u)
        done(act, A.kvar_ready, body, u - 1)
        nc.scalar.activation(ksq_sb, bank, ACT.Square).then_inc(A.ksq_ready.sem, 1)

    def key_out(act, A, body, u, bank):
        hq, b = u % HEADS // 4, u % 4
        done(act, A.kn_tr, body, u)
        half = (body if u >= 0 else body - 1) % 2
        dst = kr_sb[:, bass.ds(half, 1), 4 * hq:4 * hq + 4, b * P:(b + 1) * P].rearrange("p n h c -> p (n h) c")
        nc.scalar.activation(dst, bank.rearrange("p (j c) -> p j c", j=4), ACT.Copy, scale=gqk[:, 0:1]).then_inc(A.k_ready.sem, 1)

    def key_var(dve, A, body, u, link):
        done(dve, A.ksq_ready, body, u)
        link(nc.vector.tensor_reduce(ksq[:, u % 2, :], ksq_sb.rearrange("p (j c) -> p j c", j=4), AX.X, ALU.add))
        nc.vector.tensor_scalar(kvar[:, u % 2, :], ksq[:, u % 2, :], 1.0 / P, RMS_EPS, ALU.mult, ALU.add)\
            .then_inc(A.kvar_ready.sem, 1)

    def key_norm(dve, A, body, u, bank):
        done(dve, A.rk_ready, body, u)
        done(dve, A.kn_tr, body, u - 1)
        nc.vector.tensor_tensor(kn_sb.rearrange("p (j c) -> p j c", j=4), bank.rearrange("p (j c) -> p j c", j=4),
                                rk[:, u % 2, :].unsqueeze(2).broadcast_to([P, 4, P]), ALU.mult).then_inc(A.kn_ready.sem, 1)

    def key_rms(pool, A, body, u):
        done(pool, A.kvar_ready, body, u)
        nc.gpsimd.tensor_tensor(out=rk[:, u % 2, :], in0=kvar[:, u % 2, :], in1=neg_half[:, 0:4], op=ALU.pow)\
            .then_inc(A.rk_ready.sem, 1)

    KEY_BANKS = (B3, B5, B7)

    def first_keys_pe(pe, A):
        pe.wait_ge(A.kctx_ready.sem, A.kctx_ready.value(0, 0))
        for u in range(HEADS + 2):
            if u < HEADS:
                pe.wait_ge(A.kn_ready.sem, A.kn_ready.value(0, max(u - 3, -1)))
                key_mm(pe, A, u, KEY_BANKS[u % 3])
            if u >= 2:
                key_tr(pe, A, 0, u - 2, (B4, B6)[u % 2], 2)

    def first_keys_act(act, A):
        for u in range(HEADS + 3):
            if u >= 3:
                key_out(act, A, 0, u - 3, (B4, B6)[(u - 1) % 2])
            if u < HEADS:
                key_square(act, A, 0, u, KEY_BANKS[u % 3])

    def first_keys_dve(dve, A):
        link = Chain(dve, A.k_chain, 0)
        for u in range(HEADS + 1):
            if u < HEADS:
                key_var(dve, A, 0, u, link)
            if u >= 1:
                key_norm(dve, A, 0, u - 1, KEY_BANKS[(u - 1) % 3])
        link.close()

    def first_keys_pool(pool, A):
        nc.gpsimd.tensor_copy(ctxt_s, CTXT[:, 0:W]).then_inc(A.kctx_ready.sem, 1)
        for u in range(HEADS):
            key_rms(pool, A, 0, u)

    class Body:

        def __init__(self, A, s, new=True, old=True, ahead=False, old_ahead=False):
            self.first = new and not old
            self.A, self.s, self.new, self.old, self.ahead, self.old_ahead = A, s, new, old, ahead, old_ahead
            self.steps = range(A.n if new else A.late)
            if new:
                self.n, self.prev = tail_of(A.stage, s)

        def has(self, h):
            return self.new if h >= 0 else self.old

        def keys(self, u):
            return self.ahead if u >= 0 else self.old_ahead

        def of(self, h):
            return self.s if h >= 0 else self.s - 1

        def chain(self, eng, sig, late, body):
            return Chain(eng, sig, body, -late if self.old else 0)

    def run_ahead(engine, A, eng):
        engine(Body(A, 0, old=False, ahead=True))
        with eng.Fori(1, NS - 1, 1) as s:
            engine(Body(A, s, ahead=True))
        engine(Body(A, NS - 1))
        engine(Body(A, NS, new=False))

    TAIL_T = Y_LAG + 2

    def wide_run(engine, A, eng):
        last = NS - 1 if A.rms else NS
        engine(eng, Body(A, 0, old=False, ahead=A.rms))
        with eng.Fori(1, last, 1) as s:
            engine(eng, Body(A, s, ahead=A.rms, old_ahead=A.rms))
        if A.rms:
            engine(eng, Body(A, last, old_ahead=True))
        engine(eng, Body(A, NS, new=False))

    def wide_pe(pe, S):
        A, s = S.A, S.s

        def keys0(g):
            done(pe, A.k_ready, s, g - 1)
            mm(B3, A.wk[:, g * P:(g + 1) * P], CTXT[:, tok(s)]).then_inc(A.k_mm.sem, 1)

        if S.new:
            done(pe, xnt_ready, s + NS * A.stage, 1)
            if not A.rms:
                keys0(0)
        for t in S.steps:
            h = t - T_LAG
            if S.new:
                done(pe, A.qvar_ready if A.rms else A.q_ready, s, t - 1)
                for k in range(KD):
                    last = mm(B4, A.wq[:, k, t * P:(t + 1) * P], XNT[:, k, tok(s)], k == 0, k == KD - 1)
                last.then_inc(A.q_mm.sem, 1)
            if S.has(h):
                done(pe, A.pn_ready, s, h)
                done(pe, A.pt_ready, s, h - 1)
                if S.keys(t - 2):
                    done(pe, A.k_ready, s + 1, t - 2)
                for b in range(TB):
                    last = nc.tensor.transpose(B6[:, b * P:(b + 1) * P], p_sb[:, h % 4, b * P:(b + 1) * P], ident[:])
                last.then_inc(A.pt_tr.sem, 1)
            i = t - 1
            if S.has(i):
                done(pe, A.q_ready, s, i)
                done(pe, A.p_ready, s, i - 1)
                if A.rms:
                    done(pe, A.k_ready, s, i // 4 * 4 + 3)
                else:
                    done(pe, A.k_ready, s, i // A.share)
                    mm(B5, ones_b[0:1, :], mask_bias[0:1, tok(S.of(i))], True, False)
                for b in range(TB):
                    if A.rms:
                        keys = kr_sb[:, bass.ds(S.of(i) % 2, 1), i % HEADS, b * P:(b + 1) * P].rearrange("p n c -> p (n c)")
                    else:
                        keys = k0_sb[:, i // A.share % 2, b * P:(b + 1) * P]
                    last = mm(B5[:, b * P:(b + 1) * P], q_sb[:, i % 2, b * P:(b + 1) * P], keys, A.rms, True)
                last.then_inc(A.s_mm.sem, 1)
            i = t - Y_LAG
            if S.has(i):
                done(pe, A.o_ready, s, i)
                if i == 0:
                    done(pe, yt_ready, S.n, 1)
                for k in range(KD):
                    last = mm(Y[k], A.wo[:, i % HEADS, k * P:(k + 1) * P], o_sb[:, i % 2, :], i % HEADS == 0, i == -1 or i == HEADS - 1)
                last.then_inc(A.y_mm.sem, 1)
            if S.has(h):
                done(pe, A.pt_ready, s, h)
                done(pe, A.o_ready, s, h - 1)
                if h == 0:
                    done(pe, A.ctx_ready, s, 0)
                for b in range(TB):
                    last = mm(B7[:, b * P:(b + 1) * P], ctx_s[:, b, :], pt_sb[:, b * P:(b + 1) * P])
                last.then_inc(A.o_mm.sem, 1)
            if S.new and A.rms:
                done(pe, A.q_ready, s, t)
                for b in range(TB):
                    last = mm(B4[:, b:b + 1], qsq_sb[:, b * P:(b + 1) * P], ones_col[:])
                last.then_inc(A.qsq_mm.sem, 1)
            if S.ahead:
                if t == 0:
                    done(pe, A.kctx_ready, s + 1, 0)
                done(pe, A.kn_ready, s + 1, t - 1)
                key_mm(pe, A, t, B3)
            if S.keys(t - 1):
                key_tr(pe, A, s + 1, t - 1, B6)
            if S.new and not A.rms and t % A.share == A.share - 1 and (t + 1) // A.share < A.kv_heads:
                keys0((t + 1) // A.share)
            if S.new and t - TAIL_T in (0, 1):
                tail_pe_y(pe, S.n, t - TAIL_T)
            if S.new and t - TAIL_T in (4, 5):
                tail_pe_xn(pe, S.n, t - TAIL_T - 4)

    def wide_act(act, S):
        A, s = S.A, S.s

        def keys0(g):
            done(act, A.k_mm, s, g)
            done(act, A.s_mm, s, (g - 1) * A.share - 1)
            nc.scalar.activation(k0_sb[:, g % 2, :], B3, ACT.Copy).then_inc(A.k_ready.sem, 1)

        def out_of_y(n):
            done(act, yt_tr, n - 1, 1)
            done(act, A.y_mm, s, -1)
            g = A.stage // 2
            for k in range(KD):
                nc.scalar.activation(YT[:, k, :], Y[k], ACT.Copy, scale=gates[:, g:g + 1]).then_inc(yt_ready.sem, 1)

        if S.new and not A.rms:
            keys0(0)
        for t in S.steps:
            if t == Y_LAG and S.old:
                out_of_y(S.n)
            if S.keys(t - 2):
                key_out(act, A, s + 1, t - 2, B6)
            if S.keys(t - 1):
                key_square(act, A, s + 1, t - 1, B3)
            if S.new and not A.rms and t and t % A.share == 0:
                keys0(t // A.share)
            if S.new:
                done(act, A.q_mm, s, t)
                done(act, A.s_mm, s, t - 2)
                ins = nc.scalar.activation(q_sb[:, t % 2, :], B4, ACT.Copy)
                if A.rms:
                    done(act, A.qsq_mm, s, t - 1)
                    ins = nc.scalar.activation(qsq_sb, B4, ACT.Square)
                ins.then_inc(A.q_ready.sem, 1)
            h = t - 1
            if S.has(h):
                done(act, A.negm_ready, s, h)
                done(act, A.pt_tr, s, h - 4)
                for b in range(TB):
                    last = nc.scalar.activation(p_sb[:, h % 4, b * P:(b + 1) * P], B5[:, b * P:(b + 1) * P], ACT.Exp,
                                                bias=negm[:, h % 2, b:b + 1],
                                                scale=rq[:, h % 2, b:b + 1] if A.rms else SCALE_WIDE,
                                                accum_out=sums[:, h % 2, b:b + 1])
                last.then_inc(A.p_ready.sem, 1)
            h = t - T_LAG
            if S.has(h):
                done(act, A.o_mm, s, h)
                done(act, A.y_mm, s, h - 2)
                nc.scalar.activation(o_sb[:, h % 2, :], B7, ACT.Copy).then_inc(A.o_ready.sem, 1)
            if S.new and t - TAIL_T in (4, 5):
                tail_act(act, S.n, S.prev, t - TAIL_T - 4)
        if not S.new:
            out_of_y(tail_of(A.stage, s)[0])

    def wide_dve(dve, S):
        A, s = S.A, S.s
        link = S.chain(dve, A.chain, 1 if A.rms else 5, s)
        if S.ahead or S.old_ahead:
            k_link = Chain(dve, A.k_chain, s + 1, -1 if S.old_ahead else 0)
        for t in S.steps:
            h = t - 2
            if S.has(h):
                i = h % 2
                done(dve, A.p_ready, s, h)
                done(dve, A.pn_ready, s, h - 2)
                if A.rms:
                    nc.vector.reciprocal(rinv[:, i, :], sums[:, i, :]).then_inc(A.rinv_ready.sem, 1)
                else:
                    link(nc.vector.tensor_scalar(mx[:, i, :], sums[:, i, :], TINY, None, ALU.max))
                    link(nc.vector.reciprocal(mx[:, i, :], mx[:, i, :]))
                    nc.vector.tensor_tensor(rinv[:, i, :], mx[:, i, :], any_key[:, bass.ds(S.of(h) * TB, TB)], ALU.mult)\
                        .then_inc(A.rinv_ready.sem, 1)
            if S.keys(t - 1):
                key_var(dve, A, s + 1, t - 1, k_link)
            h = t - T_LAG
            if S.has(h):
                done(dve, A.pt_tr, s, h)
                done(dve, A.o_mm, s, h - 1)
                nc.vector.tensor_copy(pt_sb, B6).then_inc(A.pt_ready.sem, 1)
            if S.keys(t - 1):
                key_norm(dve, A, s + 1, t - 1, B3)
            h = t - 1
            if S.has(h):
                i = h % 2
                done(dve, A.s_mm, s, h)
                link(nc.vector.tensor_reduce(mx[:, i, :], B5.rearrange("p (b k) -> p b k", b=TB), AX.X, ALU.max))
                if A.rms:
                    done(dve, A.rq_ready, s, h)
                    nc.vector.scalar_tensor_tensor(negm[:, i, :], mx[:, i, :], -1.0, rq[:, i, :], ALU.mult, ALU.mult)\
                        .then_inc(A.negm_ready.sem, 1)
                else:
                    nc.vector.tensor_scalar(negm[:, i, :], mx[:, i, :], -SCALE_WIDE, None, ALU.mult)\
                        .then_inc(A.negm_ready.sem, 1)
            if S.new and A.rms:
                done(dve, A.qsq_mm, s, t)
                done(dve, A.p_ready, s, t - 2)
                nc.vector.tensor_scalar(qvar[:, t % 2, :], B4[:, 0:TB], 1.0 / P, RMS_EPS, ALU.mult, ALU.add)\
                    .then_inc(A.qvar_ready.sem, 1)
            if S.new and t - TAIL_T in (0, 1):
                tail_dve_add(dve, S.n, S.prev, t - TAIL_T)
            if S.new and t - TAIL_T == 2:
                tail_dve_stats(dve, S.n, S.prev)
            if S.new and t - TAIL_T == 3:
                tail_dve_norm(dve, S.n, S.prev)

    def wide_pool(pool, S):
        A, s = S.A, S.s
        if S.new and not S.old:
            done(pool, yt_ready, S.n, 1)
        if S.ahead:
            done(pool, A.kt_mm, s, HEADS - 1)
            nc.gpsimd.tensor_copy(ctxt_s, CTXT[:, tok(s + 1)]).then_inc(A.kctx_ready.sem, 1)
        for t in S.steps:
            h = t - 2
            if S.has(h):
                done(pool, A.rinv_ready, s, h)
                pv = p_sb[:, h % 4, :].rearrange("p (b k) -> p b k", b=TB)
                nc.gpsimd.tensor_tensor(out=pv, in0=pv, in1=rinv[:, h % 2, :].unsqueeze(2).broadcast_to([P, TB, P]),
                                        op=ALU.mult).then_inc(A.pn_ready.sem, 1)
            if S.keys(t - 1):
                key_rms(pool, A, s + 1, t - 1)
            if S.new and A.rms:
                done(pool, A.qvar_ready, s, t)
                nc.gpsimd.tensor_tensor(out=rq[:, t % 2, :], in0=qvar[:, t % 2, :], in1=neg_half[:, 0:4], op=ALU.pow)\
                    .then_inc(A.rq_ready.sem, 1)
            if S.new and t == T_LAG - 1:
                done(pool, A.o_mm, s, -1)
                nc.gpsimd.tensor_copy(ctx_s, CTX[:, bass.ds(s * TB, TB), :]).then_inc(A.ctx_ready.sem, 1)
            if S.new and t - TAIL_T == 2:
                tail_pool(pool, S.n)


    L0 = Wide("a0", 0, 8, l0_wq, l0_wk, l0_wv, l0_wo, False)

    E0 = 4
    sg0 = tile(WK, 0, 512).rearrange("p (n c) -> p n c", n=2)
    h0 = tile(WK, 512, 512).rearrange("p (n k c) -> p n k c", n=2, k=2)
    f0_gu = signal("moe_g_mm", E0)
    f0_sg = signal("moe_sg_ready", E0)
    f0_h = signal("moe_h_ready", E0)
    f0_y = signal("moe_y_mm", E0)
    TE = W // E0

    def ffn0_pe(pe, i, s):
        n, _ = tail_of(i, s)
        done(pe, xnt_ready, s + NS * i, 1)
        xe = XNT.rearrange("p k (s t e) -> p k s e t", s=NS, e=E0)
        for e in range(E0 + 1):
            if e < E0:
                done(pe, f0_h, s, max(e - 2, -1))
                bank = (B4, B5)[e % 2]
                for m in range(4):
                    for k in range(KD):
                        rhs = xe[:, k, bass.ds(s, 1), e, :].rearrange("p s t -> p (s t)")
                        last = mm(bank[:, m * P:(m + 1) * P], l0_gu[:, e, k, m * P:(m + 1) * P], rhs, k == 0, k == KD - 1)
                last.then_inc(f0_gu.sem, 1)
            if e < 2:
                tail_pe_y(pe, n, e)
            if e >= 3:
                tail_pe_xn(pe, n, e - 3)
            if e >= 1:
                j = e - 1
                done(pe, f0_h, s, j)
                if j == 0:
                    done(pe, yt_ready, n, 1)
                for k in range(KD):
                    for m in range(2):
                        last = mm(Y[k][:, j * TE:(j + 1) * TE], l0_dn[:, j, m, k * P:(k + 1) * P], h0[:, j % 2, m, :],
                                  m == 0, m == 1)
                last.then_inc(f0_y.sem, 1)

    def ffn0_act(act, i, s):
        n, prev = tail_of(i, s)
        for e in range(E0):
            done(act, f0_gu, s, e)
            done(act, f0_h, s, max(e - 2, -1))
            nc.scalar.activation(sg0[:, e % 2, :], (B4, B5)[e % 2][:, 0:2 * P], ACT.Silu).then_inc(f0_sg.sem, 1)
        tail_act(act, n, prev, 0)
        done(act, yt_tr, n, 1)
        done(act, f0_y, s, E0 - 1)
        g = 4 + i // 2
        for k in range(KD):
            nc.scalar.activation(YT[:, k, :].rearrange("p (t e) -> p e t", e=E0), Y[k].rearrange("p (e t) -> p e t", e=E0),
                                 ACT.Copy, scale=gates[:, g:g + 1]).then_inc(yt_ready.sem, 1)
        tail_act(act, n, prev, 1)

    def ffn0_dve(dve, i, s):
        n, prev = tail_of(i, s)
        for e in range(E0):
            done(dve, f0_sg, s, e)
            done(dve, f0_y, s, max(e - 2, -1))
            nc.vector.tensor_tensor(h0[:, e % 2, :, :].rearrange("p k c -> p (k c)"), sg0[:, e % 2, :],
                                    (B4, B5)[e % 2][:, 2 * P:4 * P], ALU.mult).then_inc(f0_h.sem, 1)
            if e < 2:
                tail_dve_add(dve, n, prev, e)
            if e == 1:
                tail_dve_stats(dve, n, prev)
            if e == 2:
                tail_dve_norm(dve, n, prev)

    def ffn0_pool(pool, i, s):
        n, _ = tail_of(i, s)
        tail_pool(pool, n)

    NB = 4

    N_LAG = 4
    V_LAG = N_LAG + 1
    N_END = V_LAG + 1

    class Narrow:

        def __init__(self, name, stage, heads, main, wout, bias, tail_t):
            self.name, self.stage, self.heads, self.wout, self.bias = name, stage, heads, wout, bias
            self.split = main < P
            self.parts = ((0, 0, main), (1, main, P)) if self.split else ((0, 0, P),)
            self.hd = D // heads
            self.rows = NB * self.hd
            self.per_half = P // self.rows
            self.groups = KD * self.per_half
            self.n = TB * self.groups
            self.late = N_END
            self.units = TB * KD
            n, u = self.n, self.units
            self.chain = signal("narrow_chain", n + u)
            self.needs_qk, self.needs_v = {}, {}
            self.tail_t = tail_t
            self.kblk_ready = signal("narrow_kblk_ready", u)
            self.s_mm = signal("narrow_s_mm", n)
            self.negm_ready = signal("narrow_negm_ready", n)
            self.p_ready = signal("narrow_p_ready", n)
            self.rinv_ready = signal("narrow_rinv_ready", n)
            self.pn_ready = signal("narrow_pn_ready", n)
            self.pt_tr = signal("narrow_pt_tr", n)
            self.pt_ready = signal("narrow_pt_ready", n)
            self.o_mm = signal("narrow_o_mm", n)
            self.ot_ready = signal("narrow_ot_ready", u)
            self.y_mm = signal("narrow_y_mm", KD)

        def pt_on_act(self, u):
            return not self.split and u % 2 == 0

    n_p = tile(WK, 0, 2048).rearrange("p (n h k) -> p n h k", n=4, h=NB)
    n_pt = tile(WK, 2048, 1024).rearrange("p (n c) -> p n c", n=2)
    n_kblk = tile(WK, 3072, 1024).rearrange("p (n h k) -> p n h k", n=2, h=NB)
    n_own = tile(WK, 4096, 1024).rearrange("p (n h q) -> p n h q", n=2, h=NB)
    n_mx = sb("n_mx", [P, 4, 2 * NB])
    n_negm = sb("n_negm", [P, 4, 2 * NB])
    n_sums = sb("n_sums", [P, 4, 2 * NB])
    n_rinv = sb("n_rinv", [P, 4, 2 * NB])
    S_BANKS = (B4, B5, B3)

    def nothing(S, t):
        pass

    def place(A, g):
        c, r = g % A.n // A.per_half, g % A.per_half
        return c, r, c // KD, c % KD

    def narrow_pe(pe, S, q_t, v_pad, o_t, beside):
        A, s = S.A, S.s

        def out_product():
            done(pe, A.ot_ready, s, -1)
            for k in range(KD):
                for hf in range(KD):
                    last = mm(Y[k], A.wout[:, hf, k * P:(k + 1) * P], o_t[:, hf, :], hf == 0, hf == KD - 1)
                last.then_inc(A.y_mm.sem, 1)

        for t in S.steps:
            u = t - N_LAG
            if S.has(u):
                done(pe, A.pn_ready, s, u)
                done(pe, A.pt_ready, s, u - 1)
                for j in range(NB):
                    last = nc.tensor.transpose(B6[:, j * P:(j + 1) * P], n_p[:, u % 4, j, :], ident[:])
                last.then_inc(A.pt_tr.sem, 1)
            if S.new:
                c, r, b, hf = place(A, t)
                r0 = r * A.rows
                if t in A.needs_qk:
                    done(pe, A.needs_qk[t][0], s, A.needs_qk[t][1])
                if r == 0:
                    done(pe, A.kblk_ready, s, c)
                before = t - 3 if t >= 3 else max(g for g in range(A.n - 3, A.n) if g % 3 == t) - A.n
                done(pe, A.p_ready, s, before)
                mm(S_BANKS[t % 3], q_t[r0:r0 + A.rows, hf, b * P:(b + 1) * P],
                   n_kblk[r0:r0 + A.rows, c % 2, :, :].rearrange("p h k -> p (h k)")).then_inc(A.s_mm.sem, 1)
            u = t - V_LAG
            if S.has(u):
                c, r, b, hf = place(A, u)
                done(pe, A.pt_ready, s, u)
                if u in A.needs_v:
                    done(pe, A.needs_v[u][0], s, A.needs_v[u][1])
                if r == 0:
                    done(pe, A.ot_ready, s, u // A.per_half - 2)
                    if u == A.per_half:
                        done(pe, yt_ready, S.n, 1)
                mm(narrow_out(c), v_pad[:, b, hf, r, :], n_pt[:, u % 2, :], r == 0, r == A.per_half - 1).then_inc(A.o_mm.sem, 1)
            if S.new and t - A.tail_t in (0, 1):
                tail_pe_y(pe, S.n, t - A.tail_t)
            if S.new and t - A.tail_t in (4, 5):
                tail_pe_xn(pe, S.n, t - A.tail_t - 4)
            beside(S, t)
            if S.old and t == N_END:
                out_product()
        if not S.new:
            out_product()

    def narrow_out(c):
        return (B7, Y[1])[c % 2]

    def narrow_act(act, S, scale, beside):
        A, s = S.A, S.s

        def out_of_y(n, k):
            done(act, yt_tr, n - 1, 1)
            done(act, A.y_mm, s, k - KD)
            g = A.stage // 2
            nc.scalar.activation(YT[:, k, :], Y[k], ACT.Identity, scale=gates[:, g:g + 1], bias=A.bias[:, k:k + 1])\
                .then_inc(yt_ready.sem, 1)

        for t in S.steps:
            if S.old and t - N_END in (1, 2):
                out_of_y(S.n, t - N_END - 1)
            u = t - N_LAG
            if A.pt_on_act(u) and S.has(u):
                done(act, A.pt_tr, s, u)
                done(act, A.o_mm, s, u - 2)
                nc.scalar.activation(n_pt[:, u % 2, :], B6, ACT.Copy).then_inc(A.pt_ready.sem, 1)
            if S.new:
                i = t % 4
                done(act, A.negm_ready, s, t)
                done(act, A.pt_tr, s, t - 4)
                done(act, A.rinv_ready, s, t - 4)
                for x, lo, hi in A.parts:
                    for j in range(NB):
                        m = x * NB + j
                        last = nc.scalar.activation(n_p[:, i, j, lo:hi], S_BANKS[t % 3][:, j * P + lo:j * P + hi], ACT.Exp,
                                                    bias=n_negm[:, i, m:m + 1], scale=scale, accum_out=n_sums[:, i, m:m + 1])
                last.then_inc(A.p_ready.sem, 1)
            if S.new and t - A.tail_t in (4, 5):
                tail_act(act, S.n, S.prev, t - A.tail_t - 4)
            beside(S, t)
        if not S.new:
            for k in range(KD):
                out_of_y(tail_of(A.stage, s)[0], k)

    def narrow_dve(dve, S, o_t, head_mask, scale, beside):
        A, s = S.A, S.s
        late = sum((c + 1) * A.per_half + V_LAG >= A.n for c in range(A.units))
        link = S.chain(dve, A.chain, late, s)
        m = NB * len(A.parts)
        for t in S.steps:
            u = t - N_LAG
            if not A.pt_on_act(u) and S.has(u):
                done(dve, A.pt_tr, s, u)
                done(dve, A.o_mm, s, u - 2)
                nc.vector.tensor_copy(n_pt[:, u % 2, :], B6).then_inc(A.pt_ready.sem, 1)
            if S.new:
                done(dve, A.s_mm, s, t)
                bank = S_BANKS[t % 3].rearrange("p (h k) -> p h k", h=NB)
                for x, lo, hi in A.parts:
                    ins = nc.vector.tensor_reduce(n_mx[:, t % 4, x * NB:(x + 1) * NB], bank[:, :, lo:hi], AX.X, ALU.max)
                link(ins)
                done(dve, A.p_ready, s, t - 4)
                nc.vector.tensor_scalar(n_negm[:, t % 4, 0:m], n_mx[:, t % 4, 0:m], -scale, None, ALU.mult)\
                    .then_inc(A.negm_ready.sem, 1)
            u = t - 1
            if S.has(u):
                done(dve, A.p_ready, s, u)
                done(dve, A.pn_ready, s, u - 4)
                nc.vector.reciprocal(n_rinv[:, u % 4, 0:m], n_sums[:, u % 4, 0:m]).then_inc(A.rinv_ready.sem, 1)
            if S.new and t - A.tail_t in (0, 1):
                tail_dve_add(dve, S.n, S.prev, t - A.tail_t)
            if S.new and t - A.tail_t == 2:
                tail_dve_stats(dve, S.n, S.prev)
            if S.new and t - A.tail_t == 3:
                tail_dve_norm(dve, S.n, S.prev, s if A.split else None)
            u = t - V_LAG
            if u % A.per_half == 0 and S.has(u - 1):
                c, r, b, hf = place(A, u - 1)
                done(dve, A.o_mm, s, u - 1)
                link(nc.vector.tensor_tensor(n_own[:, c % 2], narrow_out(c).rearrange("p (h q) -> p h q", h=NB),
                                             head_mask[:].unsqueeze(2).broadcast_to([P, NB, P]), ALU.mult))
                if c == 0:
                    done(dve, A.y_mm, s, -1)
                nc.vector.tensor_reduce(o_t[:, hf, b * P:(b + 1) * P], n_own[:, c % 2].rearrange("p h q -> p q h"), AX.X, ALU.add)\
                    .then_inc(A.ot_ready.sem, 1)
            beside(S, t)

    def narrow_pool(pool, S, k_t, head_mask, beside):
        A, s = S.A, S.s

        def key_blocks(body, c):
            b, hf = c // KD, c % KD
            g = c * A.per_half
            if g in A.needs_qk:
                done(pool, A.needs_qk[g][0], body, A.needs_qk[g][1])
            done(pool, A.s_mm, body, max(g - A.per_half - 1, -4))
            nc.gpsimd.tensor_tensor(out=n_kblk[:, c % 2, :, :],
                                    in0=k_t[:, hf, b * P:(b + 1) * P].unsqueeze(1).broadcast_to([P, NB, P]),
                                    in1=head_mask[:].unsqueeze(2).broadcast_to([P, NB, P]),
                                    op=ALU.mult).then_inc(A.kblk_ready.sem, 1)

        if S.new and not S.old:
            key_blocks(s, 0)
        for t in S.steps:
            if S.new and t % A.per_half == 0:
                c = t // A.per_half + 1
                if c < A.units:
                    key_blocks(s, c)
                elif S.ahead:
                    key_blocks(s + 1, 0)
            u = t - 2
            if S.has(u):
                done(pool, A.rinv_ready, s, u)
                for x, lo, hi in A.parts:
                    pv = n_p[:, u % 4, :, lo:hi]
                    ins = nc.gpsimd.tensor_tensor(out=pv, in0=pv, op=ALU.mult,
                                                  in1=n_rinv[:, u % 4, x * NB:(x + 1) * NB].unsqueeze(2).broadcast_to([P, NB, hi - lo]))
                ins.then_inc(A.pn_ready.sem, 1)
            if S.new and t - A.tail_t == 2:
                tail_pool(pool, S.n)
            beside(S, t)

    L1H, L1HD = 32, 8
    TWO_PI_HI = 6.28125
    TWO_PI_LO = 2 * 3.141592653589793 - TWO_PI_HI
    ROUND = 1.5 * 2 ** 23
    PI = 3.1415925
    l1_wq = tile(R2, 6144, 512).rearrange("p (k n) -> p k n", k=KD)
    l1_wqs = tile(R2, 6656, 512).rearrange("p (k n) -> p k n", k=KD)
    l1_wkv = tile(R2, 7168, 512)
    l1_wks = tile(R2, 7680, 256)
    l1_wout = tile(R2, 7936, 512).rearrange("p (k n) -> p k n", k=KD)
    pos_t = tile(R2, 17000, 2048)
    r_cos = tile(R2, 8448, 512)
    r_sin = tile(R2, 8960, 512)
    r_k = tile(R2, 9472, 512)
    r_a = tile(R2, 9984, 512)
    r_b = tile(R2, 10496, 512)
    l1_q = tile(R2, 11008, 1024).rearrange("p (k c) -> p k c", k=KD)
    l1_k = tile(R2, 12032, 1024).rearrange("p (k c) -> p k c", k=KD)
    l1_v = tile(R1, 0, TB * KD * 4 * P).rearrange("p (t h r c) -> p t h r c", t=TB, h=KD, r=4)
    l1_ot = tile(R2, 14080, 1024).rearrange("p (k c) -> p k c", k=KD)
    l1_cs = tile(R2, 15104, 512)
    freq = sb("freq", [2, P])
    hmask8 = sb("hmask8", [P, NB])
    hmask16 = sb("hmask16", [P, NB])
    head_sel8 = sb("head_sel8", [P, 4, NB])
    head_sel16 = sb("head_sel16", [P, 2, NB])
    pool_consts = semaphore("pool_consts")
    hmask_ready = semaphore("hmask_ready")
    l1_bias = sb("l1_bias", [P, KD])
    in_l1x = semaphore("in_l1x")
    l1w_ready = semaphore("l1w_ready")
    L1 = Narrow("a1", 2, L1H, P, l1_wout, l1_bias, 9)
    CH = 2
    CB = TB // CH
    CW = CB * P
    l1_ctx = signal("narrow_in_ready", 1)
    ang_mm = signal("a1_ang_mm", 1)
    ang_ready = signal("a1_ang_ready", 2)
    sin_ready = signal("a1_sin_ready", 2)
    rope_mm = signal("a1_rope_mm", 2 * CH)
    rope_ready = signal("a1_rope_ready", 2 * CH)
    rope_chain = signal("narrow_qk_chain", 9 + 2 * CH)
    l1_v_mm = signal("narrow_v_mm", CH)
    l1_v_ready = signal("a1_v_ready", CH)
    for j in range(CH):
        L1.needs_qk[j * CB * L1.groups] = (rope_ready, 2 * j + 1)
        L1.needs_v[j * CB * L1.groups] = (l1_v_ready, j)

    def rope_angles_pe(pe, s):
        mm(Y[0], freq[0:2, :], pos_t[0:2, tok(s)]).then_inc(ang_mm.sem, 1)

    def rope_qk_pe(pe, s, j, i):
        if i == 0:
            done(pe, l1_v_ready, s, j - 1)
            if j == 0:
                done(pe, ang_ready, s, 1)
            else:
                done(pe, rope_ready, s, 2 * j - 1)
        else:
            done(pe, rope_ready, s, 2 * j)
        cols = bass.ds(s * W + j * CW, CW)
        for bank, wq, wk in ((TP, l1_wq, l1_wkv), (Y[0], l1_wqs, l1_wks)):
            for hf in range(KD):
                out_cols = bank[:, hf * CW:(hf + 1) * CW]
                if i == 0:
                    for k in range(KD):
                        last = mm(out_cols, wq[:, k, hf * P:(hf + 1) * P], XNT[:, k, cols], k == 0, k == KD - 1)
                else:
                    last = mm(out_cols, wk[:, hf * P:(hf + 1) * P], CTXT[:, cols])
        last.then_inc(rope_mm.sem, 1)

    def rope_v_pe(pe, s, j):
        done(pe, rope_ready, s, 2 * j + 1)
        done(pe, l1_ctx, s, 0)
        for b in range(CB):
            last = mm(TP[:, b * D:(b + 1) * D], l1_cs[:, (j * CB + b) * P:(j * CB + b + 1) * P], l1_wkv[:, D:2 * D])
        last.then_inc(l1_v_mm.sem, 1)

    def rope_sin_act(act, s):
        for i, dst in enumerate((r_sin, r_cos)):
            done(act, ang_ready, s, i)
            nc.scalar.activation(dst, dst, ACT.Sin).then_inc(sin_ready.sem, 1)

    def rope_v_act(act, s, j, first):
        done(act, l1_v_mm, s, j)
        if not first:
            done(act, L1.o_mm, s, (j + 1) * CB * L1.groups - L1.n - 1)
        v = TP.rearrange("p (t h r c) -> p t h r c", t=CB, h=KD, r=4)
        for r in range(4):
            c = slice(r * P // 4, (r + 1) * P // 4)
            ins = nc.scalar.activation(l1_v[:, j * CB:(j + 1) * CB, :, r, c], v[:, :, :, r, :], ACT.Copy)
        ins.then_inc(l1_v_ready.sem, 1)

    ANGLE_STEPS = 6

    def rope_angles_dve(dve, s, step, link):
        i, part = step // 3, step % 3
        dst, shift = (r_sin, r_cos)[i], (0.0, 0.25)[i]
        if part == 0:
            done(dve, ang_mm, s, 0)
            link(nc.vector.tensor_scalar(r_k, Y[0], 1.0 / (TWO_PI_HI + TWO_PI_LO), shift, ALU.mult, ALU.add))
            link(nc.vector.tensor_scalar(r_k, r_k, ROUND, -ROUND, ALU.add, ALU.add))
        if part == 1:
            link(nc.vector.scalar_tensor_tensor(r_a, r_k, -TWO_PI_HI, Y[0], ALU.mult, ALU.add))
            link(nc.vector.scalar_tensor_tensor(r_b, r_k, -TWO_PI_LO, r_a, ALU.mult, ALU.add))
        if part == 2:
            if shift:
                link(nc.vector.tensor_scalar(r_b, r_b, 0.5 * 3.141592653589793, None, ALU.add))
            nc.vector.tensor_scalar(dst, r_b, -PI, PI, ALU.max, ALU.min).then_inc(ang_ready.sem, 1)

    def rope_qk_dve(dve, s, j, i, first, link):
        done(dve, sin_ready, s, 1)
        done(dve, rope_mm, s, 2 * j + i)
        if not first:
            if i == 0:
                done(dve, L1.s_mm, s, (j + 1) * CB * L1.groups - L1.n - 1)
            else:
                done(dve, L1.kblk_ready, s, (j + 1) * CB * KD - L1.units - 1)
        cols = slice(j * CW, (j + 1) * CW)

        def both(x):
            return x[:, cols].unsqueeze(1).broadcast_to([P, KD, CW])

        def halves(x):
            return x.rearrange("p (k c) -> p k c", k=KD)

        nc.vector.tensor_tensor(halves(r_a), halves(TP), both(r_cos), ALU.mult)
        link(nc.vector.tensor_tensor(halves(r_b), halves(Y[0]), both(r_sin), ALU.mult))
        nc.vector.tensor_tensor((l1_q, l1_k)[i][:, :, cols], halves(r_a), halves(r_b), ALU.add).then_inc(rope_ready.sem, 1)
        done(dve, rope_ready, s, 2 * j + i)

    def rope_context(dve, s):
        nc.vector.tensor_copy(l1_cs, CTXT[:, tok(s)]).then_inc(l1_ctx.sem, 1)

    def rope_pe(pe):
        def beside(S, t):
            if S.new and t in (0, 2):
                rope_qk_pe(pe, S.s, 1, t // 2)
            if S.new and t == 5:
                rope_v_pe(pe, S.s, 1)
            if S.new and t == L1.tail_t - 1:
                done(pe, l1_v_ready, S.s, 1)
            if S.ahead and t == 11:
                rope_angles_pe(pe, S.s + 1)
            if S.ahead and t in (19, 22):
                if t == 19:
                    done(pe, xnt_ready, S.n, 1)
                rope_qk_pe(pe, S.s + 1, 0, (t - 19) // 3)
            if S.ahead and t == 25:
                rope_v_pe(pe, S.s + 1, 0)

        n = tail_of(L1.stage, 0)[0]
        done(pe, xnt_ready, n, -1)
        done(pe, yt_ready, n, 1)
        rope_angles_pe(pe, 0)
        for i in range(2):
            rope_qk_pe(pe, 0, 0, i)
        rope_v_pe(pe, 0, 0)
        return beside

    def rope_act(act):
        def beside(S, t):
            if S.new and t == 6:
                rope_v_act(act, S.s, 1, not S.old)
            if S.ahead and t == 18:
                rope_sin_act(act, S.s + 1)
            if S.ahead and t == 26:
                rope_v_act(act, S.s + 1, 0, False)

        rope_sin_act(act, 0)
        rope_v_act(act, 0, 0, True)
        return beside

    def rope_dve(dve):
        links = []

        def beside(S, t):
            if S.new and t == 0:
                links[:] = [Chain(dve, rope_chain, S.s, rope_chain.per - 2)]
            if S.new and t in (1, 3):
                rope_qk_dve(dve, S.s, 1, t // 2, not S.old, links[0])
            if S.ahead and t == 7:
                done(dve, l1_v_mm, S.s, 1)
                rope_context(dve, S.s + 1)
            if S.ahead and 12 <= t < 12 + ANGLE_STEPS:
                if t == 12:
                    links[:] = [Chain(dve, rope_chain, S.s + 1)]
                rope_angles_dve(dve, S.s + 1, t - 12, links[0])
            if S.ahead and t in (20, 23):
                rope_qk_dve(dve, S.s + 1, 0, (t - 20) // 3, False, links[0])

        links[:] = [Chain(dve, rope_chain, 0)]
        done(dve, yt_ready, tail_of(L1.stage, 0)[0], 1)
        rope_context(dve, 0)
        for step in range(ANGLE_STEPS):
            rope_angles_dve(dve, 0, step, links[0])
        for i in range(2):
            rope_qk_dve(dve, 0, 0, i, True, links[0])
        return beside

    class Router:

        def __init__(self, name, stage, experts, top_k, w, arena, base, banks):
            self.name, self.stage, self.E, self.K, self.w = name, stage, experts, top_k, w
            self.lg_bank, self.lt_bank = banks
            self.lg_mm = signal("moe_lg_mm", 1)
            self.lg_ready = signal("moe_lg_ready", 1)
            self.lg_tr = signal("moe_lg_tr", 1)
            self.sub_ready = signal("moe_sub_ready", 1)
            self.e_ready = signal("moe_e_ready", 1)
            self.chain = None
            o = [base]

            def take(n):
                o[0] += n
                return tile(arena, o[0] - n, n)

            E = experts
            self.lg_sb = take(W)
            self.e = take(TB * E).rearrange("p (t e) -> p t e", t=TB)
            self.c = take(TB * E).rearrange("p (t e) -> p t e", t=TB)
            self.oh = take(TB * E).rearrange("p (t e) -> p t e", t=TB)
            self.top = take(TB * 8).rearrange("p (t k) -> p t k", t=TB)
            self.ixf = take(TB * 8).rearrange("p (t k) -> p t k", t=TB)
            self.ix = take(TB * 8).bitcast(U32).rearrange("p (t k) -> p t k", t=TB)
            self.small = take(4 * TB)
            self.end = o[0]

    iota = sb("iota", [P, 64])
    iota_i = sb("iota_i", [P, 64], I32)

    def router_logits(pe, A, s):
        done(pe, xnt_ready, s + NS * A.stage, 1)
        for k in range(KD):
            last = mm(A.lg_bank[0:A.E, :], A.w[:, k, :], XNT[:, k, tok(s)], k == 0, k == KD - 1)
        last.then_inc(A.lg_mm.sem, 1)

    def router_turn(pe, A, s):
        done(pe, A.lg_ready, s, 0)
        for t in range(TB):
            last = nc.tensor.transpose(A.lt_bank[:, t * A.E:(t + 1) * A.E], A.lg_sb[0:A.E, t * P:(t + 1) * P], ident[0:A.E, 0:A.E])
        last.then_inc(A.lg_tr.sem, 1)

    def router_out(act, A, s):
        done(act, A.lg_mm, s, 0)
        nc.scalar.activation(A.lg_sb[0:A.E, :], A.lg_bank[0:A.E, :], ACT.Copy).then_inc(A.lg_ready.sem, 1)

    def router_exp(act, A, s):
        done(act, A.sub_ready, s, 0)
        nc.scalar.activation(A.e, A.e, ACT.Exp).then_inc(A.e_ready.sem, 1)

    def router_sub(dve, A, s, link):
        done(dve, A.lg_tr, s, 0)
        lg = A.lt_bank[:, 0:TB * A.E].rearrange("p (t e) -> p t e", t=TB)
        top1 = A.small[:, 0:TB]
        link(nc.vector.tensor_reduce(top1, lg, AX.X, ALU.max))
        nc.vector.tensor_tensor(A.e, lg, top1.unsqueeze(2).broadcast_to([P, TB, A.E]), ALU.subtract).then_inc(A.sub_ready.sem, 1)

    def router_top(dve, A, s, link, over_all):
        den = A.small[:, TB:2 * TB]
        done(dve, A.e_ready, s, 0)
        for t in range(TB):
            ins = nc.vector.max(A.top[:, t, :], A.e[:, t, :])
        link(ins)
        for t in range(TB):
            ins = nc.vector.max_index(A.ix[:, t, :], A.top[:, t, :], A.e[:, t, :])
        link(ins)
        nc.vector.tensor_copy(A.ixf, A.ix)
        link(nc.vector.tensor_reduce(den, A.e if over_all else A.top[:, :, 0:A.K], AX.X, ALU.add))
        link(nc.vector.reciprocal(den, den))
        link(nc.vector.tensor_tensor(A.top, A.top, den.unsqueeze(2).broadcast_to([P, TB, 8]), ALU.mult))

    def one_hot(A, k):
        return nc.vector.tensor_tensor(A.oh, iota[:, 0:A.E].unsqueeze(1).broadcast_to([P, TB, A.E]),
                                       A.ixf[:, :, k:k + 1].broadcast_to([P, TB, A.E]), ALU.is_equal)

    class Dense:

        def __init__(self, name, stage, router, ff, extra, wg, wu, wd, sel):
            self.name, self.stage, self.r = name, stage, router
            self.cols = router.E * ff
            self.total = self.cols + extra
            self.ff = ff
            self.m = -(-self.total // P)
            self.n, self.late = self.m, 1
            self.routed = self.cols // P
            self.wg, self.wu, self.wd = wg, wu, wd
            self.E3 = 3 * router.E
            router.chain = signal("moe_r_chain", 3 * router.K + 9)
            self.c_ready = signal("moe_c_ready", 1)
            self.c_tr = signal("moe_c_tr", 1)
            self.ct_ready = signal("moe_ct_ready", 1)
            self.g_mm = signal("moe_g_mm", self.m)
            self.u_mm = signal("moe_u_mm", self.m)
            self.w_mm = signal("moe_w_mm", self.routed)
            self.sg_ready = signal("moe_sg_ready", self.m)
            self.su_ready = signal("moe_su_ready", self.m)
            self.h_ready = signal("moe_h_ready", self.m)
            self.y_mm = signal("moe_y_mm", self.m)
            o = router.end
            self.c3 = tile(WK, o, TB * self.E3 // 2).bitcast(BF16).rearrange("p (t x e) -> p t x e", t=TB, x=3)
            o += TB * self.E3 // 2
            self.ct = tile(WK, o, W // 2).bitcast(BF16)
            o += W // 2
            self.sg = tile(WK, o, 2 * W).rearrange("p (n c) -> p n c", n=2)
            self.h = tile(WK, o + 2 * W, 2 * W).rearrange("p (n c) -> p n c", n=2)
            self.sel = sel.bitcast(BF16)

        def width(self, m):
            return min(P, self.total - m * P)

    DENSE_TAIL = 2

    def dense_before(A, m):
        return m - 2 if m >= 2 else max(j for j in (A.m - 1, A.m - 2) if j % 2 == m % 2) - A.m

    def weights_turn(pe, A, s):
        done(pe, A.c_ready, s, 0)
        b7 = B7.bitcast(BF16)
        for t in range(TB):
            last = nc.tensor.transpose(b7[0:A.E3, t * P:(t + 1) * P], A.c3[:, t, :, :].rearrange("p x e -> p (x e)"), ident_b[:])
        last.then_inc(A.c_tr.sem, 1)

    def weights_out(act, A, s):
        done(act, A.c_tr, s, 0)
        nc.scalar.activation(A.ct[0:A.E3, :], B7.bitcast(BF16)[0:A.E3, 0:W], ACT.Copy).then_inc(A.ct_ready.sem, 1)

    def weights_choice(dve, A, k, link):
        R = A.r
        link(one_hot(R, k))
        link(nc.vector.tensor_tensor(R.c if k == 0 else R.oh, R.oh, R.top[:, :, k:k + 1].broadcast_to([P, TB, R.E]), ALU.mult))
        if k:
            link(nc.vector.tensor_tensor(R.c, R.c, R.oh, ALU.add))

    def weights_split(dve, A, link):
        R = A.r
        link(nc.vector.tensor_copy(A.c3[:, :, 0, :], R.c))
        link(nc.vector.tensor_tensor(R.c, R.c, A.c3[:, :, 0, :], ALU.subtract))
        link(nc.vector.tensor_copy(A.c3[:, :, 1, :], R.c))
        link(nc.vector.tensor_tensor(R.c, R.c, A.c3[:, :, 1, :], ALU.subtract))
        nc.vector.tensor_copy(A.c3[:, :, 2, :], R.c).then_inc(A.c_ready.sem, 1)
        link.close()

    def dense_pe(pe, S, beside=None):
        A, s = S.A, S.s
        if S.new and not S.old:
            router_logits(pe, A.r, s)
            router_turn(pe, A.r, s)
        for m in S.steps:
            if S.new:
                w = A.width(m)
                for sig, wt, bank, freed in ((A.g_mm, A.wg, B4, A.sg_ready), (A.u_mm, A.wu, B5, A.su_ready)):
                    done(pe, freed, s, m - 1)
                    for k in range(KD):
                        last = mm(bank[0:w, :], wt[:, k, m * P:m * P + w], XNT[:, k, tok(s)], k == 0, k == KD - 1)
                    last.then_inc(sig.sem, 1)
            j = m - 1
            if S.has(j):
                w = A.width(j % A.m)
                done(pe, A.h_ready, s, j)
                if j == 0:
                    done(pe, yt_ready, S.n, 1)
                for k in range(KD):
                    last = mm(Y[k], A.wd[0:w, j % A.m, k * P:(k + 1) * P], A.h[0:w, j % A.m % 2, :], j == 0, j == -1)
                last.then_inc(A.y_mm.sem, 1)
            if m == 0 and S.new and not S.old:
                weights_turn(pe, A, s)
            if S.new and m < A.routed:
                done(pe, A.h_ready, s, m - 1)
                done(pe, A.ct_ready, s, 0)
                mm(B6, A.sel[0:A.E3, m * P:(m + 1) * P], A.ct[0:A.E3, :]).then_inc(A.w_mm.sem, 1)
            if S.ahead and m == 0:
                router_logits(pe, A.r, s + 1)
            if S.ahead and m == 1:
                router_turn(pe, A.r, s + 1)
            if S.ahead and m == A.m - 1:
                weights_turn(pe, A, s + 1)
            if S.new and m - DENSE_TAIL in (0, 1):
                tail_pe_y(pe, S.n, m - DENSE_TAIL)
            if S.new and m - DENSE_TAIL in (4, 5):
                tail_pe_xn(pe, S.n, m - DENSE_TAIL - 4)
            if beside is not None:
                beside(pe, S, m)

    def dense_act(act, S, beside=None):
        A, s = S.A, S.s

        def out_of_y(n):
            done(act, yt_tr, n - 1, 1)
            done(act, A.y_mm, s, -1)
            g = 4 + A.stage // 2
            for k in range(KD):
                nc.scalar.activation(YT[:, k, :], Y[k], ACT.Copy, scale=gates[:, g:g + 1]).then_inc(yt_ready.sem, 1)

        if S.new and not S.old:
            router_out(act, A.r, s)
            router_exp(act, A.r, s)
            weights_out(act, A, s)
        for m in S.steps:
            if beside is not None:
                beside(act, S, m)
            if S.new:
                w = A.width(m)
                done(act, A.g_mm, s, m)
                done(act, A.h_ready, s, dense_before(A, m))
                nc.scalar.activation(A.sg[0:w, m % 2, :], B4[0:w, :], ACT.Silu).then_inc(A.sg_ready.sem, 1)
            if m == 0 and S.old:
                out_of_y(S.n if S.new else tail_of(A.stage, s)[0])
            if S.ahead and m == 1:
                router_out(act, A.r, s + 1)
            if S.ahead and m == 3:
                router_exp(act, A.r, s + 1)
            if S.ahead and m == A.m - 1:
                done(act, A.w_mm, s, A.routed - 1)
                weights_out(act, A, s + 1)
            if S.new and m - DENSE_TAIL in (4, 5):
                tail_act(act, S.n, S.prev, m - DENSE_TAIL - 4)

    def dense_dve(dve, S, over_all, beside=None):
        A, s = S.A, S.s
        if S.new and not S.old:
            link = Chain(dve, A.r.chain, s)
            router_sub(dve, A.r, s, link)
            router_top(dve, A.r, s, link, over_all)
            for k in range(A.r.K):
                weights_choice(dve, A, k, link)
            weights_split(dve, A, link)
        if S.ahead:
            link = Chain(dve, A.r.chain, s + 1)
        for m in S.steps:
            if beside is not None:
                beside(dve, S, m)
            if S.new:
                w = A.width(m)
                done(dve, A.sg_ready, s, m)
                done(dve, A.u_mm, s, m)
                if m < A.routed:
                    nc.vector.tensor_tensor(A.sg[0:w, m % 2, :], A.sg[0:w, m % 2, :], B5[0:w, :], ALU.mult)\
                        .then_inc(A.su_ready.sem, 1)
                    done(dve, A.su_ready, s, m)
                    done(dve, A.w_mm, s, m)
                    done(dve, A.y_mm, s, dense_before(A, m))
                    nc.vector.tensor_tensor(A.h[0:w, m % 2, :], A.sg[0:w, m % 2, :], B6[0:w, :], ALU.mult).then_inc(A.h_ready.sem, 1)
                else:
                    done(dve, A.y_mm, s, dense_before(A, m))
                    nc.vector.tensor_tensor(A.h[0:w, m % 2, :], A.sg[0:w, m % 2, :], B5[0:w, :], ALU.mult)\
                        .then_inc(A.su_ready.sem, 1)
                    done(dve, A.su_ready, s, m)
                    dve.sem_inc(A.h_ready.sem, 1)
            if S.new and m - DENSE_TAIL in (0, 1):
                tail_dve_add(dve, S.n, S.prev, m - DENSE_TAIL)
            if S.new and m - DENSE_TAIL == 2:
                tail_dve_stats(dve, S.n, S.prev)
            if S.new and m - DENSE_TAIL == 3:
                tail_dve_norm(dve, S.n, S.prev)
            if S.ahead and m == 2:
                router_sub(dve, A.r, s + 1, link)
            if S.ahead and m == 6:
                router_top(dve, A.r, s + 1, link, over_all)
            if S.ahead and 7 <= m < 7 + A.r.K:
                weights_choice(dve, A, m - 7, link)
            if S.ahead and m == 7 + A.r.K:
                weights_split(dve, A, link)

    def dense_pool(pool, A, s):
        n, _ = tail_of(A.stage, s)
        tail_pool(pool, n)

    def make_sel(ordered, A, sel, tmp):
        for x in range(3):
            part = tmp.bitcast(BF16)[0:A.E3, 0:A.cols]
            ordered(nc.gpsimd.memset(part, 1.0))
            for sign, base in ((1, 0), (-1, A.ff - 1)):
                ordered(nc.gpsimd.affine_select(out=part, in_=part, compare_op=ALU.is_ge, fill=0.0,
                                                base=base + sign * A.ff * A.r.E * x, pattern=[[sign, A.cols]],
                                                channel_multiplier=-sign * A.ff))
            if x == 0:
                ordered(nc.gpsimd.tensor_copy(sel[0:A.E3, :], part))
            else:
                ordered(nc.gpsimd.tensor_tensor(out=sel[0:A.E3, :], in0=sel[0:A.E3, :], in1=part, op=ALU.add))

    L1E, L1F, L1K = 8, 176, 2
    l1_wr = tile(R2, 15616, KD * L1E).rearrange("p (k n) -> p k n", k=KD)
    l1_wg = tile(R2, 0, KD * L1E * L1F).rearrange("p (k n) -> p k n", k=KD)
    l1_wu = tile(R2, 2816, KD * L1E * L1F).rearrange("p (k n) -> p k n", k=KD)
    l1_wd = tile(R2, 6144, L1E * L1F * D // P).rearrange("p (m n) -> p m n", n=D)
    F1 = Dense("f1", 3, Router("f1", 3, L1E, L1K, l1_wr, WK, 0, (B3, B3)), L1F, 0, l1_wg, l1_wu, l1_wd, tile(R2, 15632, 704))
    in_l1f = semaphore("in_l1f")

    l2_wq = tile(R1, 0, 4096).rearrange("p (k n) -> p k n", k=KD)
    l2_wk = tile(R1, 4096, 2048)
    l2_wv = tile(R1, 6144, 2048)
    l2_wo = tile(R1, 8192, 4096).rearrange("p (h n) -> p h n", h=HEADS)
    in_l2x = semaphore("in_l2x")
    gqk_ready = semaphore("gqk_ready")
    L2 = Wide("a2", 4, 16, l2_wq, l2_wk, l2_wv, l2_wo, True)

    L2E, L2F, L2S, L2K = 16, 176, 352, 4
    L2C = L2E * L2F + L2S
    L2M = -(-L2C // P)
    l2_w1t = tile(R2, 0, KD * L2C).rearrange("p (k n) -> p k n", k=KD)
    l2_w3t = tile(R2, 6336, KD * L2C).rearrange("p (k n) -> p k n", k=KD)
    l2_w2t = tile(R2, 12672, L2M * D).rearrange("p (m n) -> p m n", n=D)
    l2_wr = tile(R2, 19072, KD * L2E).rearrange("p (k n) -> p k n", k=KD)
    l2_sel_made = tile(R2, 17408, 1408)
    l2_sel = tile(WK, 4700, 1408)
    F2 = Dense("f2", 5, Router("f2", 5, L2E, L2K, l2_wr, WK, 0, (B3, B3)), L2F, L2S, l2_w1t, l2_w3t, l2_w2t, l2_sel)
    RING = 8
    raw = tile(R1, 0, RING * 6 * P).rearrange("p (n c) -> p n c", n=RING)
    raw_in = [semaphore(f"raw_in{i}") for i in range(RING)]
    wr_raw = tile(R2, 18816, D)[0:16, :]
    wr_tr = signal("small_tr", 1, 1)
    wr_ready = signal("small_ready", 1, 1)
    sel_moved = semaphore("sel_moved")
    prep_tr = signal("prep_tr", L2M, 1)
    prep_act = signal("prep_act", L2M, 1)
    prep_dve = signal("prep_dve", L2M, 1)

    def chunk_dmas(m):
        w = F2.width(m)
        slot = raw[:, m % RING, :]
        halves = slot[:, 4 * P:6 * P].rearrange("p (h c) -> p h c", h=KD)
        routed = m < F2.routed
        r0 = m * P if routed else (m - F2.routed) * P
        for x, name in enumerate(("W1", "W3")):
            src = a["L2_ffn_" + name].rearrange("e f d -> (e f) d") if routed else a["L2_ffn_" + name + "s"]
            yield slot[0:w, x * D:(x + 1) * D], src[r0:r0 + w, :]
        if not routed:
            yield halves[:, :, 0:w], a["L2_ffn_W2s"][:, r0:r0 + w].rearrange("(h p) f -> p h f", p=P)
            return
        at = r0
        while at < r0 + w:
            e, f0 = divmod(at, L2F)
            n = min(L2F - f0, r0 + w - at)
            yield halves[:, :, at - r0:at - r0 + n], a["L2_ffn_W2"][e, :, f0:f0 + n].rearrange("(h p) f -> p h f", p=P)
            at += n

    def prep_sp(sp):
        sp.wait_ge(L2.y_mm.sem, L2.y_mm.value(NS - 1, HEADS - 1))
        for m in range(L2M):
            if m >= RING:
                sp.wait_ge(prep_tr.sem, prep_tr.value(0, m - RING))
            for dst, src in chunk_dmas(m):
                sp.dma_start(dst, src).then_inc(raw_in[m % RING], 16)

    PREP_LEAD = 3
    PREP_FIRST = 2 * PREP_LEAD

    def prep_chunk_pe(pe, m, bank13, bank2):
        w = F2.width(m)
        pe.wait_ge(raw_in[m % RING], sum(16 * len(list(chunk_dmas(i))) for i in range(m % RING, m + 1, RING)))
        slot = raw[:, m % RING, :]
        for j in range(4):
            nc.tensor.transpose(bank13[:, j * P:j * P + w], slot[0:w, j * P:(j + 1) * P], ident[0:w, 0:w])
        for j in range(KD):
            last = nc.tensor.transpose(bank2[0:w, j * P:(j + 1) * P], slot[:, (4 + j) * P:(4 + j) * P + w], ident[:])
        last.then_inc(prep_tr.sem, 1)

    def prep_chunk_act(act, m, bank13):
        w = F2.width(m)
        act.wait_ge(prep_tr.sem, prep_tr.value(0, m))
        bank = bank13.rearrange("p (x k c) -> p x k c", x=2, k=KD)
        nc.scalar.activation(l2_w1t[:, :, m * P:m * P + w], bank[:, 0, :, 0:w], ACT.Copy)
        nc.scalar.activation(l2_w3t[:, :, m * P:m * P + w], bank[:, 1, :, 0:w], ACT.Copy).then_inc(prep_act.sem, 1)

    def prep_chunk_dve(dve, m, bank2):
        w = F2.width(m)
        dve.wait_ge(prep_tr.sem, prep_tr.value(0, m))
        nc.vector.tensor_copy(l2_w2t[0:w, m, :], bank2[0:w, 0:D]).then_inc(prep_dve.sem, 1)

    def prep_pe(pe):
        for k in range(KD):
            last = nc.tensor.transpose(B4[:, k * L2E:(k + 1) * L2E], wr_raw[:, k * P:(k + 1) * P], ident[0:L2E, 0:L2E])
        last.then_inc(wr_tr.sem, 1)
        pe.wait_ge(wr_ready.sem, wr_ready.value(0, 0))
        for m in range(PREP_FIRST):
            if m >= 2:
                pe.wait_ge(prep_act.sem, prep_act.value(0, m - 2))
                pe.wait_ge(prep_dve.sem, prep_dve.value(0, m - 2))
            prep_chunk_pe(pe, m, (B4, B5)[m % 2], (B6, B7)[m % 2])
        pe.wait_ge(prep_act.sem, prep_act.value(0, PREP_FIRST - 1))
        pe.wait_ge(prep_dve.sem, prep_dve.value(0, PREP_FIRST - 1))

    def prep_act_engine(act):
        act.wait_ge(L2.y_mm.sem, L2.y_mm.value(NS - 1, HEADS - 1))
        act.wait_ge(pool_consts, 3)
        nc.scalar.activation(F2.sel[0:F2.E3, :], l2_sel_made.bitcast(BF16)[0:F2.E3, :], ACT.Copy).then_inc(sel_moved, 1)
        act.wait_ge(wr_tr.sem, wr_tr.value(0, 0))
        nc.scalar.activation(l2_wr.rearrange("p k n -> p (k n)"), B4[:, 0:KD * L2E], ACT.Copy).then_inc(wr_ready.sem, 1)
        for m in range(PREP_FIRST):
            prep_chunk_act(act, m, (B4, B5)[m % 2])

    def prep_dve_engine(dve):
        dve.wait_ge(sel_moved, 1)
        for m in range(PREP_FIRST):
            prep_chunk_dve(dve, m, (B6, B7)[m % 2])

    def prep_beside_pe(pe, S, m):
        c = m + PREP_LEAD
        if S.first and PREP_FIRST <= c < L2M:
            if c == PREP_FIRST:
                pe.wait_ge(F2.r.sub_ready.sem, F2.r.sub_ready.value(1, 0))
            else:
                pe.wait_ge(prep_act.sem, prep_act.value(0, c - 1))
                pe.wait_ge(prep_dve.sem, prep_dve.value(0, c - 1))
            prep_chunk_pe(pe, c, B7, B3)
        if S.first and PREP_FIRST <= m + 1 < L2M:
            pe.wait_ge(prep_act.sem, prep_act.value(0, m + 1))
            pe.wait_ge(prep_dve.sem, prep_dve.value(0, m + 1))

    def prep_beside_act(act, S, m):
        c = m - 1 + PREP_LEAD
        if S.first and PREP_FIRST <= c < L2M:
            prep_chunk_act(act, c, B7)

    def prep_beside_dve(dve, S, m):
        c = m - 1 + PREP_LEAD
        if S.first and PREP_FIRST <= c < L2M:
            prep_chunk_dve(dve, c, B3)

    L3H, L3HD = 16, 16
    MAIN = P - 16
    l3_wq = tile(R1, 0, 512).rearrange("p (k n) -> p k n", k=KD)
    l3_cat = tile(R1, 512, 512)
    l3_wm = tile(R1, 1024, 512)
    l3_wd = tile(R1, 1536, 512)
    l3_wo = tile(R1, 2048, 512).rearrange("p (k n) -> p k n", k=KD)
    l3_bqk = tile(R1, 2560, 512)
    vec_rows = tile(R1, 3072, P)
    l3_vec = tile(R1, 3200, 6)
    l3_bo = tile(R1, 3206, KD)
    l3_mean = tile(R1, 3210, 96)
    l3_bv = tile(R1, 3328, D)
    l3_x = tile(R1, 3840, 1024).rearrange("p (k c) -> p k c", k=KD)
    l3_cm = tile(R1, 4864, 512)
    l3_cd = tile(R1, 5376, 512)
    l3_qk = tile(R1, 5888, 2048).rearrange("p (b c) -> p b c", b=TB)
    l3_sq = [tile(x, o, W) for x, o in ((R1, 7936), (R1, 7936 + W), (WK, 5120), (WK, 5120 + W))]
    l3_b1 = tile(R1, 7936, D)
    l3_b2 = tile(R1, 7936 + D, D)
    l3_q = tile(R1, 8960, 1024).rearrange("p (k c) -> p k c", k=KD)
    l3_k = tile(R1, 9984, 1024).rearrange("p (k c) -> p k c", k=KD)
    l3_ot = tile(R1, 11008, 1024).rearrange("p (k c) -> p k c", k=KD)
    l3_var = tile(R1, 12032, 128).rearrange("p (b g) -> p b g", b=TB)
    l3_r = tile(R1, 12160, 128).rearrange("p (b g) -> p b g", b=TB)
    l3_v = tile(R2, 0, TB * KD * 2 * P).rearrange("p (t h r c) -> p t h r c", t=TB, h=KD, r=2)
    l3_zero_row = tile(R1, 5888, D)
    in_l3x = semaphore("in_l3x")
    vec_tr = signal("small_tr", 1, 1)
    vec_ready = signal("small_ready", 2, 1)
    L3 = Narrow("a3", 6, L3H, MAIN, l3_wo, l3_bo, 1)
    l3_qk_ready = signal("l3_qk_ready", TB)
    L3.needs_qk[0] = (l3_qk_ready, TB - 1)
    l3_w = signal("l3_w_ready", 4, 1)
    l3_in = signal("narrow_in_ready", 1)
    l3_qk_mm = signal("l3_qk_mm", TB)
    l3_v_mm = signal("narrow_v_mm", TB)
    l3_v_ready = signal("l3_v_ready", TB)
    l3_add = signal("l3_add", TB)
    l3_sq_ready = signal("l3_sq_ready", TB)
    l3_chain = signal("narrow_qk_chain", 2)
    l3_var_ready = signal("l3_var_ready", 1)
    l3_sd_ready = signal("l3_sd_ready", 1)
    l3_n_ready = signal("l3_n_ready", TB)
    l3_tr = signal("l3_tr", TB)
    xs = nc.dram_tensor("xn_rows", ((B + 1) * P, D), F32, kind="Internal").ap()
    xs_rows = xs.rearrange("(b p) d -> p b d", p=P)
    L3_LOADS = 18

    def l3_loads(sp):
        sp.wait_ge(prep_tr.sem, prep_tr.value(0, L2M - 1))
        w = "L3_xattn_"
        count = 0

        def load(dst, src):
            nonlocal count
            sp.dma_start(dst, src).then_inc(in_l3x, 16)
            count += 1

        load(l3_wq, a[w + "Wq"].rearrange("(k p) n -> p k n", p=P))
        load(l3_cat[:, 0:D], a[w + "Wk"])
        load(l3_cat[:, D:2 * D], a[w + "Wv"])
        load(l3_wd, a[w + "Wkv_dca"])
        load(l3_wo, a[w + "Wo"].rearrange("(k p) n -> p k n", p=P))
        load(l3_bo, a[w + "bo"].rearrange("(k p) -> p k", p=P))
        for j, name in enumerate(("qn_w", "qn_b", "kn_w", "kn_b", "kn_dca_w", "kn_dca_b")):
            load(vec_rows[j:j + 1, :].rearrange("p (g d) -> p g d", d=L3HD),
                 a[w + name].rearrange("(o u d) -> o u d", o=1, u=1).broadcast_to([1, P // L3HD, L3HD]))
        load(l3_bqk[:, 0:D], a[w + "bq"].rearrange("(o n) -> o n", o=1).broadcast_to([P, D]))
        dca = a[w + "bkv_dca"].rearrange("(o x n) -> o x n", o=1, x=2)
        load(l3_bqk[MAIN:P, D:2 * D], dca[:, 0, :].broadcast_to([P - MAIN, D]))
        load(l3_bv[MAIN:P, :], dca[:, 1, :].broadcast_to([P - MAIN, D]))
        load(l3_b1[0:MAIN, :], a[w + "bk"].rearrange("(o n) -> o n", o=1).broadcast_to([MAIN, D]))
        load(l3_b2[0:MAIN, :], a[w + "bv"].rearrange("(o n) -> o n", o=1).broadcast_to([MAIN, D]))
        assert count == L3_LOADS - 1

    def l3_store(sp, n, s, prev):
        done(sp, xn_ready, n, 0)
        sp.dma_start(xs_rows[:, bass.ds(prev * TB, TB), :], XN[:]).then_inc(xs_stored.sem, 16)

    def l3_setup_pe(pe):
        pe.wait_ge(in_l3x, 16 * (L3_LOADS - 1))
        nc.tensor.transpose(B7[:, 0:6], vec_rows[0:6, :], ident[0:6, 0:6]).then_inc(vec_tr.sem, 1)

    def l3_setup_act(act):
        act.wait_ge(in_l3x, 16 * (L3_LOADS - 1))
        act.wait_ge(vec_tr.sem, vec_tr.value(0, 0))
        nc.scalar.activation(l3_vec, B7[:, 0:6], ACT.Copy).then_inc(vec_ready.sem, 1)
        nc.scalar.activation(l3_bo, l3_bo, ACT.Copy, scale=gates[:, 3:4]).then_inc(vec_ready.sem, 1)

    def l3_setup_dve(dve):
        dve.wait_ge(in_l3x, 16 * (L3_LOADS - 1))
        dve.wait_ge(pool_consts, 4)
        link = Chain(dve, l3_w, 0)
        half = L3H // 2
        for x, dst in ((0, l3_bqk[0:MAIN, D:2 * D]), (1, l3_bv[0:MAIN, :])):
            for src, h0 in ((l3_b1, 0), (l3_b2, half)):
                ins = nc.vector.tensor_copy(dst.rearrange("p (h d) -> p h d", d=L3HD)[:, h0:h0 + half, :],
                                            src[0:MAIN, :].rearrange("p (h x d) -> p h x d", x=2, d=L3HD)[:, :, x, :])
        ins = nc.vector.tensor_copy(l3_wm.rearrange("p (x h d) -> p h x d", x=2, d=L3HD), l3_cat.rearrange("p (h x d) -> p h x d", x=2, d=L3HD))
        link(ins)
        centred = (l3_wq.rearrange("p k n -> p (k n)"), l3_wm[:, 0:D], l3_wd[:, 0:D], l3_bqk)
        heads = [(t.rearrange("p (g d) -> p g d", d=L3HD), t.shape[1] // L3HD) for t in centred]
        at = 0
        for g, c in heads:
            ins = nc.vector.tensor_reduce(l3_mean[:, at:at + c], g, AX.X, ALU.add)
            at += c
        link(ins)
        link(nc.vector.tensor_scalar(l3_mean, l3_mean, 1.0 / L3HD, None, ALU.mult))
        at = 0
        for g, c in heads:
            ins = nc.vector.tensor_tensor(g, g, l3_mean[:, at:at + c].unsqueeze(2).broadcast_to([P, c, L3HD]), ALU.subtract)
            at += c
        link(ins)
        link.close()

    def l3_setup_pool(pool):
        pool.wait_ge(prep_tr.sem, prep_tr.value(0, L2M - 1))
        pool.wait_ge(F2.y_mm.sem, F2.y_mm.value(NS - 1, F2.m - 1))
        nc.gpsimd.memset(l3_v, 0.0).then_inc(pool_consts, 1)
        nc.gpsimd.memset(l3_zero_row, 0.0).then_inc(pool_consts, 1)
        nc.gpsimd.memset(l3_cm.rearrange("p (b k) -> p b k", b=TB)[:, :, MAIN:P], 0.0)
        nc.gpsimd.memset(l3_cd.rearrange("p (b k) -> p b k", b=TB)[:, :, 0:MAIN], 0.0)

    L3_BANKS = (B3, B5, B4, TP)
    L3.needs_v[0] = (l3_v_ready, TB - 1)

    def l3_qk_pe(pe, s, b):
        c = slice(b * P, (b + 1) * P)
        bank = L3_BANKS[b]
        for k in range(KD):
            mm(bank[:, 0:D], l3_x[:, k, c], l3_wq[:, k, :], k == 0, k == KD - 1)
        mm(bank[:, D:2 * D], l3_cm[:, c], l3_wm[:, 0:D], True, False)
        mm(bank[:, D:2 * D], l3_cd[:, c], l3_wd[:, 0:D], False, True).then_inc(l3_qk_mm.sem, 1)

    def l3_v_pe(pe, s, b):
        c = slice(b * P, (b + 1) * P)
        v = Y[0][:, b % 2 * D:(b % 2 + 1) * D]
        mm(v, l3_cm[:, c], l3_wm[:, D:2 * D], True, False)
        mm(v, l3_cd[:, c], l3_wd[:, D:2 * D], False, True).then_inc(l3_v_mm.sem, 1)

    def l3_turn_pe(pe, s, b):
        done(pe, l3_n_ready, s, b)
        for j in range(4):
            last = nc.tensor.transpose(L3_BANKS[b][:, j * P:(j + 1) * P], l3_qk[:, b, j * P:(j + 1) * P], ident[:])
        last.then_inc(l3_tr.sem, 1)

    def l3_square_act(act, s, b):
        done(act, l3_add, s, b)
        nc.scalar.activation(l3_sq[b], l3_qk[:, b, :], ACT.Square).then_inc(l3_sq_ready.sem, 1)

    def l3_root_act(act, s):
        done(act, l3_var_ready, s, 0)
        nc.scalar.activation(l3_r, l3_var, ACT.Sqrt).then_inc(l3_sd_ready.sem, 1)

    def l3_out_act(act, s, b):
        done(act, l3_tr, s, b)
        bank = L3_BANKS[b].rearrange("p (x k c) -> p x k c", x=2, k=KD)
        for dst, x, lo, hi, j in ((l3_q, 0, 0, P, 0), (l3_k, 1, 0, MAIN, 2), (l3_k, 1, MAIN, P, 4)):
            last = nc.scalar.activation(dst[:, :, b * P + lo:b * P + hi], bank[:, x, :, lo:hi], ACT.Identity,
                                        scale=l3_vec[:, j:j + 1], bias=l3_vec[:, j + 1:j + 2])
        last.then_inc(l3_qk_ready.sem, 1)

    def l3_add_dve(dve, s, b):
        done(dve, l3_qk_mm, s, b)
        nc.vector.tensor_tensor(l3_qk[:, b, :], L3_BANKS[b], l3_bqk, ALU.add).then_inc(l3_add.sem, 1)

    def l3_square_dve(dve, s, b):
        done(dve, l3_sq_ready, s, b)
        return nc.vector.tensor_reduce(l3_var[:, b, :], l3_sq[b].rearrange("p (g d) -> p g d", d=L3HD), AX.X, ALU.add)

    def l3_var_dve(dve, s, last):
        Chain(dve, l3_chain, s)(last)
        nc.vector.tensor_scalar(l3_var, l3_var, 1.0 / L3HD, LN3_EPS, ALU.mult, ALU.add).then_inc(l3_var_ready.sem, 1)

    def l3_norm_dve(dve, s):
        done(dve, l3_sd_ready, s, 0)
        Chain(dve, l3_chain, s, 1)(nc.vector.reciprocal(l3_r, l3_r))
        for b in range(TB):
            g = l3_qk[:, b, :].rearrange("p (g d) -> p g d", d=L3HD)
            nc.vector.tensor_tensor(g, g, l3_r[:, b, :].unsqueeze(2).broadcast_to([P, 32, L3HD]), ALU.mult)\
                .then_inc(l3_n_ready.sem, 1)

    def l3_v_dve(dve, s, b, first):
        done(dve, l3_v_mm, s, b // 2 * 2 + 1)
        if not first:
            done(dve, L3.o_mm, s, (b + 1) * L3.groups - L3.n - 1)
        v = Y[0][:, b % 2 * D:(b % 2 + 1) * D].rearrange("p (h r c) -> p h r c", h=KD, r=2)
        for r in range(2):
            c = slice(r * P // 2, (r + 1) * P // 2)
            bias = l3_bv.rearrange("p (h r c) -> p h r c", h=KD, r=2)[:, :, r, :]
            last = nc.vector.tensor_tensor(l3_v[:, b, :, r, c], v[:, :, r, :], bias, ALU.add)
        last.then_inc(l3_v_ready.sem, 1)

    def l3_start_pe(pe):
        done(pe, l3_in, 0, 0)
        done(pe, yt_ready, tail_of(L3.stage, 0)[0], 1)
        for b in range(TB):
            l3_qk_pe(pe, 0, b)
        for b in range(TB):
            if b == 2:
                done(pe, l3_v_ready, 0, 1)
            l3_v_pe(pe, 0, b)
        for b in range(TB):
            l3_turn_pe(pe, 0, b)

    def l3_start_act(act):
        for b in range(TB):
            l3_square_act(act, 0, b)
        l3_root_act(act, 0)
        for b in range(TB):
            l3_out_act(act, 0, b)

    def l3_start_dve(dve):
        dve.wait_ge(xs_stored.sem, 16)
        for b in range(TB):
            l3_add_dve(dve, 0, b)
        for b in range(2):
            l3_v_dve(dve, 0, b, True)
        for b in range(TB):
            last = l3_square_dve(dve, 0, b)
        l3_var_dve(dve, 0, last)
        for b in range(2, TB):
            l3_v_dve(dve, 0, b, True)
        l3_norm_dve(dve, 0)

    def l3_end_pe(pe, S, t, route):
        x = S.s
        if t == 0:
            done(pe, l3_in, x, 0)
            done(pe, L3.p_ready, x, -1)
        if t in (0, 1):
            if t == 1:
                done(pe, xnt_ready, tail_of(L3.stage, x)[0] - 1, 1)
            l3_qk_pe(pe, x, 2 * t)
            l3_qk_pe(pe, x, 2 * t + 1)
        if t == 3:
            if route:
                done(pe, f3_map_ready, x - 2, 0)
            for b in range(2):
                l3_v_pe(pe, x, b)
        if t == N_END - 1:
            done(pe, l3_v_ready, x, 1)
            for b in range(2, TB):
                l3_v_pe(pe, x, b)
            for b in range(TB):
                l3_turn_pe(pe, x, b)
            done(pe, l3_v_ready, x, TB - 1)

    def l3_end_act(act, S, t):
        if t in (1, 2):
            for b in (2 * t - 2, 2 * t - 1):
                l3_square_act(act, S.s, b)
        if t == 4:
            l3_root_act(act, S.s)
        if t == N_END - 1:
            for b in range(TB):
                l3_out_act(act, S.s, b)

    def l3_end_dve(dve, S, t):
        if t in (1, 2):
            for b in (2 * t - 2, 2 * t - 1):
                l3_add_dve(dve, S.s, b)
        if t in (2, 3):
            for b in (2 * t - 4, 2 * t - 3):
                last = l3_square_dve(dve, S.s, b)
            if t == 3:
                l3_var_dve(dve, S.s, last)
        if t == 4:
            for b in range(2):
                l3_v_dve(dve, S.s, b, False)
        if t == N_END - 1:
            l3_norm_dve(dve, S.s)
            for b in range(2, TB):
                l3_v_dve(dve, S.s, b, False)

    def l3_body(narrow, s, beside):
        narrow(Body(L3, s, old=False), beside)
        narrow(Body(L3, s + 1, new=False), beside)

    def l3_copies(pool, s):
        c = CTXT[:, tok(s)].rearrange("p (b k) -> p b k", b=TB)
        nc.gpsimd.tensor_copy(l3_cm.rearrange("p (b k) -> p b k", b=TB)[:, :, 0:MAIN], c[:, :, 0:MAIN])
        nc.gpsimd.tensor_copy(l3_cd.rearrange("p (b k) -> p b k", b=TB)[:, :, MAIN:P], c[:, :, MAIN:P])
        nc.gpsimd.tensor_copy(l3_x, XNT[:, :, tok(s)]).then_inc(l3_in.sem, 1)

    L3E, L3F, L3K = 64, 96, 8
    SLOTS = P * L3E
    AHEAD = 6
    XR = 8
    YR = 4
    GE = 16
    NG = L3E // GE
    QE = 4
    at = TB * KD * 2 * P

    def room(n, dt=F32):
        nonlocal at
        at += n
        return tile(R2, at - n, n).bitcast(dt) if dt != F32 else tile(R2, at - n, n)

    f3_wr = room(KD * L3E).rearrange("p (k n) -> p k n", k=KD)
    R3 = Router("f3", 7, L3E, L3K, f3_wr, R2, at, (Y[0], Y[0]))
    at = R3.end
    R3.chain = signal("moe_r_chain", 6 + 6)
    f3_oh = room(TB * L3K * L3E).rearrange("p (t k e) -> p t k e", t=TB, k=L3K)
    f3_map = room(TB * L3E).rearrange("p (t e) -> p t e", t=TB)
    f3_m = room(TB * L3E // 2, BF16).rearrange("p (t e) -> p t e", t=TB)
    f3_carry = room(L3E // 2, BF16)
    f3_msum = room(L3E)
    f3_slot = room(TB * L3K).rearrange("p (t k) -> p t k", t=TB)
    f3_slot_u = room(TB * L3K, U32).rearrange("p (t k) -> p t k", t=TB)
    f3_pay = room(TB * L3K * 2).rearrange("p (t k x) -> p t k x", t=TB, x=2)
    f3_pay_i = f3_pay.bitcast(I32)
    f3_before = room(P // 2, BF16)
    f3_ones = room(P // 2, BF16)
    f3_wr_raw = room(D)[0:L3E, :]
    f3_ids = room(B, I32)
    f3_tab = room((L3E + AHEAD) * 2).rearrange("p (e x) -> p e x", x=2)
    f3_tab_i = f3_tab.bitcast(I32)
    f3_idx_g = room(GE, U32)
    f3_idx_s = room(GE, U32)
    f3_wt = room(GE)
    f3_zero = room(D)
    f3_gu = room(GE * KD * 2 * L3F).rearrange("p (e k n) -> p e k n", e=GE, k=KD)
    f3_dn = room(GE * D).rearrange("p (e n) -> p e n", e=GE)[0:L3F]
    assert at <= 19200
    f3_xe = tile(WK, 0, XR * D).rearrange("p (n d) -> p n d", n=XR)
    f3_xt = tile(WK, 2048, 512).rearrange("p (n k c) -> p n k c", n=2, k=KD)
    f3_sg = tile(WK, 2560, 256).rearrange("p (n c) -> p n c", n=2)
    f3_h = tile(WK, 2816, 256).rearrange("p (n c) -> p n c", n=2)
    f3_y = tile(WK, 3072, YR * D).rearrange("p (n d) -> p n d", n=YR)
    f3_sum = [tile(R1, i * B * D, B * D).rearrange("p (b d) -> p b d", b=B) for i in range(2)]
    table = nc.dram_tensor("slots", (SLOTS, 2), F32, kind="Internal").ap()
    table_rows = table.rearrange("(p e) x -> p e x", e=L3E)
    acc = [nc.dram_tensor(f"moe_sum{i}", ((B + 1) * P, D), F32, kind="Internal").ap() for i in range(2)]
    in_f3r = semaphore("in_f3r")
    f3_wr_tr = signal("small_tr", 1, 1)
    f3_wr_ready = signal("small_ready", 1, 1)
    f3_made = semaphore("f3_made")
    f3_m_ready = signal("f3_m_ready", 1)
    f3_map_ready = signal("f3_map_ready", 1)
    f3_pos = Y[0][:, TB * L3E:2 * TB * L3E]
    ROUTE_END = L3.n + N_END - 1
    f3_pos_mm = signal("f3_pos_mm", 1)
    f3_slots_ready = signal("f3_slots_ready", 1)
    tab_written = Signal(semaphore("tab_written"), 16 * TB * L3K, NS, 16)
    tab_read = semaphore("tab_read")
    f3_idx_ready = signal("f3_idx_ready", 1, NG)
    f3_w_in = [Signal(semaphore(f"f3_w_in{i}"), 32, NG, 0) for i in range(GE // QE)]
    f3_gathered = [Signal(semaphore(f"f3_gathered{i}"), 16 * GE // XR, NG, 0) for i in range(XR)]
    f3_added = [Signal(semaphore(f"f3_added{i}"), 16 * GE // 2, NG, 16) for i in range(2)]
    f3_xt_tr = signal("f3_xt_tr", GE, NG)
    f3_xt_ready = signal("f3_xt_ready", GE, NG)
    f3_gu_mm = signal("moe_g_mm", GE, NG)
    f3_sg_ready = signal("moe_sg_ready", GE, NG)
    f3_h_ready = signal("moe_h_ready", GE, NG)
    f3_y_mm = signal("moe_y_mm", GE, NG)
    f3_y_ready = signal("f3_y_ready", GE, NG)
    sum_in = [semaphore(f"sum_in{i}") for i in range(NS)]
    x_done = semaphore("x_done")
    sum_chain = semaphore("sum_chain")

    def f3_weights(sp, g, q):
        es = bass.ds(g * GE + q * QE, QE)
        sp.dma_start(f3_gu[:, q * QE:(q + 1) * QE], a["L3_ffn_gate_up_proj"][es].rearrange("e (k p) n -> p e k n", p=P))\
            .then_inc(f3_w_in[q].sem, 16)
        sp.dma_start(f3_dn[:, q * QE:(q + 1) * QE], a["L3_ffn_down_proj"][es].rearrange("e f d -> f e d"))\
            .then_inc(f3_w_in[q].sem, 16)

    def f3_loads(sp):
        sp.wait_ge(F2.y_mm.sem, F2.y_mm.value(NS - 1, F2.m - 1))
        sp.dma_start(f3_wr_raw, a["L3_ffn_router_weight"]).then_inc(in_f3r, 16)
        for q in range(GE // QE):
            f3_weights(sp, 0, q)

    def f3_sp(sp):
        l3_store(sp, NS * 7 + NS - 1, 0, NS - 1)
        sp.wait_ge(tab_written.sem, tab_written.end)
        sp.dma_start(f3_tab[:, 0:L3E, :], table_rows).then_inc(tab_read, 16)
        with sp.Fori(1, NG, 1) as g:
            for q in range(GE // QE):
                done(sp, f3_y_mm, g - 1, (q + 1) * QE - 1)
                f3_weights(sp, g, q)
        for i in range(2):
            sp.wait_ge(f3_added[i].sem, f3_added[i].end)
        for j in range(NS):
            b = slice(j * TB, (j + 1) * TB)
            for i in range(2):
                sp.dma_start(f3_sum[i][:, b], acc[i].rearrange("(b p) d -> p b d", p=P)[:, b]).then_inc(sum_in[j], 16)
        for j in range(NS):
            b = slice(j * TB, (j + 1) * TB)
            sp.wait_ge(x_done, j + 1)
            sp.dma_start(out.rearrange("b p d -> p b d")[:, b], X[:, b]).then_inc(out_done, 16)
        sp.wait_ge(out_done, 16 * NS)

    def f3_setup_pool(pool):
        made = 0

        def ordered(ins):
            nonlocal made
            made += 1
            ins.then_inc(f3_made, 1)
            pool.wait_ge(f3_made, made)

        nc.gpsimd.iota(f3_tab_i[:, :, 0], pattern=[[0, L3E + AHEAD]], base=B * P, channel_multiplier=1)
        nc.gpsimd.memset(f3_tab[:, :, 1], 0.0)
        ordered(nc.gpsimd.memset(f3_zero, 0.0))
        pool.dma_start(table_rows, f3_tab[:, 0:L3E, :]).then_inc(tab_written.sem, 16)
        for i in range(2):
            pool.dma_start(acc[i].rearrange("(b p) d -> p b d", p=P), f3_zero.unsqueeze(1).broadcast_to([P, B + 1, D]))\
                .then_inc(f3_added[i].sem, 16)
        nc.gpsimd.iota(f3_ids, pattern=[[P, B]], base=0, channel_multiplier=1)
        nc.gpsimd.memset(f3_carry, 0.0)
        nc.gpsimd.memset(f3_ones, 1.0)
        ordered(nc.gpsimd.memset(f3_before, 1.0))
        ordered(nc.gpsimd.affine_select(out=f3_before, in_=f3_before, compare_op=ALU.is_ge, fill=0.0, base=-1, pattern=[[1, P]],
                                        channel_multiplier=-1))
        pool.sem_inc(pool_consts, 1)

    def f3_route_pool(pool, s, start=0, end=TB * L3K):
        if start == 0:
            done(pool, f3_slots_ready, s, 0)
            done(pool, tab_written, s, -1)
        for i in range(start, end):
            t, k = divmod(i, L3K)
            nc.gpsimd.indirect_dma_start(table, bass.IndirectOffsetOnAxis(ap=f3_slot_u[:, t, k:k + 1], axis=0),
                                         f3_pay[:, t, k, :], None, bounds_check=SLOTS - 1, oob_is_err=False)\
                .then_inc(tab_written.sem, 16)

    def f3_setup_pe(pe):
        pe.wait_ge(in_f3r, 16)
        for k in range(KD):
            last = nc.tensor.transpose(B7[:, k * L3E:(k + 1) * L3E], f3_wr_raw[:, k * P:(k + 1) * P], ident[0:L3E, 0:L3E])
        last.then_inc(f3_wr_tr.sem, 1)
        pe.wait_ge(f3_wr_ready.sem, f3_wr_ready.value(0, 0))
        pe.wait_ge(pool_consts, 6)

    def f3_setup_act(act):
        act.wait_ge(f3_wr_tr.sem, f3_wr_tr.value(0, 0))
        nc.scalar.activation(f3_wr.rearrange("p k n -> p (k n)"), B7[:, 0:KD * L3E], ACT.Copy).then_inc(f3_wr_ready.sem, 1)

    def f3_places(pe, r):
        done(pe, f3_m_ready, r, 0)
        for t in range(TB):
            pos = f3_pos[:, t * L3E:(t + 1) * L3E]
            mm(pos, f3_ones, f3_carry, True, False)
            for u in range(t):
                mm(pos, f3_ones, f3_m[:, u, :], False, False)
            last = mm(pos, f3_before, f3_m[:, t, :], False, True)
        last.then_inc(f3_pos_mm.sem, 1)

    def f3_route_pe(pe, r, t):
        if t == 7:
            router_logits(pe, R3, r)
        if t == 8:
            router_turn(pe, R3, r)
        if t == 13:
            f3_places(pe, r)
        if t == ROUTE_END:
            done(pe, f3_map_ready, r, 0)

    def f3_route_act(act, r, t):
        if t == 7:
            router_out(act, R3, r)
        if t == 10:
            router_exp(act, R3, r)

    def f3_choices(dve, r, link):
        link(nc.vector.tensor_tensor(f3_oh.rearrange("p t k e -> p (t k) e"), iota[:].unsqueeze(1).broadcast_to([P, TB * L3K, L3E]),
                                     R3.ixf.rearrange("p t k -> p (t k)").unsqueeze(2).broadcast_to([P, TB * L3K, L3E]), ALU.is_equal))
        with nc.allow_low_precision(reason="whole numbers up to 8"):
            nc.vector.tensor_reduce(f3_m, f3_oh.rearrange("p t k e -> p t e k"), AX.X, ALU.add).then_inc(f3_m_ready.sem, 1)

    def f3_slots(dve, r, link):
        done(dve, tab_written, r, -1)
        nc.vector.tensor_copy(f3_pay_i[:, :, :, 0], f3_ids[:, bass.ds(r * TB, TB)].unsqueeze(2).broadcast_to([P, TB, L3K]))
        nc.vector.tensor_copy(f3_pay[:, :, :, 1], R3.top)
        done(dve, f3_pos_mm, r, 0)
        link(nc.vector.scalar_tensor_tensor(f3_map, f3_pos.rearrange("p (t e) -> p t e", t=TB), float(L3E),
                                            iota[:].unsqueeze(1).broadcast_to([P, TB, L3E]), ALU.mult, ALU.add))
        dve.sem_inc(f3_map_ready.sem, 1)
        link(nc.vector.tensor_reduce(f3_msum, f3_m.rearrange("p t e -> p e t"), AX.X, ALU.add))
        nc.vector.tensor_tensor(f3_carry, f3_carry, f3_msum, ALU.add)
        link(nc.vector.tensor_tensor(f3_oh, f3_oh, f3_map.unsqueeze(2).broadcast_to([P, TB, L3K, L3E]), ALU.mult))
        link(nc.vector.tensor_reduce(f3_slot, f3_oh, AX.X, ALU.add))
        link(nc.vector.tensor_copy(f3_slot_u, f3_slot))
        dve.sem_inc(f3_slots_ready.sem, 1)

    def f3_route_dve(dve, r, t, link):
        if t == 9:
            router_sub(dve, R3, r, link)
        if t == 11:
            router_top(dve, R3, r, link, False)
        if t == 12:
            f3_choices(dve, r, link)
        if t == 14:
            f3_slots(dve, r, link)
            link.close()

    def f3_pool_start(pool):
        pool.wait_ge(tab_read, 16)
        pool.wait_ge(xs_stored.sem, 16 * (1 + NS + 1))
        nc.gpsimd.tensor_copy(f3_idx_g[:, 0:AHEAD], f3_tab_i.bitcast(U32)[:, 0:AHEAD, 0]).then_inc(f3_made, 1)
        pool.wait_ge(f3_made, 4)
        for j in range(AHEAD):
            nc.gpsimd.indirect_dma_start(f3_xe[:, j % XR, :], None, xs, bass.IndirectOffsetOnAxis(ap=f3_idx_g[:, j:j + 1], axis=0))\
                .then_inc(f3_gathered[j % XR].sem, 16)

    def f3_pool(pool, g):
        done(pool, f3_gathered[(AHEAD - 1) % XR], g, 15)
        done(pool, f3_added[0], g, -1)
        done(pool, f3_added[1], g, -1)
        tab = f3_tab_i.bitcast(U32)
        nc.gpsimd.tensor_copy(f3_idx_g, tab[:, bass.ds(g * GE + AHEAD, GE), 0])
        nc.gpsimd.tensor_copy(f3_idx_s, tab[:, bass.ds(g * GE, GE), 0])
        nc.gpsimd.tensor_copy(f3_wt, f3_tab[:, bass.ds(g * GE, GE), 1]).then_inc(f3_idx_ready.sem, 1)
        done(pool, f3_idx_ready, g, 0)
        for j in range(GE):
            r = (j + AHEAD) % XR
            done(pool, f3_xt_tr, g, j + AHEAD - XR)
            nc.gpsimd.indirect_dma_start(f3_xe[:, r, :], None, xs, bass.IndirectOffsetOnAxis(ap=f3_idx_g[:, j:j + 1], axis=0))\
                .then_inc(f3_gathered[r].sem, 16)
            done(pool, f3_y_ready, g, j)
            done(pool, f3_added[j % 2], g, 16 * (j // 2) - 1)
            nc.gpsimd.indirect_dma_start(acc[j % 2], bass.IndirectOffsetOnAxis(ap=f3_idx_s[:, j:j + 1], axis=0), f3_y[:, j % YR, :], None,
                                         bounds_check=(B + 1) * P - 1, compute_op=ALU.add).then_inc(f3_added[j % 2].sem, 16)

    def f3_pe(pe, g):
        for j in range(GE + 3):
            if j < GE:
                done(pe, f3_gathered[j % XR], g, 16 * (j // XR) + 15)
                done(pe, f3_xt_ready, g, j - 2 if j >= 2 else -1)
                for k in range(KD):
                    last = nc.tensor.transpose(PS[:, j % 2, k * P:(k + 1) * P], f3_xe[:, j % XR, k * P:(k + 1) * P], ident[:])
                last.then_inc(f3_xt_tr.sem, 1)
            if j >= 3:
                e = j - 3
                done(pe, f3_h_ready, g, e)
                done(pe, f3_y_ready, g, e - 2 if e >= 2 else -1)
                mm(PS[:, 4 + e % 2, 0:D], f3_h[0:L3F, e % 2, :], f3_dn[:, e, :]).then_inc(f3_y_mm.sem, 1)
            if 1 <= j <= GE:
                e = j - 1
                done(pe, f3_xt_ready, g, e)
                if e % QE == 0:
                    done(pe, f3_w_in[e // QE], g, 31)
                done(pe, f3_h_ready, g, e - 2 if e >= 2 else -1)
                for x in range(2):
                    for k in range(KD):
                        last = mm(PS[0:L3F, 2 + e % 2, x * P:(x + 1) * P], f3_gu[:, e, k, x * L3F:(x + 1) * L3F], f3_xt[:, e % 2, k, :],
                                  k == 0, k == KD - 1)
                last.then_inc(f3_gu_mm.sem, 1)

    def f3_act(act, g):
        for j in range(GE + 1):
            if j < GE:
                done(act, f3_xt_tr, g, j)
                done(act, f3_gu_mm, g, j - 2 if j >= 2 else -1)
                nc.scalar.activation(f3_xt[:, j % 2, :, :].rearrange("p k c -> p (k c)"), PS[:, j % 2, 0:D], ACT.Copy)\
                    .then_inc(f3_xt_ready.sem, 1)
            if j >= 1:
                e = j - 1
                done(act, f3_gu_mm, g, e)
                done(act, f3_h_ready, g, e - 2 if e >= 2 else -1)
                nc.scalar.activation(f3_sg[0:L3F, e % 2, :], PS[0:L3F, 2 + e % 2, 0:P], ACT.Silu).then_inc(f3_sg_ready.sem, 1)

    def f3_dve(dve, g):
        done(dve, f3_idx_ready, g, 0)
        for j in range(GE + 2):
            if j < GE:
                done(dve, f3_sg_ready, g, j)
                done(dve, f3_y_mm, g, j - 2 if j >= 2 else -1)
                nc.vector.tensor_tensor(f3_h[0:L3F, j % 2, :], f3_sg[0:L3F, j % 2, :], PS[0:L3F, 2 + j % 2, P:2 * P], ALU.mult)\
                    .then_inc(f3_h_ready.sem, 1)
            if j >= 2:
                e = j - 2
                done(dve, f3_y_mm, g, e)
                done(dve, f3_added[e % 2], g, max(16 * ((e - YR) // 2 + 1) - 1, -1))
                nc.vector.tensor_scalar(f3_y[:, e % YR, :], PS[:, 4 + e % 2, 0:D], f3_wt[:, e:e + 1], None, ALU.mult)\
                    .then_inc(f3_y_ready.sem, 1)

    def f3_end_dve(dve):
        for j in range(NS):
            b = slice(j * TB, (j + 1) * TB)
            dve.wait_ge(sum_in[j], 32)
            nc.vector.tensor_tensor(f3_sum[0][:, b], f3_sum[0][:, b], f3_sum[1][:, b], ALU.add).then_inc(sum_chain, 1)
            dve.wait_ge(sum_chain, j + 1)
            nc.vector.scalar_tensor_tensor(X[:, b], f3_sum[0][:, b], gates[:, 7:8], X[:, b], ALU.mult, ALU.add).then_inc(x_done, 1)

    block = ctx.enter_context(nc.Block())
    n_tails = NS - 1 + NS * 7 + 1

    @block.sync
    def _(sp):
        ctx.enter_context(nc.allow_non_contiguous_dma(reason="a few vectors that go one element to a partition"))
        sp.dma_start(X[:], a["x"].rearrange("b p d -> p b d")).then_inc(in_x, 16)
        sp.dma_start(CTX[:], a["ctx_1024"].rearrange("b p d -> p b d")).then_inc(in_ctx, 16)
        mask = a["mask_BxS2_bf1"].rearrange("b k -> (b k)").rearrange("(o n) -> o n", o=1)
        sp.dma_start(mask_row[0:1, :], mask).then_inc(in_small, 16)
        sp.dma_start(mask_all, mask.broadcast_to([P, B * P])).then_inc(in_small, 16)
        for j, g in enumerate(("g_xattn", "g_ffn")):
            sp.dma_start(gates[:, 4 * j:4 * j + 4], a[g].rearrange("(o n) -> o n", o=1).broadcast_to([P, 4])).then_inc(in_small, 16)
        sp.dma_start(l0_wv, a["L0_xattn_Wv"]).then_inc(in_l0x, 16)
        sp.dma_start(l0_wo, a["L0_xattn_Wo"].rearrange("(h p) n -> p h n", p=P)).then_inc(in_l0x, 16)
        sp.dma_start(l0_wk, a["L0_xattn_Wk"]).then_inc(in_l0x, 16)
        sp.dma_start(l0_wq, a["L0_xattn_Wq"].rearrange("(k p) n -> p k n", p=P)).then_inc(in_l0x, 16)
        sp.dma_start(l0_gu, a["L0_ffn_gate_up_proj"].rearrange("e (k p) n -> p e k n", p=P)).then_inc(in_l0f, 16)
        sp.dma_start(l0_dn, a["L0_ffn_down_proj"].rearrange("e (k p) n -> p e k n", p=P)).then_inc(in_l0f, 16)
        sp.dma_start(l1_wq, a["L1_xattn_Wq"].rearrange("(k p) n -> p k n", p=P)).then_inc(in_l1x, 16)
        sp.dma_start(l1_wkv, a["L1_xattn_Wkv"]).then_inc(in_l1x, 16)
        sp.dma_start(l1_wout, a["L1_xattn_Wout"].rearrange("(k p) n -> p k n", p=P)).then_inc(in_l1x, 16)
        sp.dma_start(l1_bias[:], a["L1_xattn_bout"].rearrange("(k p) -> p k", p=P)).then_inc(in_l1x, 16)
        sp.wait_ge(L0.y_mm.sem, L0.y_mm.value(NS - 1, HEADS - 1))
        sp.dma_start(pos_t[0:2, :], a["fside_BxSx2_0"].rearrange("b t c -> c (b t)")).then_inc(in_l1x, 16)
        sp.dma_start(l1_wr, a["L1_ffn_Wr"].rearrange("(k p) n -> p k n", p=P)).then_inc(in_l1f, 16)
        sp.wait_ge(f0_y.sem, f0_y.value(NS - 1, E0 - 1))
        for w, name in ((l1_wg, "L1_ffn_Wg"), (l1_wu, "L1_ffn_Wu")):
            for k in range(KD):
                sp.dma_start(w[:, k, :].rearrange("p (e n) -> p e n", e=L1E),
                             a[name][:, k * P:(k + 1) * P, :].rearrange("e p n -> p e n")).then_inc(in_l1f, 16)
        sp.wait_ge(L1.y_mm.sem, L1.y_mm.value(NS - 1, KD - 1))
        sp.dma_start(wr_raw[:], a["L2_ffn_Wg"]).then_inc(in_l2x, 16)
        sp.dma_start(l1_wd, a["L1_ffn_Wd"].rearrange("e f d -> (e f) d").rearrange("(m p) n -> p m n", p=P)).then_inc(in_l1f, 16)
        sp.dma_start(l2_wv, a["L2_xattn_Wv"]).then_inc(in_l2x, 16)
        sp.dma_start(l2_wo, a["L2_xattn_Wo"].rearrange("(h p) n -> p h n", p=P)).then_inc(in_l2x, 16)
        sp.dma_start(l2_wk, a["L2_xattn_Wk"]).then_inc(in_l2x, 16)
        sp.dma_start(l2_wq, a["L2_xattn_Wq"].rearrange("(k p) n -> p k n", p=P)).then_inc(in_l2x, 16)
        sp.dma_start(gqk[:], a["L2_xattn_gq"].rearrange("(p o) -> p o", o=1)).then_inc(in_l2x, 16)
        sp.dma_start(gk[:], a["L2_xattn_gk"].rearrange("(p o) -> p o", o=1)).then_inc(in_l2x, 16)
        prep_sp(sp)
        l3_loads(sp)
        sp.wait_ge(pool_consts, 5)
        sp.dma_start(xs[B * P:, :], l3_zero_row).then_inc(xs_stored.sem, 16)
        f3_loads(sp)
        with sp.Fori(0, NS, 1) as s:
            n, prev = tail_of(L3.stage, s)
            l3_store(sp, n, s, prev)
        f3_sp(sp)

    @block.gpsimd
    def _(pool):
        for sig in signals.values():
            pool.sem_inc(sig.sem, CREDIT)
        pool.sem_inc(go, 1)
        nc.gpsimd.memset(neg_half[:], -0.5)
        nc.gpsimd.memset(ident[:], 0.0).then_inc(ident_made, 1)
        pool.wait_ge(ident_made, 1)
        nc.gpsimd.affine_select(out=ident[:], in_=ident[:], compare_op=ALU.not_equal, fill=1.0, base=0, pattern=[[-1, P]],
                                channel_multiplier=1).then_inc(ident_made, 1)
        pool.wait_ge(ident_made, 2)
        nc.gpsimd.tensor_copy(ident_b[:], ident[:]).then_inc(ident_made, 1)
        made = 3

        def ordered(ins):
            nonlocal made
            made += 1
            ins.then_inc(ident_made, 1)
            pool.wait_ge(ident_made, made)

        fv = freq[:].rearrange("c (h p x t) -> c h p x t", h=L1H // KD, p=2, x=2)
        ordered(nc.gpsimd.memset(freq[:], 0.0))
        for x, f in enumerate((1.0, 10000.0 ** -0.5)):
            ordered(nc.gpsimd.affine_select(out=fv[:, :, :, x, :], in_=fv[:, :, :, x, :], compare_op=ALU.not_equal, fill=f, base=0,
                                            pattern=[[0, L1H // KD], [-1, 2], [0, 2]], channel_multiplier=1))
        for sel, hd in ((head_sel8, 8), (head_sel16, 16)):
            groups = P // (NB * hd)
            ordered(nc.gpsimd.memset(sel[:], 1.0))
            for sign, base in ((1, 0), (-1, hd - 1)):
                ordered(nc.gpsimd.affine_select(out=sel[:], in_=sel[:], compare_op=ALU.is_ge, fill=0.0, base=base,
                                                pattern=[[-sign * NB * hd, groups], [-sign * hd, NB]], channel_multiplier=sign))
        ordered(nc.gpsimd.iota(iota_i[:], pattern=[[1, 64]], base=0, channel_multiplier=0))
        ordered(nc.gpsimd.tensor_copy(iota[:], iota_i[:]))
        ordered(nc.gpsimd.memset(ones_col[:], 1.0))
        make_sel(ordered, F1, F1.sel, tile(R2, 8448, 704))
        pool.sem_inc(pool_consts, 1)
        with pool.Fori(0, NS - 1, 1) as n:
            tail_pool(pool, n)
        wide_run(wide_pool, L0, pool)
        with pool.Fori(0, NS, 1) as s:
            ffn0_pool(pool, 1, s)
        pool.wait_ge(hmask_ready, 2)
        pool.wait_ge(L0.y_mm.sem, L0.y_mm.value(NS - 1, HEADS - 1))
        nc.gpsimd.memset(l1_v, 0.0).then_inc(pool_consts, 1)
        run_ahead(lambda S: narrow_pool(pool, S, l1_k, hmask8, nothing), L1, pool)
        pool.wait_ge(rope_ready.sem, rope_ready.value(NS - 1, 3))
        make_sel(ordered, F2, l2_sel_made.bitcast(BF16), tile(R2, 9000, 1408))
        pool.sem_inc(pool_consts, 1)
        with pool.Fori(0, NS, 1) as s:
            dense_pool(pool, F1, s)
        first_keys_pool(pool, L2)
        wide_run(wide_pool, L2, pool)
        with pool.Fori(0, NS, 1) as s:
            dense_pool(pool, F2, s)
        l3_setup_pool(pool)
        done(pool, xnt_ready, NS * L3.stage, 1)
        l3_copies(pool, 0)

        def l3_pool(s, ahead, route):
            def beside(S, t):
                if ahead and S.new and t == 8:
                    done(pool, l3_v_mm, s, TB - 1)
                    done(pool, xnt_ready, s + (NS * L3.stage + 1), 1)
                    l3_copies(pool, s + 1)
                if route and S.new and t == L3.n - 1:
                    f3_route_pool(pool, s - 1, 0, 2)
                if route and not S.new and t < 2:
                    f3_route_pool(pool, s - 1, 2 + 3 * t, 5 + 3 * t)

            l3_body(lambda S, at: narrow_pool(pool, S, l3_k, hmask16, at), s, beside)
            if route:
                f3_route_pool(pool, s - 1, 8)

        l3_pool(0, True, False)
        f3_setup_pool(pool)
        with pool.Fori(1, NS - 1, 1) as s:
            l3_pool(s, True, True)
        l3_pool(NS - 1, False, True)
        tail_pool(pool, n_tails - 1)
        f3_route_pool(pool, NS - 1)
        f3_pool_start(pool)
        with pool.Fori(0, NG, 1) as g:
            f3_pool(pool, g)

    @block.tensor
    def _(pe):
        pe.wait_ge(go, 1)
        pe.wait_ge(ident_made, 3)
        pe.wait_ge(in_ctx, 16)
        for g in range(NS):
            for t in range(TB):
                last = nc.tensor.transpose(PS[:, 4 + g, t * P:(t + 1) * P], CTX[:, g * TB + t, :], ident[:])
            last.then_inc(ctx_tr.sem, 1)
        pe.wait_ge(in_l0x, 64)
        pe.wait_ge(ctxt_ready.sem, ctxt_ready.value(0, NS - 1))
        pe.wait_ge(const_made, 2)
        wide_prep_pe(pe, L0)
        with pe.Fori(0, NS - 1, 1) as n:
            done(pe, xnt_ready, n, -1)
            for k in range(KD):
                tail_pe_xn(pe, n, k)
        pe.wait_ge(L0.wvo_ready.sem, L0.wvo_ready.value(0, HEADS // 2 - 1))
        pe.wait_ge(mask_ready, 2)
        wide_run(wide_pe, L0, pe)
        pe.wait_ge(in_l0f, 32)
        with pe.Fori(0, NS, 1) as s:
            ffn0_pe(pe, 1, s)
        pe.wait_ge(pool_consts, 1)
        pe.wait_ge(in_l1x, 16 * 5)
        pe.wait_ge(l1w_ready, 1)
        rope = rope_pe(pe)
        run_ahead(lambda S: narrow_pe(pe, S, l1_q, l1_v, l1_ot, rope), L1, pe)
        pe.wait_ge(in_l1f, 16 * 6)
        run_ahead(lambda S: dense_pe(pe, S), F1, pe)
        pe.wait_ge(in_l2x, 16 * 7)
        first_keys_pe(pe, L2)
        wide_prep_pe(pe, L2)
        pe.wait_ge(L2.wvo_ready.sem, L2.wvo_ready.value(0, HEADS // 2 - 1))
        wide_run(wide_pe, L2, pe)
        prep_pe(pe)
        run_ahead(lambda S: dense_pe(pe, S, prep_beside_pe), F2, pe)
        l3_setup_pe(pe)
        pe.wait_ge(vec_ready.sem, vec_ready.value(0, 1))
        pe.wait_ge(l3_w.sem, l3_w.value(0, 3))
        l3_start_pe(pe)

        def l3_pe(s, ahead, route):
            def beside(S, t):
                if ahead and not S.new:
                    l3_end_pe(pe, S, t, route)
                if route:
                    f3_route_pe(pe, s - 1, t if S.new else t + L3.n)

            l3_body(lambda S, at: narrow_pe(pe, S, l3_q, l3_v, l3_ot, at), s, beside)

        l3_pe(0, True, False)
        f3_setup_pe(pe)
        with pe.Fori(1, NS - 1, 1) as s:
            l3_pe(s, True, True)
        l3_pe(NS - 1, False, True)
        tail_pe(pe, n_tails - 1)
        for t in range(ROUTE_END):
            f3_route_pe(pe, NS - 1, t)
        with pe.Fori(0, NG, 1) as g:
            f3_pe(pe, g)

    @block.scalar
    def _(act):
        act.wait_ge(go, 1)
        act.wait_ge(in_small, 64)
        nc.scalar.activation(gates[:], gates[:], ACT.Tanh).then_inc(gates_ready, 1)
        for g in range(NS):
            act.wait_ge(ctx_tr.sem, ctx_tr.value(0, g))
            nc.scalar.activation(CTXT[:, g * W:(g + 1) * W], PS[:, 4 + g, :], ACT.Copy).then_inc(ctxt_ready.sem, 1)
        act.wait_ge(mask_ready, 2)
        wide_prep_act(act, L0)
        with act.Fori(0, NS - 1, 1) as n:
            for k in range(KD):
                tail_act(act, n, n, k)
        act.wait_ge(gates_ready, 1)
        wide_run(wide_act, L0, act)
        with act.Fori(0, NS, 1) as s:
            ffn0_act(act, 1, s)
        act.wait_ge(in_l1x, 16 * 5)
        for w, ws in ((l1_wq.rearrange("p k (n t) -> p (k n) t", t=2), l1_wqs.rearrange("p k (n t) -> p (k n) t", t=2)),
                      (l1_wkv[:, 0:D].rearrange("p (n t) -> p n t", t=2), l1_wks.rearrange("p (n t) -> p n t", t=2))):
            nc.scalar.activation(ws[:, :, 0], w[:, :, 1], ACT.Copy, scale=-1.0)
            ins = nc.scalar.activation(ws[:, :, 1], w[:, :, 0], ACT.Copy)
        nc.scalar.activation(l1_bias[:], l1_bias[:], ACT.Copy, scale=gates[:, 1:2]).then_inc(l1w_ready, 1)
        act.wait_ge(l1w_ready, 1)
        act.wait_ge(pool_consts, 2)
        rope = rope_act(act)
        run_ahead(lambda S: narrow_act(act, S, float(L1HD) ** -0.5, rope), L1, act)
        run_ahead(lambda S: dense_act(act, S), F1, act)
        act.wait_ge(gqk_ready, 1)
        first_keys_act(act, L2)
        wide_prep_act(act, L2)
        wide_run(wide_act, L2, act)
        prep_act_engine(act)
        run_ahead(lambda S: dense_act(act, S, prep_beside_act), F2, act)
        l3_setup_act(act)
        act.wait_ge(vec_ready.sem, vec_ready.value(0, 1))
        l3_start_act(act)

        def l3_act(s, ahead, route):
            def beside(S, t):
                if ahead and not S.new:
                    l3_end_act(act, S, t)
                if route:
                    f3_route_act(act, s - 1, t if S.new else t + L3.n)

            l3_body(lambda S, at: narrow_act(act, S, float(L3HD) ** -0.5, at), s, beside)

        l3_act(0, True, False)
        f3_setup_act(act)
        with act.Fori(1, NS - 1, 1) as s:
            l3_act(s, True, True)
        l3_act(NS - 1, False, True)
        for k in range(KD):
            tail_act(act, n_tails - 1, NS - 1, k)
        for t in range(ROUTE_END):
            f3_route_act(act, NS - 1, t)
        with act.Fori(0, NG, 1) as g:
            f3_act(act, g)

    @block.vector
    def _(dve):
        dve.wait_ge(go, 1)
        nc.vector.memset(YT[:], 0.0).then_inc(const_made, 1)
        dve.wait_ge(const_made, 1)
        dve.sem_inc(yt_ready.sem, NS * KD)
        dve.sem_inc(yt_tr.sem, 2 * (NS - 1))
        dve.sem_inc(y_added.sem, 2 * (NS - 1))
        nc.vector.memset(ones_b[:], 1.0).then_inc(const_made, 1)
        dve.wait_ge(in_small, 64)
        nc.vector.tensor_scalar(mask_bias[0:1, :], mask_row[0:1, :], 1.0, NEG_BIG, ALU.subtract, ALU.mult).then_inc(mask_ready, 1)
        nc.vector.tensor_reduce(any_key[:], mask_all.rearrange("p (b k) -> p b k", b=B), AX.X, ALU.max).then_inc(mask_ready, 1)
        dve.wait_ge(pool_consts, 1)
        for sel, mask in ((head_sel8, hmask8), (head_sel16, hmask16)):
            nc.vector.tensor_reduce(mask[:], sel[:].rearrange("p r j -> p j r"), AX.X, ALU.add).then_inc(hmask_ready, 1)
        dve.wait_ge(in_x, 16)
        with dve.Fori(0, NS - 1, 1) as n:
            tail_dve_stats(dve, n, n)
            done(dve, xn_tr, n, -1)
            tail_dve_norm(dve, n, n)
        dve.wait_ge(mask_ready, 2)
        wide_run(wide_dve, L0, dve)
        with dve.Fori(0, NS, 1) as s:
            ffn0_dve(dve, 1, s)
        rope = rope_dve(dve)
        run_ahead(lambda S: narrow_dve(dve, S, l1_ot, hmask8, float(L1HD) ** -0.5, rope), L1, dve)
        run_ahead(lambda S: dense_dve(dve, S, False), F1, dve)
        dve.wait_ge(in_l2x, 16 * 7)
        nc.vector.scalar_tensor_tensor(gqk[:], gqk[:], SCALE_WIDE, gk[:], ALU.mult, ALU.mult).then_inc(gqk_ready, 1)
        first_keys_dve(dve, L2)
        wide_run(wide_dve, L2, dve)
        prep_dve_engine(dve)
        run_ahead(lambda S: dense_dve(dve, S, True, prep_beside_dve), F2, dve)
        l3_setup_dve(dve)
        l3_start_dve(dve)

        def l3_dve(s, ahead, route):
            link = Chain(dve, R3.chain, s - 1) if route else None

            def beside(S, t):
                if ahead and not S.new:
                    l3_end_dve(dve, S, t)
                if route:
                    f3_route_dve(dve, s - 1, t if S.new else t + L3.n, link)

            l3_body(lambda S, at: narrow_dve(dve, S, l3_ot, hmask16, float(L3HD) ** -0.5, at), s, beside)

        l3_dve(0, True, False)
        dve.wait_ge(pool_consts, 6)
        with dve.Fori(1, NS - 1, 1) as s:
            l3_dve(s, True, True)
        l3_dve(NS - 1, False, True)
        tail_dve(dve, n_tails - 1, NS - 1, NS)
        link = Chain(dve, R3.chain, NS - 1)
        for t in range(ROUTE_END):
            f3_route_dve(dve, NS - 1, t, link)
        with dve.Fori(0, NG, 1) as g:
            f3_dve(dve, g)
        f3_end_dve(dve)


def kernel(**inputs):
    import numpy as _np
    import concourse.bacc as _bacc
    from concourse import mybir as _mybir
    from concourse.bass_utils import run_bass_kernel_spmd as _run

    nc = _bacc.Bacc("TRN2", target_bir_lowering=False, num_devices=1)
    arrays, args = {}, {}
    for name, x in inputs.items():
        x = _np.ascontiguousarray(x)
        if x.dtype == _np.bool_:
            x = x.view(_np.uint8)
        arrays["in_" + name] = x
        args[name] = nc.dram_tensor("in_" + name, x.shape, _mybir.dt.from_np(x.dtype), kind="ExternalInput").ap()
    out = nc.dram_tensor("out_0", (16, 128, 256), _mybir.dt.float32, kind="ExternalOutput").ap()
    build(nc, args, out)
    r = _run(nc, [arrays], core_ids=[0])
    return r.results[0]["out_0"]
```
